# Optimizing a Trainium2 kernel written in Bass

```python
import numpy as np
import jax
import jax.numpy as jnp

def _softmax(x, axis=-1):
    return jax.nn.softmax(x, axis=axis)

def _gelu(x):
    return jax.nn.gelu(x, approximate=True)

def _silu(x):
    return jax.nn.silu(x)

def _sigmoid(x):
    return jax.nn.sigmoid(x)

def _layernorm(x, axis=-1, eps=1e-05):
    m = jnp.mean(x, axis=axis, keepdims=True)
    v = jnp.var(x, axis=axis, keepdims=True)
    return (x - m) / jnp.sqrt(v + eps)

def _scatter_add(tgt, idx, src, axis=0):
    return tgt.at[idx].add(src)

def _segment_sum(src, seg, n):
    return jax.ops.segment_sum(src, seg, n)
kernel_name = 'mk_gnn_preln_d4_gnn_r32_cd4fd2'

def setup_inputs(seed: int=0):
    np.random.seed(seed)
    _w = jnp.asarray

    def _rec_inputs():
        import jax
        import jax.numpy as jnp
        _gk = jax.random.key(seed)
        x = -8.49e-07 + 0.004471 * jax.random.normal(jax.random.fold_in(_gk, 1), (3125, 64), jnp.float32)
        _s = jax.random.randint(jax.random.fold_in(_gk, 2), (25000,), 0, 3125, jnp.int32)
        _d = jax.random.randint(jax.random.fold_in(_gk, 3), (25000,), 0, 3125, jnp.int32)
        _loop = jnp.arange(3125, dtype=jnp.int32)
        src = jnp.concatenate([_s, _d, _loop])
        dst = jnp.concatenate([_d, _s, _loop])
        _o = jnp.argsort(dst, stable=True)
        src = src[_o]
        dst = dst[_o]
        edge_attr_64 = -8.16379e-05 + 0.999858 * jax.random.normal(jax.random.fold_in(_gk, 12), (53125, 64), jnp.float32)
        edge_weight = jax.random.uniform(jax.random.fold_in(_gk, 14), (53125,), jnp.float32, 0.0, 0.999998)
        return (x, src, dst, edge_attr_64, edge_weight)
    x, src, dst, edge_attr_64, edge_weight = _rec_inputs()

    def _L0_gnn_setup():
        import jax, jax.numpy as jnp
        import numpy as np
        NUM_NODES = 3125
        EMB_DIM = 64
        N_LAYERS = 3
        N_EDGES = 37500
        key = jax.random.key(seed)
        k_emb, k_edge = jax.random.split(key)
        limit = float(np.sqrt(6.0 / (NUM_NODES + EMB_DIM)))
        emb = jax.random.uniform(k_emb, (NUM_NODES, EMB_DIM), jnp.float32, -limit, limit)
        edge_index = jax.random.randint(k_edge, (2, N_EDGES), 0, NUM_NODES, dtype=jnp.int64)
        return {'emb': emb, 'edge_index': edge_index}
    _L0_gnn_all = _L0_gnn_setup()
    _L0_gnn_in = {k: v for k, v in _L0_gnn_all.items() if k in ()}
    del _L0_gnn_all

    def _L1_gnn_setup():
        import jax, jax.numpy as jnp
        import numpy as np
        N_NODES = 50000
        N_EDGES = 25000
        D_IN = 64
        D_OUT = 64

        def _gcn_conv(x, edge_index, edge_weight, W, b):
            n = x.shape[0]
            loop = jnp.arange(n, dtype=edge_index.dtype)
            row = jnp.concatenate([edge_index[0], loop])
            col = jnp.concatenate([edge_index[1], loop])
            w = jnp.concatenate([edge_weight, jnp.ones((n,), dtype=edge_weight.dtype)])
            deg = jax.ops.segment_sum(w, col, num_segments=n)
            dinv = jnp.where(deg > 0, jax.lax.rsqrt(jnp.where(deg > 0, deg, 1.0)), 0.0)
            norm = dinv[row] * w * dinv[col]
            h = x @ W
            msg = h[row] * norm[:, None]
            out = jax.ops.segment_sum(msg, col, num_segments=n)
            return out + b
        key = jax.random.key(seed)
        k1, k2, k3, k4 = jax.random.split(key, 4)
        ins = jax.random.normal(k1, (N_NODES, D_IN), dtype=jnp.float32)
        edge_index = jax.random.randint(k2, (2, N_EDGES), 0, N_NODES, dtype=jnp.int64)
        edge_attr = jax.random.uniform(k3, (N_EDGES,), dtype=jnp.float32)
        W = jax.random.normal(k4, (D_IN, D_OUT), dtype=jnp.float32) * (1.0 / np.sqrt(D_IN))
        b = jnp.zeros((D_OUT,), dtype=jnp.float32)
        return {'ins': ins, 'edge_index': edge_index, 'edge_attr': edge_attr, 'W': W, 'b': b}
    _L1_gnn_all = _L1_gnn_setup()
    _L1_gnn_in = {k: v for k, v in _L1_gnn_all.items() if k in ('W', 'b')}
    del _L1_gnn_all

    def _L2_gnn_setup():
        import jax, jax.numpy as jnp
        import numpy as np
        N_NODES = 3125
        N_EDGES = 50000
        D_IN = 64
        D_OUT = 64
        key = jax.random.key(seed)
        k1, k2, k3, k4, k5 = jax.random.split(key, 5)
        feat = jax.random.normal(k1, (N_NODES, D_IN), dtype=jnp.float32)
        W_self = jax.random.normal(k2, (D_OUT, D_IN), dtype=jnp.float32) * (1.0 / np.sqrt(D_IN))
        W_neigh = jax.random.normal(k3, (D_OUT, D_IN), dtype=jnp.float32) * (1.0 / np.sqrt(D_IN))
        src = jax.random.randint(k4, (N_EDGES,), 0, N_NODES, dtype=jnp.int32)
        dst = jax.random.randint(k5, (N_EDGES,), 0, N_NODES, dtype=jnp.int32)
        return {'feat': feat, 'W_self': W_self, 'W_neigh': W_neigh, 'src': src, 'dst': dst}
    _L2_gnn_all = _L2_gnn_setup()
    _L2_gnn_in = {k: v for k, v in _L2_gnn_all.items() if k in ('W_self', 'W_neigh')}
    del _L2_gnn_all

    def _L3_gnn_setup():
        import jax, jax.numpy as jnp
        import numpy as np
        N, D = (3125, 64)
        E, DE = (50000, 64)
        MSG_H, MSG_OUT = (128, 64)
        NODE_H = 128
        LN_EPS = 1e-05
        key = jax.random.key(seed)
        ks = jax.random.split(key, 10)

        def glorot(k, shape):
            fan_in = shape[0]
            return jax.random.normal(k, shape, jnp.float32) / jnp.sqrt(jnp.float32(fan_in))
        return {'nodes': jax.random.normal(ks[0], (N, D), jnp.float32), 'edges': jax.random.normal(ks[1], (E, DE), jnp.float32), 'senders': jax.random.randint(ks[2], (E,), 0, N, jnp.int32), 'receivers': jax.random.randint(ks[3], (E,), 0, N, jnp.int32), 'msg_W1': glorot(ks[4], (2 * D + DE, MSG_H)), 'msg_b1': jnp.zeros((MSG_H,), jnp.float32), 'msg_W2': glorot(ks[5], (MSG_H, MSG_OUT)), 'msg_b2': jnp.zeros((MSG_OUT,), jnp.float32), 'node_W1': glorot(ks[6], (D + MSG_OUT, NODE_H)), 'node_b1': jnp.zeros((NODE_H,), jnp.float32), 'node_W2': glorot(ks[7], (NODE_H, D)), 'node_b2': jnp.zeros((D,), jnp.float32), 'ln_scale': jnp.ones((D,), jnp.float32), 'ln_offset': jnp.zeros((D,), jnp.float32)}
    _L3_gnn_all = _L3_gnn_setup()
    _L3_gnn_in = {k: v for k, v in _L3_gnn_all.items() if k in ('msg_W1', 'msg_b1', 'msg_W2', 'msg_b2', 'node_W1', 'node_b1', 'node_W2', 'node_b2', 'ln_scale', 'ln_offset')}
    del _L3_gnn_all
    return {'x': x, 'src': src, 'dst': dst, 'edge_attr_64': edge_attr_64, 'edge_weight': edge_weight, 'L1_gnn_W': _L1_gnn_in['W'], 'L1_gnn_b': _L1_gnn_in['b'], 'L2_gnn_W_self': _L2_gnn_in['W_self'], 'L2_gnn_W_neigh': _L2_gnn_in['W_neigh'], 'L3_gnn_msg_W1': _L3_gnn_in['msg_W1'], 'L3_gnn_msg_b1': _L3_gnn_in['msg_b1'], 'L3_gnn_msg_W2': _L3_gnn_in['msg_W2'], 'L3_gnn_msg_b2': _L3_gnn_in['msg_b2'], 'L3_gnn_node_W1': _L3_gnn_in['node_W1'], 'L3_gnn_node_b1': _L3_gnn_in['node_b1'], 'L3_gnn_node_W2': _L3_gnn_in['node_W2'], 'L3_gnn_node_b2': _L3_gnn_in['node_b2'], 'L3_gnn_ln_scale': _L3_gnn_in['ln_scale'], 'L3_gnn_ln_offset': _L3_gnn_in['ln_offset']}

def reference(x, src, dst, edge_attr_64, edge_weight, L1_gnn_W, L1_gnn_b, L2_gnn_W_self, L2_gnn_W_neigh, L3_gnn_msg_W1, L3_gnn_msg_b1, L3_gnn_msg_W2, L3_gnn_msg_b2, L3_gnn_node_W1, L3_gnn_node_b1, L3_gnn_node_W2, L3_gnn_node_b2, L3_gnn_ln_scale, L3_gnn_ln_offset):
    import jax
    import jax.numpy as jnp

    def _L0_gnn_ref(emb, edge_index):
        import jax, jax.numpy as jnp
        import numpy as np
        NUM_NODES = 3125
        EMB_DIM = 64
        N_LAYERS = 3
        N_EDGES = 37500
        row, col = (edge_index[0], edge_index[1])
        num_nodes = emb.shape[0]
        ones = jnp.ones(row.shape[0], dtype=emb.dtype)
        deg = jax.ops.segment_sum(ones, col, num_segments=num_nodes)
        deg_inv_sqrt = jnp.where(deg > 0, jax.lax.rsqrt(jnp.maximum(deg, 1.0)), 0.0)
        norm = deg_inv_sqrt[row] * deg_inv_sqrt[col]

        def lgconv(x):
            msgs = x[row] * norm[:, None]
            return jax.ops.segment_sum(msgs, col, num_segments=num_nodes)
        x = emb
        acc = x
        for _ in range(N_LAYERS):
            x = lgconv(x)
            acc = acc + x
        return acc / (N_LAYERS + 1)

    def _L1_gnn_ref(ins, edge_index, edge_attr, W, b):
        import jax, jax.numpy as jnp
        import numpy as np
        N_NODES = 50000
        N_EDGES = 25000
        D_IN = 64
        D_OUT = 64

        def _gcn_conv(x, edge_index, edge_weight, W, b):
            n = x.shape[0]
            loop = jnp.arange(n, dtype=edge_index.dtype)
            row = jnp.concatenate([edge_index[0], loop])
            col = jnp.concatenate([edge_index[1], loop])
            w = jnp.concatenate([edge_weight, jnp.ones((n,), dtype=edge_weight.dtype)])
            deg = jax.ops.segment_sum(w, col, num_segments=n)
            dinv = jnp.where(deg > 0, jax.lax.rsqrt(jnp.where(deg > 0, deg, 1.0)), 0.0)
            norm = dinv[row] * w * dinv[col]
            h = x @ W
            msg = h[row] * norm[:, None]
            out = jax.ops.segment_sum(msg, col, num_segments=n)
            return out + b
        x = _gcn_conv(ins, edge_index, edge_attr, W, b)
        return jax.nn.relu(x)

    def _L2_gnn_ref(feat, W_self, W_neigh, src, dst):
        import jax, jax.numpy as jnp
        import numpy as np
        N_NODES = 3125
        N_EDGES = 50000
        D_IN = 64
        D_OUT = 64
        n = feat.shape[0]
        msgs = feat[src]
        summed = jax.ops.segment_sum(msgs, dst, num_segments=n)
        deg = jax.ops.segment_sum(jnp.ones((dst.shape[0],), feat.dtype), dst, num_segments=n)
        h_neigh = summed / jnp.maximum(deg, 1.0)[:, None]
        return feat @ W_self.T + h_neigh @ W_neigh.T

    def _L3_gnn_ref(nodes, edges, senders, receivers, msg_W1, msg_b1, msg_W2, msg_b2, node_W1, node_b1, node_W2, node_b2, ln_scale, ln_offset):
        import jax, jax.numpy as jnp
        import numpy as np
        N, D = (3125, 64)
        E, DE = (50000, 64)
        MSG_H, MSG_OUT = (128, 64)
        NODE_H = 128
        LN_EPS = 1e-05
        x = jnp.concatenate([nodes[senders], nodes[receivers], edges], axis=-1)
        h = jax.nn.relu(x @ msg_W1 + msg_b1)
        messages = jax.nn.relu(h @ msg_W2 + msg_b2)
        agg = jax.ops.segment_sum(messages, receivers, num_segments=nodes.shape[0])
        y = jnp.concatenate([nodes, agg], axis=-1)
        y = jax.nn.relu(y @ node_W1 + node_b1)
        y = y @ node_W2 + node_b2
        mean = jnp.mean(y, axis=-1, keepdims=True)
        var = jnp.var(y, axis=-1, keepdims=True)
        y = (y - mean) * jax.lax.rsqrt(var + LN_EPS) * ln_scale + ln_offset
        return nodes + y
    edge_index = jnp.stack([src, dst])
    h = jnp.maximum(_layernorm(x, axis=-1), 0.0)
    x = x + _L0_gnn_ref(h, edge_index)
    h = jnp.maximum(_layernorm(x, axis=-1), 0.0)
    x = x + _L1_gnn_ref(h, edge_index, edge_weight, L1_gnn_W, L1_gnn_b)
    h = jnp.maximum(_layernorm(x, axis=-1), 0.0)
    x = x + _L2_gnn_ref(h, L2_gnn_W_self, L2_gnn_W_neigh, src, dst)
    h = jnp.maximum(_layernorm(x, axis=-1), 0.0)
    x = x + _L3_gnn_ref(h, edge_attr_64, src, dst, L3_gnn_msg_W1, L3_gnn_msg_b1, L3_gnn_msg_W2, L3_gnn_msg_b2, L3_gnn_node_W1, L3_gnn_node_b1, L3_gnn_node_W2, L3_gnn_node_b2, L3_gnn_ln_scale, L3_gnn_ln_offset)
    return x

_drawn_inputs = setup_inputs


def setup_inputs(seed=0):
    import zlib

    import numpy as np

    out = dict(_drawn_inputs(seed))
    spreads = {'L1_gnn_b': (0.0, 0.1),
     'L3_gnn_msg_b1': (0.0, 0.1),
     'L3_gnn_msg_b2': (0.0, 0.1),
     'L3_gnn_node_b1': (0.0, 0.427),
     'L3_gnn_node_b2': (0.0, 0.31),
     'L3_gnn_ln_scale': (1.0, 0.2),
     'L3_gnn_ln_offset': (0.0, 0.1)}
    factors = {}
    for name, (base, spread) in spreads.items():
        noise = np.random.default_rng([zlib.crc32(name.encode()), seed]).standard_normal(out[name].shape)
        drawn = base * np.exp(spread * noise) if base else spread * noise
        out[name] = jnp.asarray(drawn.astype(out[name].dtype))
    for name, factor in factors.items():
        out[name] = (out[name] * factor).astype(out[name].dtype)
    return out
```

```python
from contextlib import ExitStack

import concourse.bass as bass
from concourse import mybir

F32 = mybir.dt.float32
I32 = mybir.dt.int32
ALU = mybir.AluOpType
ACT = mybir.ActivationFunctionType
AX = mybir.AxisListType

N = 3125
E = 53125
D = 64
HID = 128
NP, NC = 125, 25
P = 128
T = -(-E // P)
FULL = E // P
TAIL = E - FULL * P
G = 4
Q = 4
IT = T // (G * Q)
ROUNDS = -(-NC // 4)
LAST_GROUP = T // G - 1
LAST_EDGES = E - LAST_GROUP * G * P
EPS = 1e-5
W = 128
assert T == G * Q * IT and NP * NC == N

PASS_DEG, PASS_L0, PASS_L1, PASS_L2, PASS_L3 = 0, 1, 4, 5, 6
NPASS = 7


def build(nc, x, src, dst, edge_attr, edge_weight, w1, b1, w2s, w2n, mw1, mb1, mw2, mb2,
          nw1, nb1, nw2, nb2, ln_scale, ln_offset, out):
    with ExitStack() as ctx:
        def sb(name, shape, dt=F32):
            return ctx.enter_context(nc.sbuf_tensor(name, shape, dt))

        def sem(name):
            return ctx.enter_context(nc.semaphore(name))

        table = nc.dram_tensor("table", [N, D], F32, kind="Internal").ap()
        pr_table = nc.dram_tensor("pr_table", [N + W, HID], F32, kind="Internal").ap()
        drel_flat = nc.dram_tensor("drel_flat", [T * P], F32, kind="Internal").ap()

        raw_dst = sb("raw_dst", [P, 4, P], I32)
        raw_src = sb("raw_src", [P, 4, P], I32)
        raw_w = sb("raw_w", [P, 4, P])
        drel_t = sb("drel_t", [P, 4, P])
        src_t = sb("src_t", [P, 4, P])
        drel = sb("drel", [P, 4 * P])
        src_i = sb("src_i", [P, 4 * P], I32)
        wcol = sb("wcol", [P, 4 * P])
        base_row = sb("base_row", [1, T], I32)
        ident = sb("ident", [P, P])
        iota_i = sb("iota_i", [P, P], I32)
        iota_row = sb("iota_row", [P, P])
        iota_ip = sb("iota_ip", [P, 1], I32)
        iota_p = sb("iota_p", [P, 1])
        ones_row = sb("ones_row", [1, P])
        neg_half = sb("neg_half", [P, NC])
        w1_sb = sb("w1_sb", [D, D])
        w2s_sb = sb("w2s_sb", [D, D])
        w2n_sb = sb("w2n_sb", [D, D])
        w2s_t = sb("w2s_t", [D, D])
        w2n_t = sb("w2n_t", [D, D])
        mw1_se = sb("mw1_se", [P, HID])
        mw1_r = sb("mw1_r", [D, HID])
        mb1_sb = sb("mb1_sb", [HID, 1])
        mw2_sb = sb("mw2_sb", [HID, D])
        mb2_row = sb("mb2_row", [1, G, D])
        nw1_h = sb("nw1_h", [D, HID])
        nw1_a = sb("nw1_a", [D, HID])
        nb1_sb = sb("nb1_sb", [HID, 1])
        nw2_sb = sb("nw2_sb", [HID, D])
        b1_bc = sb("b1_bc", [P, D])
        nb2_bc = sb("nb2_bc", [P, D])
        scale_bc = sb("scale_bc", [P, D])
        offset_bc = sb("offset_bc", [P, D])
        xs = sb("xs", [NP, NC, D])
        hs = sb("hs", [NP, NC, D])
        cur = sb("cur", [NP, NC, D])
        tmp = sb("tmp", [NP, NC, D])
        total = sb("total", [NP, NC, D])
        st_a = sb("st_a", [NP, NC])
        st_b = sb("st_b", [NP, NC])
        st_c = sb("st_c", [NP, NC])
        deg = sb("deg", [NP, NC, 2])
        dinv0 = sb("dinv0", [NP, NC])
        dinv0sq = sb("dinv0sq", [NP, NC])
        dinv1 = sb("dinv1", [NP, NC])
        rdeg = sb("rdeg", [NP, NC])
        h_t = sb("h_t", [D, NC, NP])
        acc_t = sb("acc_t", [D, N + W])
        acc_deg = sb("acc_deg", [2, N + W])
        pr_sb = sb("pr_sb", [NP, NC, HID])
        y1_t = sb("y1_t", [HID, 2, 4 * NP])
        X = sb("X", [P, Q, G, 2 * D])
        idx = sb("idx", [P, Q, G], I32)
        ow = sb("ow", [P, Q, G, 2])
        onehot = sb("onehot", [P, Q, G, W])
        onehot_t = sb("onehot_t", [P, Q, G * P])
        drel_bc = sb("drel_bc", [P, Q, G * P])
        prw = sb("prw", [W, Q, G, HID])
        x_t = sb("x_t", [P, 2, G * P])
        hid_t = sb("hid_t", [HID, 2, G * P])
        msg = sb("msg", [P, 2, G, D])

        big = ctx.enter_context(nc.psum_tensor("big", [P, 4, 512], F32))
        seg = ctx.enter_context(nc.psum_tensor("seg", [P, 4, 512], F32))
        big_nodes = big[:, :, :].rearrange("p a b -> p (a b)")[0:NP, 0:NC * D].rearrange("p (c d) -> p c d", d=D)

        ld_edges, ld_x, ld_w, ld_base = sem("ld_edges"), sem("ld_x"), sem("ld_w"), sem("ld_base")
        fills = sem("fills")
        pads = sem("pads")
        drel_stored = sem("drel_stored")
        gathered = [sem(f"gathered{q}") for q in range(Q)]
        idx_ready = [sem(f"idx_ready{q}") for q in range(Q)]
        onehot_ready = [sem(f"onehot_ready{q}") for q in range(Q)]
        seg_done = [sem(f"seg_done{q}") for q in range(Q)]
        edges_loaded = [sem(f"edges_loaded{q}") for q in range(Q)]
        drel_loaded = [sem(f"drel_loaded{q}") for q in range(Q)]
        prw_loaded = [sem(f"prw_loaded{q}") for q in range(Q)]
        onehot_t_ready = [sem(f"onehot_t_ready{q}") for q in range(Q)]
        transposed = [sem(f"transposed{r}") for r in range(2)]
        x_t_ready = [sem(f"x_t_ready{r}") for r in range(2)]
        hid_done = [sem(f"hid_done{r}") for r in range(2)]
        hid_ready = [sem(f"hid_ready{r}") for r in range(2)]
        msg_done = [sem(f"msg_done{r}") for r in range(2)]
        msg_ready = [sem(f"msg_ready{r}") for r in range(2)]
        acc_step = sem("acc_step")
        dve_chain = sem("dve_chain")
        pool_chain = sem("pool_chain")
        acc_cleared = sem("acc_cleared")
        table_ready, table_stored = sem("table_ready"), sem("table_stored")
        rstd_in, rstd_out = sem("rstd_in"), sem("rstd_out")
        gathers_begun = sem("gathers_begun")
        tail_loaded = sem("tail_loaded")
        events = {}

        def ev(name):
            if name not in events:
                events[name] = sem(name)
            return events[name]

        block = ctx.enter_context(nc.Block())

        @block.sync
        def _(sp):
            sp.dma_start(xs[:, :, :], x.rearrange("(p c) d -> p c d", c=NC)).then_inc(ld_x, 16)
            sp.wait_ge(pads, 3)
            for raw, flat in ((raw_dst, dst), (raw_src, src), (raw_w, edge_weight)):
                sp.dma_start(raw[:, 0:3, :], flat[0:3 * P * P].rearrange("(c p e) -> p c e", p=P, e=P)).then_inc(ld_edges, 16)
                sp.dma_start(raw[0:FULL - 3 * P, 3, :], flat[3 * P * P:FULL * P].rearrange("(p e) -> p e", e=P)).then_inc(ld_edges, 16)
                sp.dma_start(raw[FULL - 3 * P:T - 3 * P, 3, 0:TAIL], flat[FULL * P:E].rearrange("(p e) -> p e", p=1)).then_inc(ld_edges, 16)
            sp.dma_start(base_row[:, 0:FULL], dst[0:FULL * P].rearrange("(a t e) -> a t e", a=1, e=P)[:, :, 0],
                         allow_slow_non_contiguous=True).then_inc(ld_base, 16)
            sp.dma_start(base_row[:, FULL:T], dst[FULL * P:FULL * P + 1].rearrange("(a t) -> a t", a=1)).then_inc(ld_base, 16)
            loads = [(w1_sb[:, :], w1), (w2s_sb[:, :], w2s), (w2n_sb[:, :], w2n),
                     (mw1_se[0:D, :], mw1[0:D, :]), (mw1_se[D:2 * D, :], mw1[2 * D:3 * D, :]), (mw1_r[:, :], mw1[D:2 * D, :]),
                     (mb1_sb[:, :], mb1.rearrange("(p a) -> p a", a=1)), (mw2_sb[:, :], mw2),
                     (nw1_h[:, :], nw1[0:D, :]), (nw1_a[:, :], nw1[D:2 * D, :]),
                     (nb1_sb[:, :], nb1.rearrange("(p a) -> p a", a=1)), (nw2_sb[:, :], nw2),
                     (b1_bc[:, :], b1.partition_broadcast(P)), (nb2_bc[:, :], nb2.partition_broadcast(P)),
                     (scale_bc[:, :], ln_scale.partition_broadcast(P)), (offset_bc[:, :], ln_offset.partition_broadcast(P))]
            loads += [(mb2_row[:, j, :], mb2.rearrange("(a d) -> a d", a=1)) for j in range(G)]
            for a, b in loads:
                sp.dma_start(a, b).then_inc(ld_w, 16)
            sp.wait_ge(ev("drel_t_ready"), 1)
            sp.dma_start(drel_flat[0:3 * P * P].rearrange("(c p e) -> p c e", p=P, e=P), drel_t[:, 0:3, :]).then_inc(drel_stored, 16)
            sp.dma_start(drel_flat[3 * P * P:T * P].rearrange("(p e) -> p e", e=P), drel_t[0:T - 3 * P, 3, :]).then_inc(drel_stored, 16)

            sp.wait_ge(fills, 7)
            sp.dma_start(pr_table[N:N + W, :], ident[:, :]).then_inc(ev("pr_stored"), 16)

            for k in range(6):
                sp.wait_ge(table_ready, k + 1)
                sp.dma_start(table.rearrange("(p c) d -> p c d", c=NC), cur[:, :, :]).then_inc(table_stored, 16)
            sp.wait_ge(ev("pr_ready"), 1)
            sp.dma_start(pr_table[0:N, :].rearrange("(p c) h -> p c h", c=NC), pr_sb[:, :, :]).then_inc(ev("pr_stored"), 16)
            sp.wait_ge(ev("pr_stored"), 32)
            sp.wait_ge(drel_stored, 32)

            def l3_loads(it, q, base, edges):
                sp.wait_ge(seg_done[q], 1 + PASS_L3 * IT + it)
                if edges == G * P:
                    sp.dma_start(X[:, q, :, D:2 * D],
                                 edge_attr[bass.ds(base * P, G * P), :].rearrange("(j e) d -> e j d", e=P)).then_inc(edges_loaded[q], 16)
                else:
                    whole = edges // P
                    sp.dma_start(X[:, q, 0:whole, D:2 * D],
                                 edge_attr[base * P:(base + whole) * P, :].rearrange("(j e) d -> e j d", e=P)).then_inc(tail_loaded, 16)
                    sp.wait_ge(tail_loaded, 16)
                    sp.dma_start(X[0:edges - whole * P, q, whole, D:2 * D],
                                 edge_attr[(base + whole) * P:E, :]).then_inc(edges_loaded[q], 16)
                sp.dma_start(drel_bc[:, q, :], drel_flat[bass.ds(base * P, G * P)].partition_broadcast(P)).then_inc(drel_loaded[q], 16)
                _, nodes = nc.values_load_multi_w_load_instructions(
                    base_row[0:1, bass.ds(base, G)], engines=[sp.engine], min_val=0, max_val=N - 1,
                    skip_runtime_bounds_check_because="dst holds node numbers")
                for j in range(G):
                    sp.dma_start(prw[:, q, j, :], pr_table[bass.ds(nodes[j], W), :]).then_inc(prw_loaded[q], 16)

            with sp.Fori(0, IT - 1) as it:
                for q in range(Q):
                    l3_loads(it, q, it * (Q * G) + q * G, G * P)
            for q in range(Q):
                l3_loads(IT - 1, q, (IT - 1) * Q * G + q * G, G * P if q < Q - 1 else LAST_EDGES)
            sp.wait_ge(ev("out_ready"), 1)
            sp.dma_start(out.rearrange("(p c) d -> p c d", c=NC), xs[:, :, :]).then_inc(ev("out_stored"), 16)
            sp.wait_ge(ev("out_stored"), 16)

        @block.gpsimd
        def _(pool):
            pool.memset(raw_dst[:, 3, :], 1000000).then_inc(pads, 1)
            pool.memset(raw_src[:, 3, :], 0).then_inc(pads, 1)
            pool.memset(raw_w[:, 3, :], 0.0).then_inc(pads, 1)
            pool.memset(ident[:, :], 0.0).then_inc(pool_chain, 1)
            pool.iota(iota_i[:, :], [[1, P]], base=0, channel_multiplier=0).then_inc(pool_chain, 1)
            pool.iota(iota_ip[:, :], [[1, 1]], base=0, channel_multiplier=1).then_inc(pool_chain, 1)
            pool.wait_ge(pool_chain, 3)
            pool.affine_select(out=ident[:, :], in_=ident[:, :], compare_op=ALU.not_equal, fill=1.0,
                               base=0, pattern=[[-1, P]], channel_multiplier=1).then_inc(fills, 1)
            pool.tensor_copy(iota_row[:, :], iota_i[:, :]).then_inc(fills, 1)
            pool.tensor_copy(iota_p[:, :], iota_ip[:, :]).then_inc(fills, 1)
            pool.memset(ones_row[:, :], 1.0).then_inc(fills, 1)
            pool.memset(neg_half[:, :], -0.5).then_inc(fills, 1)
            pool.memset(ow[:, :, :, :], 1.0).then_inc(fills, 1)
            pool.memset(X[:, :, :, :], 0.0).then_inc(fills, 1)

            def powers(k):
                pool.wait_ge(rstd_in, k)
                pool.tensor_tensor(st_b[:, :], st_a[:, :], neg_half[0:NP, :], ALU.pow).then_inc(rstd_out, 1)

            def gathers(g):
                pool.wait_ge(table_stored, 16 * (g + 1))
                with pool.Fori(0, IT) as it:
                    for q in range(Q):
                        pool.wait_ge(idx_ready[q], g * IT + it + 1)
                        pool.wait_ge(seg_done[q], 1 + (g + 1) * IT + it)
                        pool.sem_inc(gathers_begun, 1)
                        for j in range(G):
                            pool.indirect_dma_start(
                                out=X[:, q, j, 0:D], out_offset=None, in_=table,
                                in_offset=bass.IndirectOffsetOnAxis(ap=idx[:, q, j:j + 1], axis=0)).then_inc(gathered[q], 16)

            pool.wait_ge(fills, 7)
            powers(1)
            powers(2)
            powers(3)
            for g in range(3):
                gathers(g)
            powers(4)
            gathers(3)
            powers(5)
            gathers(4)
            powers(6)
            gathers(5)
            powers(7)

        def evacuate_h(act, layer):
            for k in range(ROUNDS):
                chunks = min(4, NC - 4 * k)
                act.wait_ge(ev(f"h_ps_{layer}"), k + 1)
                nc.scalar.copy(h_t[:, 4 * k:4 * k + chunks, :],
                               seg[0:D, k % 4, 0:chunks * NP].rearrange("d (c p) -> d c p", p=NP)).then_inc(ev(f"h_t_{layer}"), 1)

        @block.scalar
        def _(act):
            for free in x_t_ready + hid_ready + msg_ready:
                act.sem_inc(free, 1)

            def copy_idx(n, g, it, q):
                act.wait_ge(seg_done[q], 1 + n)
                nc.scalar.copy(idx[:, q, :], src_i[:, bass.ds(it * (Q * G) + q * G, G)]).then_inc(idx_ready[q], 1)

            act.wait_ge(ev("edge_cols"), 3)
            act.wait_ge(fills, 7)
            with act.Fori(0, IT) as it:
                for q in range(Q):
                    act.wait_ge(seg_done[q], 1 + it)
                    nc.scalar.copy(ow[:, q, :, 1], wcol[:, bass.ds(it * (Q * G) + q * G, G)]).then_inc(ev(f"ow_ready{q}"), 1)
            for g in range(5):
                with act.Fori(0, IT) as it:
                    for q in range(Q):
                        copy_idx((g + 1) * IT + it, g, it, q)
                if g == 3:
                    evacuate_h(act, "L2")
            evacuate_h(act, "L3")
            for k in range(ROUNDS):
                chunks = min(4, NC - 4 * k)
                act.wait_ge(ev("pr_ps"), k + 1)
                op = nc.scalar.copy(pr_sb[:, 4 * k:4 * k + chunks, :],
                                    big[0:NP, k % 4, 0:chunks * HID].rearrange("p (c h) -> p c h", h=HID))
                op.then_inc(ev("pr_copied"), 1)
            act.wait_ge(ev("pr_copied"), ROUNDS)
            act.sem_inc(ev("pr_ready"), 1)
            with act.Fori(0, IT) as it:
                for q in range(Q):
                    copy_idx(PASS_L3 * IT + it, 5, it, q)
                for s in range(Q + 2):
                    if s < Q:
                        r, k = s % 2, it * 2 + s // 2
                        act.wait_ge(transposed[r], k + 1)
                        act.wait_ge(hid_done[r], 1 + k)
                        nc.scalar.copy(x_t[:, r, :], big[:, r, :]).then_inc(x_t_ready[r], 1)
                    if 1 <= s <= Q:
                        r, k = (s - 1) % 2, it * 2 + (s - 1) // 2
                        act.wait_ge(hid_done[r], 1 + k + 1)
                        act.wait_ge(msg_done[r], 1 + k)
                        nc.scalar.activation(hid_t[:, r, :], big[:, 2 + r, :], ACT.Relu, bias=mb1_sb[:, 0:1]).then_inc(hid_ready[r], 1)
                    if s >= 2:
                        q = s - 2
                        r, k = q % 2, it * 2 + q // 2
                        act.wait_ge(msg_done[r], 1 + k + 1)
                        if q >= 2:
                            act.wait_ge(seg_done[q - 2], 1 + PASS_L3 * IT + it + 1)
                        else:
                            act.wait_ge(seg_done[q + 2], 1 + PASS_L3 * IT + it)
                        nc.scalar.activation(msg[:, r, :, :], seg[:, 2 + r, 0:G * D].rearrange("p (j d) -> p j d", d=D),
                                             ACT.Relu).then_inc(msg_ready[r], 1)
            for k in range(ROUNDS):
                cols = min(4, NC - 4 * k) * NP
                act.wait_ge(ev("y1_ps"), k + 1)
                if k >= 2:
                    act.wait_ge(ev("y1_used"), k - 1)
                nc.scalar.activation(y1_t[:, k % 2, 0:cols], seg[:, k % 4, 0:cols], ACT.Relu, bias=nb1_sb[:, 0:1]).then_inc(ev("y1_ready"), 1)

        @block.tensor
        def _(pe):
            for free in seg_done + hid_done + msg_done:
                pe.sem_inc(free, 1)

            def edge_pass(n0, lhs, more=None):
                with pe.Fori(0, IT) as it:
                    for q in range(Q):
                        more(it, q)
                        pe.wait_ge(onehot_ready[q], n0 + it + 1)
                        pe.wait_ge(acc_step, n0 * (Q * G) + it * (Q * G) + (q + 1) * G)
                        for j in range(G):
                            a = lhs(q, j)
                            op = nc.tensor.matmul(seg[0:a.shape[1], q, j * W:(j + 1) * W], a, onehot[:, q, j, :],
                                                  start=True, stop=True)
                        op.then_inc(seg_done[q], 1)

            def wait_rows(g):
                def f(it, q):
                    pe.wait_ge(gathered[q], 16 * G * (g * IT + it + 1))
                return f

            def wait_ow(it, q):
                pe.wait_ge(ev(f"ow_ready{q}"), it + 1)

            def turn_acc(name):
                pe.wait_ge(acc_step, Q * G + turn_acc.passes * T)
                for c in range(NC):
                    op = nc.tensor.transpose(big_nodes[:, c, :], acc_t[:, c:N:NC], ident[0:D, 0:D])
                op.then_inc(ev(name), 1)

            def turn_h(layer):
                pe.wait_ge(ev(f"h_{layer}"), 1)
                for k in range(ROUNDS):
                    if k >= 4:
                        pe.wait_ge(ev(f"h_t_{layer}"), k - 3)
                    for c in range(4 * k, min(4 * k + 4, NC)):
                        op = nc.tensor.transpose(seg[0:D, k % 4, (c % 4) * NP:(c % 4 + 1) * NP], hs[:, c, :], ident[0:NP, 0:NP])
                    op.then_inc(ev(f"h_ps_{layer}"), 1)

            pe.wait_ge(fills, 7)
            pe.wait_ge(ev("drel_t_ready"), 1)
            pe.wait_ge(ev("src_t_ready"), 1)
            for b, t in enumerate((drel_t, src_t, raw_w)):
                for c in range(4):
                    op = nc.tensor.transpose(big[:, b, c * P:(c + 1) * P], t[:, c, :], ident[:, :])
                op.then_inc(ev("cols_ps"), 1)
            pe.wait_ge(ld_w, 16 * 20)
            nc.tensor.transpose(big[0:D, 3, 0:D], w2s_sb[:, :], ident[0:D, 0:D])
            nc.tensor.transpose(big[0:D, 3, D:2 * D], w2n_sb[:, :], ident[0:D, 0:D]).then_inc(ev("w2_ps"), 1)

            edge_pass(0, lambda q, j: ow[:, q, j, :], wait_ow)
            pe.wait_ge(acc_step, Q * G + T)
            pe.wait_ge(ev("w2_t"), 2)
            for c in range(NC):
                op = nc.tensor.transpose(big[0:NP, 0, 2 * c:2 * c + 2], acc_deg[:, c:N:NC], ident[0:2, 0:2])
            op.then_inc(ev("deg_ps"), 1)
            rows = lambda q, j: X[:, q, j, 0:D]
            for g in range(3):
                edge_pass((g + 1) * IT, rows, wait_rows(g))
                turn_acc.passes = g + 2
                turn_acc(f"sum_ps{g}")
            edge_pass(PASS_L1 * IT, rows, wait_rows(3))
            turn_acc.passes = 5
            turn_acc("sum_ps3")
            pe.wait_ge(ev("conv1_in"), 1)
            for k in range(ROUNDS):
                if k >= 4:
                    pe.wait_ge(ev("conv1_t"), k - 3)
                for c in range(4 * k, min(4 * k + 4, NC)):
                    op = nc.tensor.transpose(seg[0:D, k % 4, (c % 4) * NP:(c % 4 + 1) * NP], cur[:, c, :], ident[0:NP, 0:NP])
                op.then_inc(ev("conv1_ps"), 1)
            pe.wait_ge(ev("conv1_t"), ROUNDS)
            for c in range(NC):
                op = nc.tensor.matmul(big_nodes[:, c, :], h_t[:, c, :], w1_sb[:, :], start=True, stop=True)
            op.then_inc(ev("conv1_out"), 1)
            turn_h("L2")
            pe.wait_ge(ev("h_t_L2"), ROUNDS)
            for c in range(NC):
                op = nc.tensor.matmul(big_nodes[:, c, :], h_t[:, c, :], w2s_t[:, :], start=True, stop=True)
            op.then_inc(ev("self_out"), 1)
            edge_pass(PASS_L2 * IT, rows, wait_rows(4))
            pe.wait_ge(acc_step, Q * G + 6 * T)
            pe.wait_ge(ev("self_kept"), 1)
            for c in range(NC):
                op = nc.tensor.matmul(big_nodes[:, c, :], acc_t[:, c:N:NC], w2n_t[:, :], start=True, stop=True)
            op.then_inc(ev("neigh_out"), 1)
            turn_h("L3")
            pe.wait_ge(ev("h_t_L3"), ROUNDS)
            for k in range(ROUNDS):
                if k >= 4:
                    pe.wait_ge(ev("pr_copied"), k - 3)
                for c in range(4 * k, min(4 * k + 4, NC)):
                    op = nc.tensor.matmul(big[0:NP, k % 4, (c % 4) * HID:(c % 4 + 1) * HID], h_t[:, c, :], mw1_r[:, :], start=True, stop=True)
                op.then_inc(ev("pr_ps"), 1)
            pe.wait_ge(ev("pr_copied"), ROUNDS)
            n0 = PASS_L3 * IT
            with pe.Fori(0, IT) as it:
                for s in range(Q + 3):
                    if s < Q:
                        r, k = s % 2, it * 2 + s // 2
                        pe.wait_ge(gathered[s], 16 * G * (5 * IT + it + 1))
                        pe.wait_ge(edges_loaded[s], (it + 1) * 16)
                        pe.wait_ge(x_t_ready[r], 1 + k)
                        for j in range(G):
                            op = nc.tensor.transpose(big[:, r, j * P:(j + 1) * P], X[:, s, j, :], ident[:, :])
                        op.then_inc(transposed[r], 1)
                    if 1 <= s <= Q:
                        q = s - 1
                        r, k = q % 2, it * 2 + q // 2
                        pe.wait_ge(x_t_ready[r], 1 + k + 1)
                        pe.wait_ge(hid_ready[r], 1 + k)
                        pe.wait_ge(onehot_t_ready[q], it + 1)
                        pe.wait_ge(prw_loaded[q], (it + 1) * (16 * G))
                        nc.tensor.matmul(big[:, 2 + r, :], mw1_se[:, :], x_t[:, r, :], start=True, stop=True)
                        for j in range(G):
                            op = nc.tensor.matmul(big[:, 2 + r, j * P:(j + 1) * P], prw[:, q, j, :],
                                                  onehot_t[:, q, j * P:(j + 1) * P], start=False, stop=True,
                                                  skip_group_check=True)
                        op.then_inc(hid_done[r], 1)
                    if 2 <= s <= Q + 1:
                        q = s - 2
                        r, k = q % 2, it * 2 + q // 2
                        pe.wait_ge(hid_ready[r], 1 + k + 1)
                        pe.wait_ge(msg_ready[r], 1 + k)
                        nc.tensor.matmul(seg[:, 2 + r, 0:G * D], ones_row[:, :], mb2_row[:, :, :].rearrange("a j d -> a (j d)"),
                                         start=True, stop=True)
                        for j in range(G):
                            op = nc.tensor.matmul(seg[:, 2 + r, j * D:(j + 1) * D], hid_t[:, r, j * P:(j + 1) * P],
                                                  mw2_sb[:, :], start=False, stop=True, skip_group_check=True)
                        op.then_inc(msg_done[r], 1)
                    if s >= 3:
                        q = s - 3
                        r, k = q % 2, it * 2 + q // 2
                        pe.wait_ge(msg_ready[r], 1 + k + 1)
                        pe.wait_ge(onehot_ready[q], n0 + it + 1)
                        pe.wait_ge(acc_step, Q * G - G + PASS_L3 * T + it * (Q * G) + q * G)
                        for j in range(G):
                            op = nc.tensor.matmul(seg[0:D, r, j * W:(j + 1) * W], msg[:, r, j, :], onehot[:, q, j, :],
                                                  start=True, stop=True)
                        op.then_inc(seg_done[q], 1)
            pe.wait_ge(acc_step, Q * G + NPASS * T)
            for k in range(ROUNDS + 1):
                if k < ROUNDS:
                    n = min(4, NC - 4 * k)
                    if k >= 4:
                        pe.wait_ge(ev("y1_ready"), k - 3)
                    nc.tensor.matmul(seg[:, k % 4, 0:n * NP], nw1_h[:, :], h_t[:, 4 * k:4 * k + n, :], start=True, stop=False)
                    nc.tensor.matmul(seg[:, k % 4, 0:n * NP], nw1_a[:, :],
                                     acc_t[:, 0:N].rearrange("d (p c) -> d c p", c=NC)[:, 4 * k:4 * k + n, :],
                                     start=False, stop=True).then_inc(ev("y1_ps"), 1)
                if k >= 1:
                    pe.wait_ge(ev("y1_ready"), k)
                    for c in range(4 * k - 4, min(4 * k, NC)):
                        op = nc.tensor.matmul(big_nodes[:, c, :], y1_t[:, (k - 1) % 2, (c % 4) * NP:(c % 4 + 1) * NP], nw2_sb[:, :],
                                              start=True, stop=True)
                    op.then_inc(ev("y1_used"), 1)

        @block.vector
        def _(dve):
            dve.sem_inc(acc_step, Q * G)
            links = [0]
            pows = [0]

            def link(op):
                links[0] += 1
                op.then_inc(dve_chain, 1)
                dve.wait_ge(dve_chain, links[0])

            def per_node(v):
                return v[:, :].rearrange("p (c a) -> p c a", a=1).broadcast_to([NP, NC, D])

            def per_feature(v):
                return v[0:NP, :].rearrange("p (a d) -> p a d", a=1).broadcast_to([NP, NC, D])

            def invsqrt():
                pows[0] += 1
                dve.wait_ge(rstd_out, pows[0])

            def normalize(dst_, src_):
                link(dve.tensor_reduce(st_a[:, :], src_, AX.X, ALU.add))
                link(dve.tensor_scalar(st_c[:, :], st_a[:, :], 1.0 / D, None, ALU.mult))
                link(dve.tensor_tensor(dst_, src_, per_node(st_c), ALU.subtract))
                link(dve.tensor_tensor(tmp[:, :, :], dst_, dst_, ALU.mult))
                link(dve.tensor_reduce(st_c[:, :], tmp[:, :, :], AX.X, ALU.add))
                dve.tensor_scalar(st_a[:, :], st_c[:, :], 1.0 / D, EPS, ALU.mult, ALU.add).then_inc(rstd_in, 1)
                invsqrt()
                link(dve.tensor_tensor(dst_, dst_, per_node(st_b), ALU.mult))

            def pre_ln():
                normalize(hs[:, :, :], xs[:, :, :])
                link(dve.tensor_scalar(hs[:, :, :], hs[:, :, :], 0.0, None, ALU.max))

            def clear_acc():
                link(dve.memset(acc_t[:, :], 0.0))

            def edge_pass(n, weighted=False, acc=acc_t, rows=D, l3=False):
                with dve.Fori(0, IT) as it:
                    for q in range(Q):
                        base = it * (Q * G) + q * G
                        dve.wait_ge(seg_done[q], 1 + n * IT + it)
                        for j in range(G):
                            t = base + j
                            if weighted:
                                op = dve.tensor_scalar(onehot[:, q, j, :], iota_row[:, :], drel[:, bass.ds(t, 1)], wcol[:, bass.ds(t, 1)],
                                                       ALU.is_equal, ALU.mult)
                            else:
                                op = dve.tensor_scalar(onehot[:, q, j, :], iota_row[:, :], drel[:, bass.ds(t, 1)], None, ALU.is_equal)
                        op.then_inc(onehot_ready[q], 1)
                        if l3:
                            dve.wait_ge(drel_loaded[q], (it + 1) * 16)
                            dve.tensor_scalar(onehot_t[:, q, :], drel_bc[:, q, :], iota_p[:, 0:1], None, ALU.is_equal).then_inc(onehot_t_ready[q], 1)
                    for q in range(Q):
                        base = it * (Q * G) + q * G
                        bank = q % 2 if l3 else q
                        _, nodes = nc.values_load_multi_w_load_instructions(
                            base_row[0:1, bass.ds(base, G)], engines=[dve.engine], min_val=0, max_val=N - 1,
                            skip_runtime_bounds_check_because="dst holds node numbers")
                        dve.wait_ge(seg_done[q], 1 + n * IT + it + 1)
                        for j in range(G):
                            dve.wait_ge(acc_step, Q * G + n * T + base + j)
                            window = acc[:, bass.ds(nodes[j], W)]
                            dve.tensor_tensor(window, window, seg[0:rows, bank, j * W:(j + 1) * W], ALU.add).then_inc(acc_step, 1)

            dve.wait_ge(ld_edges, 9 * 16)
            dve.tensor_copy(src_t[:, :, :], raw_src[:, :, :]).then_inc(ev("src_t_ready"), 1)
            dve.tensor_tensor(drel_t[:, :, :], raw_dst[:, :, :], raw_dst[:, :, 0:1].broadcast_to([P, 4, P]), ALU.subtract).then_inc(ev("drel_t_ready"), 1)
            dve.wait_ge(ev("cols_ps"), 3)
            dve.tensor_copy(drel[:, :], big[:, 0, :]).then_inc(ev("edge_cols"), 1)
            dve.tensor_copy(src_i[:, :], big[:, 1, :]).then_inc(ev("edge_cols"), 1)
            dve.tensor_copy(wcol[:, :], big[:, 2, :]).then_inc(ev("edge_cols"), 1)
            dve.wait_ge(ev("edge_cols"), 3)
            dve.wait_ge(ev("w2_ps"), 1)
            dve.tensor_copy(w2s_t[:, :], big[0:D, 3, 0:D]).then_inc(ev("w2_t"), 1)
            dve.tensor_copy(w2n_t[:, :], big[0:D, 3, D:2 * D]).then_inc(ev("w2_t"), 1)
            dve.wait_ge(ev("w2_t"), 2)
            dve.wait_ge(ld_x, 16)
            dve.wait_ge(fills, 7)
            dve.wait_ge(ld_base, 32)
            link(dve.memset(acc_deg[:, :], 0.0))
            pre_ln()
            edge_pass(PASS_DEG, acc=acc_deg, rows=2)
            dve.wait_ge(ev("deg_ps"), 1)
            link(dve.tensor_copy(deg[:, :, :], big[0:NP, 0, 0:2 * NC].rearrange("p (c a) -> p c a", a=2)))
            link(dve.tensor_scalar(rdeg[:, :], deg[:, :, 0], 1.0, None, ALU.max))
            dve.tensor_copy(st_a[:, :], rdeg[:, :]).then_inc(rstd_in, 1)
            link(dve.tensor_scalar(st_c[:, :], deg[:, :, 0], 0.0, None, ALU.is_gt))
            invsqrt()
            link(dve.tensor_tensor(dinv0[:, :], st_b[:, :], st_c[:, :], ALU.mult))
            link(dve.tensor_tensor(dinv0sq[:, :], dinv0[:, :], dinv0[:, :], ALU.mult))
            link(dve.reciprocal(rdeg[:, :], rdeg[:, :]))
            link(dve.tensor_scalar(deg[:, :, 1], deg[:, :, 1], 1.0, None, ALU.add))
            link(dve.tensor_scalar(dinv1[:, :], deg[:, :, 1], 0.0, None, ALU.is_gt))
            link(dve.tensor_tensor(st_c[:, :], deg[:, :, 1], dinv1[:, :], ALU.mult))
            link(dve.tensor_tensor(st_c[:, :], st_c[:, :], dinv1[:, :], ALU.subtract))
            dve.tensor_scalar(st_a[:, :], st_c[:, :], 1.0, None, ALU.add).then_inc(rstd_in, 1)
            invsqrt()
            link(dve.tensor_tensor(dinv1[:, :], dinv1[:, :], st_b[:, :], ALU.mult))

            link(dve.tensor_copy(total[:, :, :], hs[:, :, :]))
            link(dve.tensor_tensor(cur[:, :, :], hs[:, :, :], per_node(dinv0), ALU.mult))
            for g in range(3):
                clear_acc()
                dve.sem_inc(table_ready, 1)
                edge_pass(PASS_L0 + g)
                dve.wait_ge(ev(f"sum_ps{g}"), 1)
                link(dve.tensor_tensor(tmp[:, :, :], big_nodes, per_node(dinv0), ALU.mult))
                link(dve.tensor_tensor(total[:, :, :], total[:, :, :], tmp[:, :, :], ALU.add))
                if g < 2:
                    dve.wait_ge(table_stored, 16 * (g + 1))
                    link(dve.tensor_tensor(cur[:, :, :], big_nodes, per_node(dinv0sq), ALU.mult))
            link(dve.tensor_scalar(total[:, :, :], total[:, :, :], 0.25, None, ALU.mult))
            link(dve.tensor_tensor(xs[:, :, :], xs[:, :, :], total[:, :, :], ALU.add))

            pre_ln()
            link(dve.tensor_tensor(cur[:, :, :], hs[:, :, :], per_node(dinv1), ALU.mult))
            clear_acc()
            dve.sem_inc(table_ready, 1)
            edge_pass(PASS_L1, weighted=True)
            dve.wait_ge(ev("sum_ps3"), 1)
            dve.wait_ge(table_stored, 16 * 4)
            dve.tensor_tensor(cur[:, :, :], cur[:, :, :], big_nodes, ALU.add).then_inc(ev("conv1_in"), 1)
            for k in range(ROUNDS):
                chunks = min(4, NC - 4 * k)
                dve.wait_ge(ev("conv1_ps"), k + 1)
                dve.tensor_copy(h_t[:, 4 * k:4 * k + chunks, :],
                                seg[0:D, k % 4, 0:chunks * NP].rearrange("d (c p) -> d c p", p=NP)).then_inc(ev("conv1_t"), 1)
            dve.wait_ge(ev("conv1_out"), 1)
            link(dve.tensor_tensor(tmp[:, :, :], big_nodes, per_node(dinv1), ALU.mult))
            link(dve.tensor_tensor(tmp[:, :, :], tmp[:, :, :], per_feature(b1_bc), ALU.add))
            link(dve.scalar_tensor_tensor(xs[:, :, :], tmp[:, :, :], 0.0, xs[:, :, :], ALU.max, ALU.add))

            pre_ln()
            link(dve.tensor_copy(cur[:, :, :], hs[:, :, :]))
            clear_acc()
            dve.sem_inc(table_ready, 1)
            dve.sem_inc(ev("h_L2"), 1)
            dve.wait_ge(ev("self_out"), 1)
            dve.tensor_copy(total[:, :, :], big_nodes).then_inc(ev("self_kept"), 1)
            edge_pass(PASS_L2)
            dve.wait_ge(ev("self_kept"), 1)
            link(dve.tensor_tensor(xs[:, :, :], xs[:, :, :], total[:, :, :], ALU.add))
            dve.wait_ge(ev("neigh_out"), 1)
            link(dve.tensor_tensor(tmp[:, :, :], big_nodes, per_node(rdeg), ALU.mult))
            link(dve.tensor_tensor(xs[:, :, :], xs[:, :, :], tmp[:, :, :], ALU.add))

            pre_ln()
            dve.wait_ge(table_stored, 16 * 5)
            link(dve.tensor_copy(cur[:, :, :], hs[:, :, :]))
            clear_acc()
            dve.sem_inc(table_ready, 1)
            dve.sem_inc(ev("h_L3"), 1)
            edge_pass(PASS_L3, l3=True)
            dve.wait_ge(ev("y1_used"), ROUNDS)
            link(dve.tensor_tensor(total[:, :, :], big_nodes, per_feature(nb2_bc), ALU.add))
            normalize(cur[:, :, :], total[:, :, :])
            link(dve.tensor_tensor(cur[:, :, :], cur[:, :, :], per_feature(scale_bc), ALU.mult))
            link(dve.tensor_tensor(cur[:, :, :], cur[:, :, :], per_feature(offset_bc), ALU.add))
            link(dve.tensor_tensor(hs[:, :, :], hs[:, :, :], cur[:, :, :], ALU.add))
            dve.tensor_tensor(xs[:, :, :], xs[:, :, :], hs[:, :, :], ALU.add).then_inc(ev("out_ready"), 1)


_INS = ['x', 'src', 'dst', 'edge_attr_64', 'edge_weight', 'L1_gnn_W', 'L1_gnn_b', 'L2_gnn_W_self', 'L2_gnn_W_neigh',
        'L3_gnn_msg_W1', 'L3_gnn_msg_b1', 'L3_gnn_msg_W2', 'L3_gnn_msg_b2', 'L3_gnn_node_W1', 'L3_gnn_node_b1',
        'L3_gnn_node_W2', 'L3_gnn_node_b2', 'L3_gnn_ln_scale', 'L3_gnn_ln_offset']
_OUTS = [((N, D), 'float32')]


def kernel(**inputs):
    import numpy as _np
    import concourse.bacc as _bacc
    from concourse import mybir as _mybir
    from concourse.bass_utils import run_bass_kernel_spmd as _run

    nc = _bacc.Bacc("TRN2", target_bir_lowering=False, num_devices=1)
    arrays, args = {}, []
    for name in _INS:
        a = _np.ascontiguousarray(inputs[name])
        arrays[f"in_{name}_dram"] = a
        args.append(nc.dram_tensor(f"in_{name}_dram", a.shape, _mybir.dt.from_np(a.dtype), kind="ExternalInput").ap())
    for i, (shape, dtype) in enumerate(_OUTS):
        dt = _mybir.dt.from_np(_np.dtype(dtype))
        args.append(nc.dram_tensor(f"out_{i}_dram", shape, dt, kind="ExternalOutput").ap())
    build(nc, *args)
    r = _run(nc, [arrays], core_ids=[0])
    got = tuple(r.results[0][f"out_{i}_dram"] for i in range(len(_OUTS)))
    return got[0]
```

```python
from contextlib import ExitStack

import concourse.bass as bass
from concourse import mybir

F32 = mybir.dt.float32
F16 = mybir.dt.float16
BF16 = mybir.dt.bfloat16
I32 = mybir.dt.int32
ALU = mybir.AluOpType
ACT = mybir.ActivationFunctionType
AX = mybir.AxisListType

N = 3125
E = 53125
D = 64
HID = 128
P = 128
NC = -(-N // P)
NPAD = NC * P
LASTN = N - (NC - 1) * P
T = -(-E // P)
FULL = E // P
TAIL = E - FULL * P
G = 4
Q = 4
IT = T // (G * Q)
ROUNDS = -(-NC // 4)
LAST_GROUP = T // G - 1
LAST_EDGES = E - LAST_GROUP * G * P
EPS = 1e-5
W = 128
assert T == G * Q * IT

B = 16
NB = -(-N // B)
WIDE = NB * B
KB = 4
BC = P // B
LASTB = NB - (NC - 1) * BC
KC, KG = 20, 5
LOW = 2048.0
NOWHERE = 4000
THR = 208

GP = 125
PASS_DEG, PASS_L0, PASS_L1, PASS_L2, PASS_L3 = 0, 1, 4, 5, 6
NPASS = 7


def general_path(nc, sem, base_row, x, src, dst, edge_attr, edge_weight, w1, b1, w2s, w2n, mw1, mb1, mw2, mb2,
                 nw1, nb1, nw2, nb2, ln_scale, ln_offset, out):
    with ExitStack() as ctx:
        def sb(name, shape, dt=F32):
            return ctx.enter_context(nc.sbuf_tensor(name, shape, dt))

        table = nc.dram_tensor("general_table", [N, D], F32, kind="Internal").ap()
        pr_table = nc.dram_tensor("general_pr_table", [N + W, HID], F32, kind="Internal").ap()
        drel_flat = nc.dram_tensor("general_drel_flat", [T * P], F32, kind="Internal").ap()

        raw_dst = sb("general_raw_dst", [P, 4, P], I32)
        raw_src = sb("general_raw_src", [P, 4, P], I32)
        raw_w = sb("general_raw_w", [P, 4, P])
        drel_t = sb("general_drel_t", [P, 4, P])
        src_t = sb("general_src_t", [P, 4, P])
        drel = sb("general_drel", [P, 4 * P])
        src_i = sb("general_src_i", [P, 4 * P], I32)
        wcol = sb("general_wcol", [P, 4 * P])
        ident = sb("general_ident", [P, P])
        iota_i = sb("general_iota_i", [P, P], I32)
        iota_row = sb("general_iota_row", [P, P])
        iota_ip = sb("general_iota_ip", [P, 1], I32)
        iota_p = sb("general_iota_p", [P, 1])
        ones_row = sb("general_ones_row", [1, P])
        neg_half = sb("general_neg_half", [P, NC])
        w1_sb = sb("general_w1_sb", [D, D])
        w2s_sb = sb("general_w2s_sb", [D, D])
        w2n_sb = sb("general_w2n_sb", [D, D])
        w2s_t = sb("general_w2s_t", [D, D])
        w2n_t = sb("general_w2n_t", [D, D])
        mw1_se = sb("general_mw1_se", [P, HID])
        mw1_r = sb("general_mw1_r", [D, HID])
        mb1_sb = sb("general_mb1_sb", [HID, 1])
        mw2_sb = sb("general_mw2_sb", [HID, D])
        mb2_row = sb("general_mb2_row", [1, G, D])
        nw1_h = sb("general_nw1_h", [D, HID])
        nw1_a = sb("general_nw1_a", [D, HID])
        nb1_sb = sb("general_nb1_sb", [HID, 1])
        nw2_sb = sb("general_nw2_sb", [HID, D])
        b1_bc = sb("general_b1_bc", [P, D])
        nb2_bc = sb("general_nb2_bc", [P, D])
        scale_bc = sb("general_scale_bc", [P, D])
        offset_bc = sb("general_offset_bc", [P, D])
        xs = sb("general_xs", [GP, NC, D])
        hs = sb("general_hs", [GP, NC, D])
        cur = sb("general_cur", [GP, NC, D])
        tmp = sb("general_tmp", [GP, NC, D])
        total = sb("general_total", [GP, NC, D])
        st_a = sb("general_st_a", [GP, NC])
        st_b = sb("general_st_b", [GP, NC])
        st_c = sb("general_st_c", [GP, NC])
        deg = sb("general_deg", [GP, NC, 2])
        dinv0 = sb("general_dinv0", [GP, NC])
        dinv0sq = sb("general_dinv0sq", [GP, NC])
        dinv1 = sb("general_dinv1", [GP, NC])
        rdeg = sb("general_rdeg", [GP, NC])
        h_t = sb("general_h_t", [D, NC, GP])
        acc_t = sb("general_acc_t", [D, N + W])
        acc_deg = sb("general_acc_deg", [2, N + W])
        pr_sb = sb("general_pr_sb", [GP, NC, HID])
        y1_t = sb("general_y1_t", [HID, 2, 4 * GP])
        X = sb("general_X", [P, Q, G, 2 * D])
        idx = sb("general_idx", [P, Q, G], I32)
        ow = sb("general_ow", [P, Q, G, 2])
        onehot = sb("general_onehot", [P, Q, G, W])
        onehot_t = sb("general_onehot_t", [P, Q, G * P])
        drel_bc = sb("general_drel_bc", [P, Q, G * P])
        prw = sb("general_prw", [W, Q, G, HID])
        x_t = sb("general_x_t", [P, 2, G * P])
        hid_t = sb("general_hid_t", [HID, 2, G * P])
        msg = sb("general_msg", [P, 2, G, D])

        big = ctx.enter_context(nc.psum_tensor("general_big", [P, 4, 512], F32))
        seg = ctx.enter_context(nc.psum_tensor("general_seg", [P, 4, 512], F32))
        big_nodes = big[:, :, :].rearrange("p a b -> p (a b)")[0:GP, 0:NC * D].rearrange("p (c d) -> p c d", d=D)

        ld_edges, ld_x, ld_w = sem("ld_edges"), sem("ld_x"), sem("ld_w")
        fills = sem("fills")
        pads = sem("pads")
        drel_stored = sem("drel_stored")
        gathered = [sem(f"gathered{q}") for q in range(Q)]
        idx_ready = [sem(f"idx_ready{q}") for q in range(Q)]
        onehot_ready = [sem(f"onehot_ready{q}") for q in range(Q)]
        seg_done = [sem(f"seg_done{q}") for q in range(Q)]
        edges_loaded = [sem(f"edges_loaded{q}") for q in range(Q)]
        drel_loaded = [sem(f"drel_loaded{q}") for q in range(Q)]
        prw_loaded = [sem(f"prw_loaded{q}") for q in range(Q)]
        onehot_t_ready = [sem(f"onehot_t_ready{q}") for q in range(Q)]
        transposed = [sem(f"transposed{r}") for r in range(2)]
        x_t_ready = [sem(f"x_t_ready{r}") for r in range(2)]
        hid_done = [sem(f"hid_done{r}") for r in range(2)]
        hid_ready = [sem(f"hid_ready{r}") for r in range(2)]
        msg_done = [sem(f"msg_done{r}") for r in range(2)]
        msg_ready = [sem(f"msg_ready{r}") for r in range(2)]
        acc_step = sem("acc_step")
        dve_chain = sem("dve_chain")
        pool_chain = sem("pool_chain")
        acc_cleared = sem("acc_cleared")
        table_ready, table_stored = sem("table_ready"), sem("table_stored")
        rstd_in, rstd_out = sem("rstd_in"), sem("rstd_out")
        gathers_begun = sem("gathers_begun")
        tail_loaded = sem("tail_loaded")
        ev = sem

        def on_sync(sp):
            sp.dma_start(xs[:, :, :], x.rearrange("(p c) d -> p c d", c=NC)).then_inc(ld_x, 16)
            sp.wait_ge(pads, 3)
            for raw, flat in ((raw_dst, dst), (raw_src, src), (raw_w, edge_weight)):
                sp.dma_start(raw[:, 0:3, :], flat[0:3 * P * P].rearrange("(c p e) -> p c e", p=P, e=P)).then_inc(ld_edges, 16)
                sp.dma_start(raw[0:FULL - 3 * P, 3, :], flat[3 * P * P:FULL * P].rearrange("(p e) -> p e", e=P)).then_inc(ld_edges, 16)
                sp.dma_start(raw[FULL - 3 * P:T - 3 * P, 3, 0:TAIL], flat[FULL * P:E].rearrange("(p e) -> p e", p=1)).then_inc(ld_edges, 16)
            loads = [(w1_sb[:, :], w1), (w2s_sb[:, :], w2s), (w2n_sb[:, :], w2n),
                     (mw1_se[0:D, :], mw1[0:D, :]), (mw1_se[D:2 * D, :], mw1[2 * D:3 * D, :]), (mw1_r[:, :], mw1[D:2 * D, :]),
                     (mb1_sb[:, :], mb1.rearrange("(p a) -> p a", a=1)), (mw2_sb[:, :], mw2),
                     (nw1_h[:, :], nw1[0:D, :]), (nw1_a[:, :], nw1[D:2 * D, :]),
                     (nb1_sb[:, :], nb1.rearrange("(p a) -> p a", a=1)), (nw2_sb[:, :], nw2),
                     (b1_bc[:, :], b1.partition_broadcast(P)), (nb2_bc[:, :], nb2.partition_broadcast(P)),
                     (scale_bc[:, :], ln_scale.partition_broadcast(P)), (offset_bc[:, :], ln_offset.partition_broadcast(P))]
            loads += [(mb2_row[:, j, :], mb2.rearrange("(a d) -> a d", a=1)) for j in range(G)]
            for a, b in loads:
                sp.dma_start(a, b).then_inc(ld_w, 16)
            sp.wait_ge(ev("drel_t_ready"), 1)
            sp.dma_start(drel_flat[0:3 * P * P].rearrange("(c p e) -> p c e", p=P, e=P), drel_t[:, 0:3, :]).then_inc(drel_stored, 16)
            sp.dma_start(drel_flat[3 * P * P:T * P].rearrange("(p e) -> p e", e=P), drel_t[0:T - 3 * P, 3, :]).then_inc(drel_stored, 16)

            sp.wait_ge(fills, 7)
            sp.dma_start(pr_table[N:N + W, :], ident[:, :]).then_inc(ev("pr_stored"), 16)

            for k in range(6):
                sp.wait_ge(table_ready, k + 1)
                sp.dma_start(table.rearrange("(p c) d -> p c d", c=NC), cur[:, :, :]).then_inc(table_stored, 16)
            sp.wait_ge(ev("pr_ready"), 1)
            sp.dma_start(pr_table[0:N, :].rearrange("(p c) h -> p c h", c=NC), pr_sb[:, :, :]).then_inc(ev("pr_stored"), 16)
            sp.wait_ge(ev("pr_stored"), 32)
            sp.wait_ge(drel_stored, 32)

            def l3_loads(it, q, base, edges):
                sp.wait_ge(seg_done[q], 1 + PASS_L3 * IT + it)
                if edges == G * P:
                    sp.dma_start(X[:, q, :, D:2 * D],
                                 edge_attr[bass.ds(base * P, G * P), :].rearrange("(j e) d -> e j d", e=P)).then_inc(edges_loaded[q], 16)
                else:
                    whole = edges // P
                    sp.dma_start(X[:, q, 0:whole, D:2 * D],
                                 edge_attr[base * P:(base + whole) * P, :].rearrange("(j e) d -> e j d", e=P)).then_inc(tail_loaded, 16)
                    sp.wait_ge(tail_loaded, 16)
                    sp.dma_start(X[0:edges - whole * P, q, whole, D:2 * D],
                                 edge_attr[(base + whole) * P:E, :]).then_inc(edges_loaded[q], 16)
                sp.dma_start(drel_bc[:, q, :], drel_flat[bass.ds(base * P, G * P)].partition_broadcast(P)).then_inc(drel_loaded[q], 16)
                _, nodes = nc.values_load_multi_w_load_instructions(
                    base_row[0:1, bass.ds(base, G)], engines=[sp.engine], min_val=0, max_val=N - 1,
                    skip_runtime_bounds_check_because="dst holds node numbers")
                for j in range(G):
                    sp.dma_start(prw[:, q, j, :], pr_table[bass.ds(nodes[j], W), :]).then_inc(prw_loaded[q], 16)

            with sp.Fori(0, IT - 1) as it:
                for q in range(Q):
                    l3_loads(it, q, it * (Q * G) + q * G, G * P)
            for q in range(Q):
                l3_loads(IT - 1, q, (IT - 1) * Q * G + q * G, G * P if q < Q - 1 else LAST_EDGES)
            sp.wait_ge(ev("out_ready"), 1)
            sp.dma_start(out.rearrange("(p c) d -> p c d", c=NC), xs[:, :, :]).then_inc(ev("out_stored"), 16)
            sp.wait_ge(ev("out_stored"), 16)

        def on_gpsimd(pool):
            pool.memset(raw_dst[:, 3, :], 1000000).then_inc(pads, 1)
            pool.memset(raw_src[:, 3, :], 0).then_inc(pads, 1)
            pool.memset(raw_w[:, 3, :], 0.0).then_inc(pads, 1)
            pool.memset(ident[:, :], 0.0).then_inc(pool_chain, 1)
            pool.iota(iota_i[:, :], [[1, P]], base=0, channel_multiplier=0).then_inc(pool_chain, 1)
            pool.iota(iota_ip[:, :], [[1, 1]], base=0, channel_multiplier=1).then_inc(pool_chain, 1)
            pool.wait_ge(pool_chain, 3)
            pool.affine_select(out=ident[:, :], in_=ident[:, :], compare_op=ALU.not_equal, fill=1.0,
                               base=0, pattern=[[-1, P]], channel_multiplier=1).then_inc(fills, 1)
            pool.tensor_copy(iota_row[:, :], iota_i[:, :]).then_inc(fills, 1)
            pool.tensor_copy(iota_p[:, :], iota_ip[:, :]).then_inc(fills, 1)
            pool.memset(ones_row[:, :], 1.0).then_inc(fills, 1)
            pool.memset(neg_half[:, :], -0.5).then_inc(fills, 1)
            pool.memset(ow[:, :, :, :], 1.0).then_inc(fills, 1)
            pool.memset(X[:, :, :, :], 0.0).then_inc(fills, 1)

            def powers(k):
                pool.wait_ge(rstd_in, k)
                pool.tensor_tensor(st_b[:, :], st_a[:, :], neg_half[0:GP, :], ALU.pow).then_inc(rstd_out, 1)

            def gathers(g):
                pool.wait_ge(table_stored, 16 * (g + 1))
                with pool.Fori(0, IT) as it:
                    for q in range(Q):
                        pool.wait_ge(idx_ready[q], g * IT + it + 1)
                        pool.wait_ge(seg_done[q], 1 + (g + 1) * IT + it)
                        pool.sem_inc(gathers_begun, 1)
                        for j in range(G):
                            pool.indirect_dma_start(
                                out=X[:, q, j, 0:D], out_offset=None, in_=table,
                                in_offset=bass.IndirectOffsetOnAxis(ap=idx[:, q, j:j + 1], axis=0)).then_inc(gathered[q], 16)

            pool.wait_ge(fills, 7)
            powers(1)
            powers(2)
            powers(3)
            for g in range(3):
                gathers(g)
            powers(4)
            gathers(3)
            powers(5)
            gathers(4)
            powers(6)
            gathers(5)
            powers(7)

        def evacuate_h(act, layer):
            for k in range(ROUNDS):
                chunks = min(4, NC - 4 * k)
                act.wait_ge(ev(f"h_ps_{layer}"), k + 1)
                nc.scalar.copy(h_t[:, 4 * k:4 * k + chunks, :],
                               seg[0:D, k % 4, 0:chunks * GP].rearrange("d (c p) -> d c p", p=GP)).then_inc(ev(f"h_t_{layer}"), 1)

        def on_scalar(act):
            for free in x_t_ready + hid_ready + msg_ready:
                act.sem_inc(free, 1)

            def copy_idx(n, g, it, q):
                act.wait_ge(seg_done[q], 1 + n)
                nc.scalar.copy(idx[:, q, :], src_i[:, bass.ds(it * (Q * G) + q * G, G)]).then_inc(idx_ready[q], 1)

            act.wait_ge(ev("edge_cols"), 3)
            act.wait_ge(fills, 7)
            with act.Fori(0, IT) as it:
                for q in range(Q):
                    act.wait_ge(seg_done[q], 1 + it)
                    nc.scalar.copy(ow[:, q, :, 1], wcol[:, bass.ds(it * (Q * G) + q * G, G)]).then_inc(ev(f"ow_ready{q}"), 1)
            for g in range(5):
                with act.Fori(0, IT) as it:
                    for q in range(Q):
                        copy_idx((g + 1) * IT + it, g, it, q)
                if g == 3:
                    evacuate_h(act, "L2")
            evacuate_h(act, "L3")
            for k in range(ROUNDS):
                chunks = min(4, NC - 4 * k)
                act.wait_ge(ev("pr_ps"), k + 1)
                op = nc.scalar.copy(pr_sb[:, 4 * k:4 * k + chunks, :],
                                    big[0:GP, k % 4, 0:chunks * HID].rearrange("p (c h) -> p c h", h=HID))
                op.then_inc(ev("pr_copied"), 1)
            act.wait_ge(ev("pr_copied"), ROUNDS)
            act.sem_inc(ev("pr_ready"), 1)
            with act.Fori(0, IT) as it:
                for q in range(Q):
                    copy_idx(PASS_L3 * IT + it, 5, it, q)
                for s in range(Q + 2):
                    if s < Q:
                        r, k = s % 2, it * 2 + s // 2
                        act.wait_ge(transposed[r], k + 1)
                        act.wait_ge(hid_done[r], 1 + k)
                        nc.scalar.copy(x_t[:, r, :], big[:, r, :]).then_inc(x_t_ready[r], 1)
                    if 1 <= s <= Q:
                        r, k = (s - 1) % 2, it * 2 + (s - 1) // 2
                        act.wait_ge(hid_done[r], 1 + k + 1)
                        act.wait_ge(msg_done[r], 1 + k)
                        nc.scalar.activation(hid_t[:, r, :], big[:, 2 + r, :], ACT.Relu, bias=mb1_sb[:, 0:1]).then_inc(hid_ready[r], 1)
                    if s >= 2:
                        q = s - 2
                        r, k = q % 2, it * 2 + q // 2
                        act.wait_ge(msg_done[r], 1 + k + 1)
                        if q >= 2:
                            act.wait_ge(seg_done[q - 2], 1 + PASS_L3 * IT + it + 1)
                        else:
                            act.wait_ge(seg_done[q + 2], 1 + PASS_L3 * IT + it)
                        nc.scalar.activation(msg[:, r, :, :], seg[:, 2 + r, 0:G * D].rearrange("p (j d) -> p j d", d=D),
                                             ACT.Relu).then_inc(msg_ready[r], 1)
            for k in range(ROUNDS):
                cols = min(4, NC - 4 * k) * GP
                act.wait_ge(ev("y1_ps"), k + 1)
                if k >= 2:
                    act.wait_ge(ev("y1_used"), k - 1)
                nc.scalar.activation(y1_t[:, k % 2, 0:cols], seg[:, k % 4, 0:cols], ACT.Relu, bias=nb1_sb[:, 0:1]).then_inc(ev("y1_ready"), 1)

        def on_tensor(pe):
            for free in seg_done + hid_done + msg_done:
                pe.sem_inc(free, 1)

            def edge_pass(n0, lhs, more=None):
                with pe.Fori(0, IT) as it:
                    for q in range(Q):
                        more(it, q)
                        pe.wait_ge(onehot_ready[q], n0 + it + 1)
                        pe.wait_ge(acc_step, n0 * (Q * G) + it * (Q * G) + (q + 1) * G)
                        for j in range(G):
                            a = lhs(q, j)
                            op = nc.tensor.matmul(seg[0:a.shape[1], q, j * W:(j + 1) * W], a, onehot[:, q, j, :],
                                                  start=True, stop=True)
                        op.then_inc(seg_done[q], 1)

            def wait_rows(g):
                def f(it, q):
                    pe.wait_ge(gathered[q], 16 * G * (g * IT + it + 1))
                return f

            def wait_ow(it, q):
                pe.wait_ge(ev(f"ow_ready{q}"), it + 1)

            def turn_acc(name):
                pe.wait_ge(acc_step, Q * G + turn_acc.passes * T)
                for c in range(NC):
                    op = nc.tensor.transpose(big_nodes[:, c, :], acc_t[:, c:N:NC], ident[0:D, 0:D])
                op.then_inc(ev(name), 1)

            def turn_h(layer):
                pe.wait_ge(ev(f"h_{layer}"), 1)
                for k in range(ROUNDS):
                    if k >= 4:
                        pe.wait_ge(ev(f"h_t_{layer}"), k - 3)
                    for c in range(4 * k, min(4 * k + 4, NC)):
                        op = nc.tensor.transpose(seg[0:D, k % 4, (c % 4) * GP:(c % 4 + 1) * GP], hs[:, c, :], ident[0:GP, 0:GP])
                    op.then_inc(ev(f"h_ps_{layer}"), 1)

            pe.wait_ge(fills, 7)
            pe.wait_ge(ev("drel_t_ready"), 1)
            pe.wait_ge(ev("src_t_ready"), 1)
            for b, t in enumerate((drel_t, src_t, raw_w)):
                for c in range(4):
                    op = nc.tensor.transpose(big[:, b, c * P:(c + 1) * P], t[:, c, :], ident[:, :])
                op.then_inc(ev("cols_ps"), 1)
            pe.wait_ge(ld_w, 16 * 20)
            nc.tensor.transpose(big[0:D, 3, 0:D], w2s_sb[:, :], ident[0:D, 0:D])
            nc.tensor.transpose(big[0:D, 3, D:2 * D], w2n_sb[:, :], ident[0:D, 0:D]).then_inc(ev("w2_ps"), 1)

            edge_pass(0, lambda q, j: ow[:, q, j, :], wait_ow)
            pe.wait_ge(acc_step, Q * G + T)
            pe.wait_ge(ev("w2_t"), 2)
            for c in range(NC):
                op = nc.tensor.transpose(big[0:GP, 0, 2 * c:2 * c + 2], acc_deg[:, c:N:NC], ident[0:2, 0:2])
            op.then_inc(ev("deg_ps"), 1)
            rows = lambda q, j: X[:, q, j, 0:D]
            for g in range(3):
                edge_pass((g + 1) * IT, rows, wait_rows(g))
                turn_acc.passes = g + 2
                turn_acc(f"sum_ps{g}")
            edge_pass(PASS_L1 * IT, rows, wait_rows(3))
            turn_acc.passes = 5
            turn_acc("sum_ps3")
            pe.wait_ge(ev("conv1_in"), 1)
            for k in range(ROUNDS):
                if k >= 4:
                    pe.wait_ge(ev("conv1_t"), k - 3)
                for c in range(4 * k, min(4 * k + 4, NC)):
                    op = nc.tensor.transpose(seg[0:D, k % 4, (c % 4) * GP:(c % 4 + 1) * GP], cur[:, c, :], ident[0:GP, 0:GP])
                op.then_inc(ev("conv1_ps"), 1)
            pe.wait_ge(ev("conv1_t"), ROUNDS)
            for c in range(NC):
                op = nc.tensor.matmul(big_nodes[:, c, :], h_t[:, c, :], w1_sb[:, :], start=True, stop=True)
            op.then_inc(ev("conv1_out"), 1)
            turn_h("L2")
            pe.wait_ge(ev("h_t_L2"), ROUNDS)
            for c in range(NC):
                op = nc.tensor.matmul(big_nodes[:, c, :], h_t[:, c, :], w2s_t[:, :], start=True, stop=True)
            op.then_inc(ev("self_out"), 1)
            edge_pass(PASS_L2 * IT, rows, wait_rows(4))
            pe.wait_ge(acc_step, Q * G + 6 * T)
            pe.wait_ge(ev("self_kept"), 1)
            for c in range(NC):
                op = nc.tensor.matmul(big_nodes[:, c, :], acc_t[:, c:N:NC], w2n_t[:, :], start=True, stop=True)
            op.then_inc(ev("neigh_out"), 1)
            turn_h("L3")
            pe.wait_ge(ev("h_t_L3"), ROUNDS)
            for k in range(ROUNDS):
                if k >= 4:
                    pe.wait_ge(ev("pr_copied"), k - 3)
                for c in range(4 * k, min(4 * k + 4, NC)):
                    op = nc.tensor.matmul(big[0:GP, k % 4, (c % 4) * HID:(c % 4 + 1) * HID], h_t[:, c, :], mw1_r[:, :], start=True, stop=True)
                op.then_inc(ev("pr_ps"), 1)
            pe.wait_ge(ev("pr_copied"), ROUNDS)
            n0 = PASS_L3 * IT
            with pe.Fori(0, IT) as it:
                for s in range(Q + 3):
                    if s < Q:
                        r, k = s % 2, it * 2 + s // 2
                        pe.wait_ge(gathered[s], 16 * G * (5 * IT + it + 1))
                        pe.wait_ge(edges_loaded[s], (it + 1) * 16)
                        pe.wait_ge(x_t_ready[r], 1 + k)
                        for j in range(G):
                            op = nc.tensor.transpose(big[:, r, j * P:(j + 1) * P], X[:, s, j, :], ident[:, :])
                        op.then_inc(transposed[r], 1)
                    if 1 <= s <= Q:
                        q = s - 1
                        r, k = q % 2, it * 2 + q // 2
                        pe.wait_ge(x_t_ready[r], 1 + k + 1)
                        pe.wait_ge(hid_ready[r], 1 + k)
                        pe.wait_ge(onehot_t_ready[q], it + 1)
                        pe.wait_ge(prw_loaded[q], (it + 1) * (16 * G))
                        nc.tensor.matmul(big[:, 2 + r, :], mw1_se[:, :], x_t[:, r, :], start=True, stop=True)
                        for j in range(G):
                            op = nc.tensor.matmul(big[:, 2 + r, j * P:(j + 1) * P], prw[:, q, j, :],
                                                  onehot_t[:, q, j * P:(j + 1) * P], start=False, stop=True,
                                                  skip_group_check=True)
                        op.then_inc(hid_done[r], 1)
                    if 2 <= s <= Q + 1:
                        q = s - 2
                        r, k = q % 2, it * 2 + q // 2
                        pe.wait_ge(hid_ready[r], 1 + k + 1)
                        pe.wait_ge(msg_ready[r], 1 + k)
                        nc.tensor.matmul(seg[:, 2 + r, 0:G * D], ones_row[:, :], mb2_row[:, :, :].rearrange("a j d -> a (j d)"),
                                         start=True, stop=True)
                        for j in range(G):
                            op = nc.tensor.matmul(seg[:, 2 + r, j * D:(j + 1) * D], hid_t[:, r, j * P:(j + 1) * P],
                                                  mw2_sb[:, :], start=False, stop=True, skip_group_check=True)
                        op.then_inc(msg_done[r], 1)
                    if s >= 3:
                        q = s - 3
                        r, k = q % 2, it * 2 + q // 2
                        pe.wait_ge(msg_ready[r], 1 + k + 1)
                        pe.wait_ge(onehot_ready[q], n0 + it + 1)
                        pe.wait_ge(acc_step, Q * G - G + PASS_L3 * T + it * (Q * G) + q * G)
                        for j in range(G):
                            op = nc.tensor.matmul(seg[0:D, r, j * W:(j + 1) * W], msg[:, r, j, :], onehot[:, q, j, :],
                                                  start=True, stop=True)
                        op.then_inc(seg_done[q], 1)
            pe.wait_ge(acc_step, Q * G + NPASS * T)
            for k in range(ROUNDS + 1):
                if k < ROUNDS:
                    n = min(4, NC - 4 * k)
                    if k >= 4:
                        pe.wait_ge(ev("y1_ready"), k - 3)
                    nc.tensor.matmul(seg[:, k % 4, 0:n * GP], nw1_h[:, :], h_t[:, 4 * k:4 * k + n, :], start=True, stop=False)
                    nc.tensor.matmul(seg[:, k % 4, 0:n * GP], nw1_a[:, :],
                                     acc_t[:, 0:N].rearrange("d (p c) -> d c p", c=NC)[:, 4 * k:4 * k + n, :],
                                     start=False, stop=True).then_inc(ev("y1_ps"), 1)
                if k >= 1:
                    pe.wait_ge(ev("y1_ready"), k)
                    for c in range(4 * k - 4, min(4 * k, NC)):
                        op = nc.tensor.matmul(big_nodes[:, c, :], y1_t[:, (k - 1) % 2, (c % 4) * GP:(c % 4 + 1) * GP], nw2_sb[:, :],
                                              start=True, stop=True)
                    op.then_inc(ev("y1_used"), 1)

        def on_vector(dve):
            dve.sem_inc(acc_step, Q * G)
            links = [0]
            pows = [0]

            def link(op):
                links[0] += 1
                op.then_inc(dve_chain, 1)
                dve.wait_ge(dve_chain, links[0])

            def per_node(v):
                return v[:, :].rearrange("p (c a) -> p c a", a=1).broadcast_to([GP, NC, D])

            def per_feature(v):
                return v[0:GP, :].rearrange("p (a d) -> p a d", a=1).broadcast_to([GP, NC, D])

            def invsqrt():
                pows[0] += 1
                dve.wait_ge(rstd_out, pows[0])

            def normalize(dst_, src_):
                link(dve.tensor_reduce(st_a[:, :], src_, AX.X, ALU.add))
                link(dve.tensor_scalar(st_c[:, :], st_a[:, :], 1.0 / D, None, ALU.mult))
                link(dve.tensor_tensor(dst_, src_, per_node(st_c), ALU.subtract))
                link(dve.tensor_tensor(tmp[:, :, :], dst_, dst_, ALU.mult))
                link(dve.tensor_reduce(st_c[:, :], tmp[:, :, :], AX.X, ALU.add))
                dve.tensor_scalar(st_a[:, :], st_c[:, :], 1.0 / D, EPS, ALU.mult, ALU.add).then_inc(rstd_in, 1)
                invsqrt()
                link(dve.tensor_tensor(dst_, dst_, per_node(st_b), ALU.mult))

            def pre_ln():
                normalize(hs[:, :, :], xs[:, :, :])
                link(dve.tensor_scalar(hs[:, :, :], hs[:, :, :], 0.0, None, ALU.max))

            def clear_acc():
                link(dve.memset(acc_t[:, :], 0.0))

            def edge_pass(n, weighted=False, acc=acc_t, rows=D, l3=False):
                with dve.Fori(0, IT) as it:
                    for q in range(Q):
                        base = it * (Q * G) + q * G
                        dve.wait_ge(seg_done[q], 1 + n * IT + it)
                        for j in range(G):
                            t = base + j
                            if weighted:
                                op = dve.tensor_scalar(onehot[:, q, j, :], iota_row[:, :], drel[:, bass.ds(t, 1)], wcol[:, bass.ds(t, 1)],
                                                       ALU.is_equal, ALU.mult)
                            else:
                                op = dve.tensor_scalar(onehot[:, q, j, :], iota_row[:, :], drel[:, bass.ds(t, 1)], None, ALU.is_equal)
                        op.then_inc(onehot_ready[q], 1)
                        if l3:
                            dve.wait_ge(drel_loaded[q], (it + 1) * 16)
                            dve.tensor_scalar(onehot_t[:, q, :], drel_bc[:, q, :], iota_p[:, 0:1], None, ALU.is_equal).then_inc(onehot_t_ready[q], 1)
                    for q in range(Q):
                        base = it * (Q * G) + q * G
                        bank = q % 2 if l3 else q
                        _, nodes = nc.values_load_multi_w_load_instructions(
                            base_row[0:1, bass.ds(base, G)], engines=[dve.engine], min_val=0, max_val=N - 1,
                            skip_runtime_bounds_check_because="dst holds node numbers")
                        dve.wait_ge(seg_done[q], 1 + n * IT + it + 1)
                        for j in range(G):
                            dve.wait_ge(acc_step, Q * G + n * T + base + j)
                            window = acc[:, bass.ds(nodes[j], W)]
                            dve.tensor_tensor(window, window, seg[0:rows, bank, j * W:(j + 1) * W], ALU.add).then_inc(acc_step, 1)

            dve.wait_ge(ld_edges, 9 * 16)
            dve.tensor_copy(src_t[:, :, :], raw_src[:, :, :]).then_inc(ev("src_t_ready"), 1)
            dve.tensor_tensor(drel_t[:, :, :], raw_dst[:, :, :], raw_dst[:, :, 0:1].broadcast_to([P, 4, P]), ALU.subtract).then_inc(ev("drel_t_ready"), 1)
            dve.wait_ge(ev("cols_ps"), 3)
            dve.tensor_copy(drel[:, :], big[:, 0, :]).then_inc(ev("edge_cols"), 1)
            dve.tensor_copy(src_i[:, :], big[:, 1, :]).then_inc(ev("edge_cols"), 1)
            dve.tensor_copy(wcol[:, :], big[:, 2, :]).then_inc(ev("edge_cols"), 1)
            dve.wait_ge(ev("edge_cols"), 3)
            dve.wait_ge(ev("w2_ps"), 1)
            dve.tensor_copy(w2s_t[:, :], big[0:D, 3, 0:D]).then_inc(ev("w2_t"), 1)
            dve.tensor_copy(w2n_t[:, :], big[0:D, 3, D:2 * D]).then_inc(ev("w2_t"), 1)
            dve.wait_ge(ev("w2_t"), 2)
            dve.wait_ge(ld_x, 16)
            dve.wait_ge(fills, 7)
            link(dve.memset(acc_deg[:, :], 0.0))
            pre_ln()
            edge_pass(PASS_DEG, acc=acc_deg, rows=2)
            dve.wait_ge(ev("deg_ps"), 1)
            link(dve.tensor_copy(deg[:, :, :], big[0:GP, 0, 0:2 * NC].rearrange("p (c a) -> p c a", a=2)))
            link(dve.tensor_scalar(rdeg[:, :], deg[:, :, 0], 1.0, None, ALU.max))
            dve.tensor_copy(st_a[:, :], rdeg[:, :]).then_inc(rstd_in, 1)
            link(dve.tensor_scalar(st_c[:, :], deg[:, :, 0], 0.0, None, ALU.is_gt))
            invsqrt()
            link(dve.tensor_tensor(dinv0[:, :], st_b[:, :], st_c[:, :], ALU.mult))
            link(dve.tensor_tensor(dinv0sq[:, :], dinv0[:, :], dinv0[:, :], ALU.mult))
            link(dve.reciprocal(rdeg[:, :], rdeg[:, :]))
            link(dve.tensor_scalar(deg[:, :, 1], deg[:, :, 1], 1.0, None, ALU.add))
            link(dve.tensor_scalar(dinv1[:, :], deg[:, :, 1], 0.0, None, ALU.is_gt))
            link(dve.tensor_tensor(st_c[:, :], deg[:, :, 1], dinv1[:, :], ALU.mult))
            link(dve.tensor_tensor(st_c[:, :], st_c[:, :], dinv1[:, :], ALU.subtract))
            dve.tensor_scalar(st_a[:, :], st_c[:, :], 1.0, None, ALU.add).then_inc(rstd_in, 1)
            invsqrt()
            link(dve.tensor_tensor(dinv1[:, :], dinv1[:, :], st_b[:, :], ALU.mult))

            link(dve.tensor_copy(total[:, :, :], hs[:, :, :]))
            link(dve.tensor_tensor(cur[:, :, :], hs[:, :, :], per_node(dinv0), ALU.mult))
            for g in range(3):
                clear_acc()
                dve.sem_inc(table_ready, 1)
                edge_pass(PASS_L0 + g)
                dve.wait_ge(ev(f"sum_ps{g}"), 1)
                link(dve.tensor_tensor(tmp[:, :, :], big_nodes, per_node(dinv0), ALU.mult))
                link(dve.tensor_tensor(total[:, :, :], total[:, :, :], tmp[:, :, :], ALU.add))
                if g < 2:
                    dve.wait_ge(table_stored, 16 * (g + 1))
                    link(dve.tensor_tensor(cur[:, :, :], big_nodes, per_node(dinv0sq), ALU.mult))
            link(dve.tensor_scalar(total[:, :, :], total[:, :, :], 0.25, None, ALU.mult))
            link(dve.tensor_tensor(xs[:, :, :], xs[:, :, :], total[:, :, :], ALU.add))

            pre_ln()
            link(dve.tensor_tensor(cur[:, :, :], hs[:, :, :], per_node(dinv1), ALU.mult))
            clear_acc()
            dve.sem_inc(table_ready, 1)
            edge_pass(PASS_L1, weighted=True)
            dve.wait_ge(ev("sum_ps3"), 1)
            dve.wait_ge(table_stored, 16 * 4)
            dve.tensor_tensor(cur[:, :, :], cur[:, :, :], big_nodes, ALU.add).then_inc(ev("conv1_in"), 1)
            for k in range(ROUNDS):
                chunks = min(4, NC - 4 * k)
                dve.wait_ge(ev("conv1_ps"), k + 1)
                dve.tensor_copy(h_t[:, 4 * k:4 * k + chunks, :],
                                seg[0:D, k % 4, 0:chunks * GP].rearrange("d (c p) -> d c p", p=GP)).then_inc(ev("conv1_t"), 1)
            dve.wait_ge(ev("conv1_out"), 1)
            link(dve.tensor_tensor(tmp[:, :, :], big_nodes, per_node(dinv1), ALU.mult))
            link(dve.tensor_tensor(tmp[:, :, :], tmp[:, :, :], per_feature(b1_bc), ALU.add))
            link(dve.scalar_tensor_tensor(xs[:, :, :], tmp[:, :, :], 0.0, xs[:, :, :], ALU.max, ALU.add))

            pre_ln()
            link(dve.tensor_copy(cur[:, :, :], hs[:, :, :]))
            clear_acc()
            dve.sem_inc(table_ready, 1)
            dve.sem_inc(ev("h_L2"), 1)
            dve.wait_ge(ev("self_out"), 1)
            dve.tensor_copy(total[:, :, :], big_nodes).then_inc(ev("self_kept"), 1)
            edge_pass(PASS_L2)
            dve.wait_ge(ev("self_kept"), 1)
            link(dve.tensor_tensor(xs[:, :, :], xs[:, :, :], total[:, :, :], ALU.add))
            dve.wait_ge(ev("neigh_out"), 1)
            link(dve.tensor_tensor(tmp[:, :, :], big_nodes, per_node(rdeg), ALU.mult))
            link(dve.tensor_tensor(xs[:, :, :], xs[:, :, :], tmp[:, :, :], ALU.add))

            pre_ln()
            dve.wait_ge(table_stored, 16 * 5)
            link(dve.tensor_copy(cur[:, :, :], hs[:, :, :]))
            clear_acc()
            dve.sem_inc(table_ready, 1)
            dve.sem_inc(ev("h_L3"), 1)
            edge_pass(PASS_L3, l3=True)
            dve.wait_ge(ev("y1_used"), ROUNDS)
            link(dve.tensor_tensor(total[:, :, :], big_nodes, per_feature(nb2_bc), ALU.add))
            normalize(cur[:, :, :], total[:, :, :])
            link(dve.tensor_tensor(cur[:, :, :], cur[:, :, :], per_feature(scale_bc), ALU.mult))
            link(dve.tensor_tensor(cur[:, :, :], cur[:, :, :], per_feature(offset_bc), ALU.add))
            link(dve.tensor_tensor(hs[:, :, :], hs[:, :, :], cur[:, :, :], ALU.add))
            dve.tensor_tensor(xs[:, :, :], xs[:, :, :], hs[:, :, :], ALU.add).then_inc(ev("out_ready"), 1)

        return {'sync': on_sync, 'gpsimd': on_gpsimd, 'scalar': on_scalar, 'tensor': on_tensor, 'vector': on_vector}


def dense_path(nc, sem, base_row, x, src, dst, edge_attr, edge_weight, w1, b1, w2s, w2n, mw1, mb1, mw2, mb2,
               nw1, nb1, nw2, nb2, ln_scale, ln_offset, out):
    with ExitStack() as ctx:
        def sb(name, shape, dt=F32):
            return ctx.enter_context(nc.sbuf_tensor(name, shape, dt))

        table = nc.dram_tensor("table", [NPAD, D], F32, kind="Internal").ap()
        pr_table = nc.dram_tensor("pr_table", [NPAD + W, HID], F32, kind="Internal").ap()
        drel_flat = nc.dram_tensor("drel_flat", [T * P], F32, kind="Internal").ap()

        A = sb("A", [P, NC, WIDE], F16)
        a_words = A[:, :, :].rearrange("p s d -> p (s d)").bitcast(F32)
        carved = {"prep": 0, "l3": 0}

        def carve(phase, n):
            at = carved[phase]
            carved[phase] = at + n
            assert at + n <= NC * WIDE // 2
            return a_words[:, at:at + n]

        raw_dst, raw_src, raw_w = (carve("prep", 4 * P) for _ in range(3))
        raw_dst, raw_src = raw_dst.bitcast(I32), raw_src.bitcast(I32)
        src_lo, src_hi, dst_lo, dst_hi = (carve("prep", 4 * P).bitcast(I32) for _ in range(4))
        drel_t, src_t, dst_t, key_r_t, key_l_t = (carve("prep", 4 * P) for _ in range(5))
        below = carve("prep", 4 * THR)
        starts = carve("prep", THR)
        starts_i = carve("prep", THR).bitcast(I32)
        w_res = carve("prep", 4 * P)

        drel = sb("drel", [P, 4 * P])
        src_i = sb("src_i", [P, 4 * P], I32)
        wcol = sb("wcol", [P, 4 * P])
        first_row = sb("first_row", [1, THR], I32)
        ident = sb("ident", [P, P])
        iota_row = sb("iota_row", [P, P])
        iota_p = sb("iota_p", [P, 1])
        iota_4 = sb("iota_4", [P, P, 4], F16)
        block_rel = sb("block_rel", [P, 2, KB], F16)
        chunk_rel = sb("chunk_rel", [P, KC], F16)
        iota_r = sb("iota_r", [P, NC * B], F16)
        block_key = sb("block_key", [P, NC * BC])
        chunk_start = sb("chunk_start", [P, NC])
        ones = sb("ones", [P, 1])
        ones_row = sb("ones_row", [1, P], BF16)
        neg_half = sb("neg_half", [P, NC])
        join = sb("join", [P, D])
        w1_sb = sb("w1_sb", [D, D])
        w2_cat = sb("w2_cat", [D, 2 * D])
        w2_t = sb("w2_t", [2 * D, D])
        mw1_r = sb("mw1_r", [D, HID])
        b1_bc = sb("b1_bc", [P, D])
        xs = sb("xs", [P, NC, D])
        cur = sb("cur", [P, NC, D])
        pair = sb("pair", [P, NC * 2 * D])
        acc_mem = sb("acc_mem", [P, NPAD + W])
        st_a = sb("st_a", [P, NC])
        st_b = sb("st_b", [P, NC])
        st_c = sb("st_c", [P, NC])
        deg = sb("deg", [P, NC, 4])
        dinv0 = sb("dinv0", [P, NC])
        dinv0sq = sb("dinv0sq", [P, NC])
        dinv1 = sb("dinv1", [P, NC])
        rdeg = sb("rdeg", [P, NC])
        idx = sb("idx", [P, Q, G], I32)

        key_r, key_l, dst_c = (pair[:, k * 4 * P:(k + 1) * 4 * P] for k in range(3))
        total = pair[:, NC * D:2 * NC * D].rearrange("p (c d) -> p c d", d=D)
        hop = pair[:, 0:NC * D].rearrange("p (c d) -> p c d", d=D)
        rows1 = pair[:, 0:Q * G * D].rearrange("p (q j d) -> p q j d", q=Q, j=G)
        onehot1 = pair[:, Q * G * D:Q * G * (D + W)].rearrange("p (q j w) -> p q j w", q=Q, j=G)
        turn1 = pair[0:D, Q * G * (D + W):Q * G * (D + W) + P]
        h_nb = pair[:, :].rearrange("p (c d) -> p c d", d=2 * D)
        hs = h_nb[:, :, 0:D]
        nb = h_nb[:, :, D:2 * D]
        acc_h = acc_mem[:, :].bitcast(F16)
        hot_r = acc_h[:, 0:2 * KB * NC * B].rearrange("p (b k v) -> p b k v", b=2, k=KB)
        hot_l = acc_h[:, 2 * KB * NC * B:2 * KB * (NC * B + P)].rearrange("p (b v k) -> p b v k", b=2, k=KB)
        w_parts = acc_mem[:, :].bitcast(BF16)[:, 2 * KB * (NC * B + P):2 * KB * (NC * B + P) + 4 * P * 4].rearrange("p (t v) -> p t v", v=4)
        half = NC * 2 * D
        x_parts = [m.bitcast(F16)[:, 0:half].rearrange("p (s k d) -> p s k d", k=2, d=D)
                   for m in (acc_mem[:, 0:half // 2], pair[:, 0:half // 2])]
        sums_t = acc_mem[:, half // 2:half // 2 + 2 * 4 * P].rearrange("p (r e) -> p r e", r=2)
        ln_tmp = acc_mem[:, 0:NC * D].rearrange("p (c d) -> p c d", d=D)
        acc_t = acc_mem[0:D, :]
        hot_d = cur[:, :, :].rearrange("p c d -> p (c d)").bitcast(F16)[:, 0:KG * 4 * P].rearrange("p (g v k) -> p g v k", g=KG, k=4)

        X = carve("l3", Q * G * 2 * D).rearrange("p (q j d) -> p q j d", q=Q, j=G)
        onehot3 = carve("l3", Q * G * W).rearrange("p (q j w) -> p q j w", q=Q, j=G)
        onehot_t = carve("l3", Q * G * P).rearrange("p (q e) -> p q e", q=Q)
        drel_bc = carve("l3", Q * G * P).rearrange("p (q e) -> p q e", q=Q)
        prw = carve("l3", Q * G * HID).rearrange("p (q j h) -> p q j h", q=Q, j=G)
        x_t = carve("l3", 2 * G * P).rearrange("p (r e) -> p r e", r=2)
        hid_t = carve("l3", 2 * G * P).rearrange("p (r e) -> p r e", r=2)
        msg = carve("l3", 2 * G * D).rearrange("p (r j d) -> p r j d", r=2, j=G)
        pr_sb = carve("l3", NC * HID).rearrange("p (c h) -> p c h", h=HID)
        h_t = carve("l3", NPAD)[0:D, :]
        y1_t = carve("l3", 2 * 4 * P).rearrange("p (r e) -> p r e", r=2)
        mw1_se = carve("l3", HID)
        mb1_sb = carve("l3", 1)
        mw2_sb = carve("l3", D)
        mb2_row = carve("l3", G * D)[0:1, :]
        mb2_rest = carve("l3", G * D)[0:1, :]
        mb2_parts = carve("l3", 3 * G * D // 2).bitcast(BF16)[0:1, :].rearrange("a (k d) -> a k d", k=3)
        nw1_h = carve("l3", HID)[0:D, :]
        nw1_a = carve("l3", HID)[0:D, :]
        nb1_sb = carve("l3", 1)
        nw2_sb = carve("l3", D)
        nb2_bc = carve("l3", D)
        scale_bc = carve("l3", D)
        offset_bc = carve("l3", D)
        turn2_ring = acc_mem[:, 0:2 * 4 * P].rearrange("p (r e) -> p r e", r=2)
        scratch = a_words[:, NC * WIDE // 2 - NC * D:NC * WIDE // 2].rearrange("p (c d) -> p c d", d=D)

        big = ctx.enter_context(nc.psum_tensor("big", [P, 4, 512], F32))
        seg = ctx.enter_context(nc.psum_tensor("seg", [P, 4, 512], F32))
        big_nodes = big[:, :, :].rearrange("p a b -> p (a b)")[:, 0:NC * D].rearrange("p (c d) -> p c d", d=D)
        banks = [big[:, b, :] for b in range(4)] + [seg[:, b, :] for b in range(4)]

        ld_edges, ld_x, ld_w, ld_l3 = sem("ld_edges"), sem("ld_x"), sem("ld_w"), sem("ld_l3")
        fills = sem("fills")
        pads = sem("pads")
        drel_stored = sem("drel_stored")
        hots_ready = [sem(f"hots_ready{b}") for b in range(2)]
        block_built = [sem(f"block_built{b}") for b in range(2)]
        block_kept = [sem(f"block_kept{b}") for b in range(2)]
        hot_d_ready = [sem(f"hot_d_ready{g}") for g in range(KG)]
        hot_d_used = [sem(f"hot_d_used{g}") for g in range(KG)]
        block_rel_ready, chunk_rel_ready = sem("block_rel_ready"), sem("chunk_rel_ready")
        gathered = [sem(f"gathered{q}") for q in range(Q)]
        idx_ready = [sem(f"idx_ready{q}") for q in range(Q)]
        onehot_ready = [sem(f"onehot_ready{q}") for q in range(Q)]
        seg_done = [sem(f"seg_done{q}") for q in range(Q)]
        edges_loaded = [sem(f"edges_loaded{q}") for q in range(Q)]
        drel_loaded = [sem(f"drel_loaded{q}") for q in range(Q)]
        prw_loaded = [sem(f"prw_loaded{q}") for q in range(Q)]
        onehot_t_ready = [sem(f"onehot_t_ready{q}") for q in range(Q)]
        transposed = [sem(f"transposed{r}") for r in range(2)]
        x_t_ready = [sem(f"x_t_ready{r}") for r in range(2)]
        hid_done = [sem(f"hid_done{r}") for r in range(2)]
        hid_ready = [sem(f"hid_ready{r}") for r in range(2)]
        msg_done = [sem(f"msg_done{r}") for r in range(2)]
        msg_ready = [sem(f"msg_ready{r}") for r in range(2)]
        acc_step = sem("acc_step")
        dve_chain = sem("dve_chain")
        pool_chain = sem("pool_chain")
        table_ready, table_stored = sem("table_ready"), sem("table_stored")
        rstd_in, rstd_out = sem("rstd_in"), sem("rstd_out")
        waits_carried = sem("waits_carried")
        tail_loaded = sem("tail_loaded")
        ev = sem

        def round_nodes(n, k):
            return big[:, (n * ROUNDS + k) % 4, 0:4 * D].rearrange("p (c d) -> p c d", d=D)

        def load_nodes(eng, row, at, n, top):
            _, v = nc.values_load_multi_w_load_instructions(
                row[0:1, bass.ds(at, n)], engines=[eng.engine], min_val=0, max_val=top,
                skip_runtime_bounds_check_because="node or tile numbers, bounded where they were made")
            return v

        def on_sync(sp):
            sp.wait_ge(pads, 4)
            for raw, flat in ((raw_dst, dst), (raw_src, src), (raw_w, edge_weight)):
                raw = raw.rearrange("p (c e) -> p c e", e=P)
                sp.dma_start(raw[:, 0:3, :], flat[0:3 * P * P].rearrange("(c p e) -> p c e", p=P, e=P)).then_inc(ld_edges, 16)
                sp.dma_start(raw[0:FULL - 3 * P, 3, :], flat[3 * P * P:FULL * P].rearrange("(p e) -> p e", e=P)).then_inc(ld_edges, 16)
                sp.dma_start(raw[FULL - 3 * P:T - 3 * P, 3, 0:TAIL], flat[FULL * P:E].rearrange("(p e) -> p e", p=1)).then_inc(ld_edges, 16)
            sp.dma_start(xs[:, 0:NC - 1, :], x[0:(NC - 1) * P, :].rearrange("(c p) d -> p c d", p=P)).then_inc(ld_x, 16)
            sp.dma_start(xs[0:LASTN, NC - 1, :], x[(NC - 1) * P:N, :]).then_inc(ld_x, 16)
            for a, b in ((w1_sb[:, :], w1), (w2_cat[:, 0:D], w2s), (w2_cat[:, D:2 * D], w2n),
                         (mw1_r[:, :], mw1[D:2 * D, :]), (b1_bc[:, :], b1.partition_broadcast(P))):
                sp.dma_start(a, b).then_inc(ld_w, 16)
            sp.wait_ge(ev("drel_t_ready"), 1)
            flat_t = drel_t.rearrange("p (c e) -> p c e", e=P)
            sp.dma_start(drel_flat[0:3 * P * P].rearrange("(c p e) -> p c e", p=P, e=P), flat_t[:, 0:3, :]).then_inc(drel_stored, 16)
            sp.dma_start(drel_flat[3 * P * P:T * P].rearrange("(p e) -> p e", e=P), flat_t[0:T - 3 * P, 3, :]).then_inc(drel_stored, 16)
            sp.wait_ge(fills, 9)
            sp.dma_start(pr_table[NPAD:NPAD + W, :], ident[:, :]).then_inc(ev("pr_stored"), 16)

            sp.wait_ge(table_ready, 1)
            sp.dma_start(table.rearrange("(c p) d -> p c d", p=P), cur[:, :, :]).then_inc(table_stored, 16)

            sp.wait_ge(ev("adjacency_over"), 1)
            for a, b in ((mw1_se[0:D, :], mw1[0:D, :]), (mw1_se[D:2 * D, :], mw1[2 * D:3 * D, :]),
                         (mb1_sb, mb1.rearrange("(p a) -> p a", a=1)), (mw2_sb, mw2),
                         (nw1_h, nw1[0:D, :]), (nw1_a, nw1[D:2 * D, :]),
                         (nb1_sb, nb1.rearrange("(p a) -> p a", a=1)), (nw2_sb, nw2),
                         (nb2_bc, nb2.partition_broadcast(P)),
                         (scale_bc, ln_scale.partition_broadcast(P)), (offset_bc, ln_offset.partition_broadcast(P)),
                         (mb2_row[:, 0:D], mb2.rearrange("(a d) -> a d", a=1)), (mb2_row[:, D:2 * D], mb2.rearrange("(a d) -> a d", a=1)),
                         (mb2_row[:, 2 * D:3 * D], mb2.rearrange("(a d) -> a d", a=1)), (mb2_row[:, 3 * D:4 * D], mb2.rearrange("(a d) -> a d", a=1))):
                sp.dma_start(a, b).then_inc(ld_l3, 16)
            sp.wait_ge(table_ready, 2)
            sp.dma_start(table.rearrange("(c p) d -> p c d", p=P), hs).then_inc(table_stored, 16)
            sp.wait_ge(ev("pr_ready"), 1)
            sp.dma_start(pr_table[0:NPAD, :].rearrange("(c p) h -> p c h", p=P), pr_sb).then_inc(ev("pr_stored"), 16)
            sp.wait_ge(ev("pr_stored"), 32)
            sp.wait_ge(drel_stored, 32)

            def l3_loads(it, q, base, edges):
                sp.wait_ge(seg_done[q], 1 + IT + it)
                if edges == G * P:
                    sp.dma_start(X[:, q, :, D:2 * D],
                                 edge_attr[bass.ds(base * P, G * P), :].rearrange("(j e) d -> e j d", e=P)).then_inc(edges_loaded[q], 16)
                else:
                    whole = edges // P
                    sp.dma_start(X[:, q, 0:whole, D:2 * D],
                                 edge_attr[base * P:(base + whole) * P, :].rearrange("(j e) d -> e j d", e=P)).then_inc(tail_loaded, 16)
                    sp.wait_ge(tail_loaded, 16)
                    sp.dma_start(X[0:edges - whole * P, q, whole, D:2 * D],
                                 edge_attr[(base + whole) * P:E, :]).then_inc(edges_loaded[q], 16)
                sp.dma_start(drel_bc[:, q, :], drel_flat[bass.ds(base * P, G * P)].partition_broadcast(P)).then_inc(drel_loaded[q], 16)
                nodes = load_nodes(sp, base_row, base, G, N - 1)
                for j in range(G):
                    sp.dma_start(prw[:, q, j, :], pr_table[bass.ds(nodes[j], W), :]).then_inc(prw_loaded[q], 16)

            with sp.Fori(0, IT - 1) as it:
                for q in range(Q):
                    l3_loads(it, q, it * (Q * G) + q * G, G * P)
            for q in range(Q):
                l3_loads(IT - 1, q, (IT - 1) * Q * G + q * G, G * P if q < Q - 1 else LAST_EDGES)
            sp.wait_ge(ev("out_ready"), 1)
            sp.dma_start(out[0:(NC - 1) * P, :].rearrange("(c p) d -> p c d", p=P), xs[:, 0:NC - 1, :]).then_inc(ev("out_stored"), 16)
            sp.dma_start(out[(NC - 1) * P:N, :], xs[0:LASTN, NC - 1, :]).then_inc(ev("out_stored"), 16)
            sp.wait_ge(ev("out_stored"), 32)

        def on_gpsimd(pool):
            pool.memset(raw_dst[:, 3 * P:4 * P], NOWHERE).then_inc(pads, 1)
            pool.memset(raw_src[:, 3 * P:4 * P], 0).then_inc(pads, 1)
            pool.memset(raw_w[:, 3 * P:4 * P], 0.0).then_inc(pads, 1)
            pool.memset(xs[:, NC - 1, :], 0.0).then_inc(pads, 1)
            pool.memset(ident[:, :], 0.0).then_inc(pool_chain, 1)
            pool.wait_ge(pool_chain, 1)
            pool.affine_select(out=ident[:, :], in_=ident[:, :], compare_op=ALU.not_equal, fill=1.0,
                               base=0, pattern=[[-1, P]], channel_multiplier=1).then_inc(fills, 1)
            for tile, pattern, per_partition in (
                    (iota_row[:, :], [[1, P]], 0), (iota_p[:, :], [[1, 1]], 1), (iota_4[:, :, :], [[1, P], [0, 4]], 0),
                    (iota_r[:, :], [[1, NC * B]], 0), (block_key[:, :], [[P, NC * BC]], 0), (chunk_start[:, :], [[P, NC]], 0),
                    (starts, [[B, THR]], 0)):
                pool.iota(tile, pattern, base=0, channel_multiplier=per_partition,
                          allow_small_or_imprecise_dtypes=True).then_inc(fills, 1)
            pool.memset(ones[:, :], 1.0)
            pool.memset(neg_half[:, :], -0.5)
            pool.memset(ones_row[:, :], 1.0).then_inc(fills, 1)

            def powers(k):
                pool.wait_ge(rstd_in, k)
                pool.tensor_tensor(st_b[:, :], st_a[:, :], neg_half[:, :], ALU.pow).then_inc(rstd_out, 1)

            def gathers(g, rows):
                pool.wait_ge(table_stored, 16 * (g + 1))
                with pool.Fori(0, IT) as it:
                    for q in range(Q):
                        pool.wait_ge(idx_ready[q], g * IT + it + 1)
                        pool.wait_ge(seg_done[q], 1 + g * IT + it)
                        pool.sem_inc(waits_carried, 1)
                        for j in range(G):
                            pool.indirect_dma_start(
                                out=rows[:, q, j, 0:D], out_offset=None, in_=table,
                                in_offset=bass.IndirectOffsetOnAxis(ap=idx[:, q, j:j + 1], axis=0)).then_inc(gathered[q], 16)

            pool.wait_ge(fills, 9)
            powers(1)
            powers(2)
            powers(3)
            powers(4)
            gathers(0, rows1)
            powers(5)
            powers(6)
            gathers(1, X)
            powers(7)

        def copy_idx(act, g, it, q):
            act.wait_ge(seg_done[q], 1 + g * IT + it)
            nc.scalar.copy(idx[:, q, :], src_i[:, bass.ds(it * (Q * G) + q * G, G)]).then_inc(idx_ready[q], 1)

        def on_scalar(act):
            for free in x_t_ready + hid_ready + msg_ready + block_kept:
                act.sem_inc(free, 1)
            act.wait_ge(ev("keys_ready"), 1)
            act.wait_ge(ev("ranges_ready"), 1)
            act.wait_ge(drel_stored, 32)

            def keep_blocks(c, blocks):
                for j in range(blocks):
                    b = j % 2
                    act.wait_ge(block_built[b], c * (BC // 2) + j // 2 + 2)
                    nc.scalar.copy(A[:, :, bass.ds(c * P + j * B, B)],
                                   big[:, b, 0:NC * B].rearrange("p (s d) -> p s d", d=B)).then_inc(block_kept[b], 1)

            with act.Fori(0, NC - 1) as c:
                keep_blocks(c, BC)
            keep_blocks(NC - 1, LASTB)

            def copy_sums(n):
                for k in range(ROUNDS):
                    cols = min(4 * P, WIDE - 4 * k * P)
                    act.wait_ge(ev("sums_ps"), n * ROUNDS + k + 1)
                    if n * ROUNDS + k >= 2:
                        act.wait_ge(ev("sums_nodes"), n * ROUNDS + k - 1)
                    nc.scalar.copy(sums_t[:, k % 2, 0:cols], seg[:, 2 + k % 2, 0:cols]).then_inc(ev("sums_t"), 1)

            for n in range(3):
                copy_sums(n)

            for c in range(NC):
                act.wait_ge(ev("turn1_ps"), c + 1)
                nc.scalar.copy(turn1, seg[0:D, 0, 0:P]).then_inc(ev("turn1_ready"), 1)
            with act.Fori(0, IT) as it:
                for q in range(Q):
                    copy_idx(act, 0, it, q)

            copy_sums(3)
            for k in range(ROUNDS):
                n = min(4, NC - 4 * k) * P
                act.wait_ge(ev("turn2_ps"), k + 1)
                if k >= 2:
                    act.wait_ge(ev("turn2_used"), k - 1)
                nc.scalar.copy(turn2_ring[:, k % 2, 0:n], seg[:, k % 2, 0:n]).then_inc(ev("turn2_ready"), 1)

            for k in range(ROUNDS):
                n = min(4, NC - 4 * k) * P
                act.wait_ge(ev("h_ps"), k + 1)
                nc.scalar.copy(h_t[:, 4 * k * P:4 * k * P + n], seg[0:D, k % 4, 0:n]).then_inc(ev("h_t"), 1)
            for k in range(ROUNDS):
                chunks = min(4, NC - 4 * k)
                act.wait_ge(ev("pr_ps"), k + 1)
                nc.scalar.copy(pr_sb[:, 4 * k:4 * k + chunks, :],
                               big[:, k % 4, 0:chunks * HID].rearrange("p (c h) -> p c h", h=HID)).then_inc(ev("pr_copied"), 1)
            act.wait_ge(ev("pr_copied"), ROUNDS)
            act.sem_inc(ev("pr_ready"), 1)
            act.wait_ge(ld_l3, 15 * 16)
            with act.Fori(0, IT) as it:
                for q in range(Q):
                    copy_idx(act, 1, it, q)
                for s in range(Q + 2):
                    if s < Q:
                        r, k = s % 2, it * 2 + s // 2
                        act.wait_ge(transposed[r], k + 1)
                        act.wait_ge(hid_done[r], 1 + k)
                        nc.scalar.copy(x_t[:, r, :], big[:, r, :]).then_inc(x_t_ready[r], 1)
                    if 1 <= s <= Q:
                        r, k = (s - 1) % 2, it * 2 + (s - 1) // 2
                        act.wait_ge(hid_done[r], k + 2)
                        act.wait_ge(msg_done[r], 1 + k)
                        nc.scalar.activation(hid_t[:, r, :], big[:, 2 + r, :], ACT.Relu, bias=mb1_sb).then_inc(hid_ready[r], 1)
                    if s >= 2:
                        q = s - 2
                        r, k = q % 2, it * 2 + q // 2
                        act.wait_ge(msg_done[r], k + 2)
                        if q >= 2:
                            act.wait_ge(seg_done[q - 2], 2 + IT + it)
                        else:
                            act.wait_ge(seg_done[q + 2], 1 + IT + it)
                        nc.scalar.activation(msg[:, r, :, :], seg[:, 2 + r, 0:G * D].rearrange("p (j d) -> p j d", d=D),
                                             ACT.Relu).then_inc(msg_ready[r], 1)
            for k in range(ROUNDS):
                n = min(4, NC - 4 * k) * P
                act.wait_ge(ev("y1_ps"), k + 1)
                if k >= 2:
                    act.wait_ge(ev("y1_used"), k - 1)
                nc.scalar.activation(y1_t[:, k % 2, 0:n], seg[:, k % 4, 0:n], ACT.Relu, bias=nb1_sb).then_inc(ev("y1_ready"), 1)

        def on_tensor(pe):
            for free in seg_done + hid_done + msg_done + hot_d_used + block_built:
                pe.sem_inc(free, 1)

            pe.wait_ge(fills, 9)
            for b, (t, name) in enumerate(((dst_t, "dst_t"), (key_r_t, "key_r_t"), (key_l_t, "key_l_t"),
                                           (drel_t, "drel_t"), (src_t, "src_t"), (raw_w, None))):
                if name:
                    pe.wait_ge(ev(name + "_ready"), 1)
                for c in range(4):
                    op = nc.tensor.transpose(banks[b][:, c * P:(c + 1) * P], t[:, c * P:(c + 1) * P], ident[:, :])
                op.then_inc(ev("cols_ps"), 1)
            pe.wait_ge(ev("below_ready"), 1)
            for c in range(4):
                op = nc.tensor.matmul(banks[6][0:1, 0:THR], ones[:, :], below[:, c * THR:(c + 1) * THR], start=(c == 0), stop=(c == 3))
            op.then_inc(ev("counts_ps"), 1)
            pe.wait_ge(ld_w, 16 * 5)
            nc.tensor.transpose(banks[7][:, 0:D], w2_cat[:, :], ident[0:D, 0:D]).then_inc(ev("w2_ps"), 1)
            pe.wait_ge(ev("keys_ready"), 1)
            pe.wait_ge(ev("ranges_ready"), 1)

            def blocks_and_degrees(c, blocks):
                first = load_nodes(pe, first_row, c * BC, 1, T)[0]
                degree_groups = 0
                for j in range(blocks):
                    b = j % 2
                    use = c * (BC // 2) + j // 2
                    pe.wait_ge(hots_ready[b], use + 1)
                    pe.wait_ge(block_kept[b], use + 1)
                    for k in range(KB):
                        op = nc.tensor.matmul(big[:, b, 0:NC * B], hot_l[:, b, :, k], hot_r[:, b, k, :], start=(k == 0), stop=(k == KB - 1))
                    op.then_inc(block_built[b], 1)
                    while degree_groups < (j + 1) * KG // blocks:
                        g = degree_groups
                        pe.wait_ge(hot_d_ready[g], c + 1)
                        for k in range(4):
                            t = 4 * g + k
                            op = nc.tensor.matmul(seg[:, 0, bass.ds(c * 4, 4)], hot_d[:, g, :, k], w_parts[:, bass.ds(first + t, 1), :],
                                                  start=(t == 0), stop=(t == KC - 1))
                        op.then_inc(hot_d_used[g], 1)
                        degree_groups += 1

            with pe.Fori(0, NC - 1) as c:
                blocks_and_degrees(c, BC)
            blocks_and_degrees(NC - 1, LASTB)
            for b in range(2):
                pe.wait_ge(block_kept[b], 1 + NB // 2)
            pe.sem_inc(ev("degrees_ps"), 1)

            def dense_sums(n):
                parts = x_parts[n % 2 if n < 3 else 0]
                pe.wait_ge(ev("parts_ready"), [1, 1 + ROUNDS, 1 + 2 * ROUNDS, 2 + 2 * ROUNDS][n])

                def turn_round(k):
                    pe.wait_ge(ev("sums_t"), n * ROUNDS + k + 1)
                    if n * ROUNDS + k >= 4:
                        pe.wait_ge(ev("sums_read"), n * ROUNDS + k - 3)
                    for c in range(4 * k, min(4 * k + 4, NC)):
                        wide = min(P, WIDE - c * P)
                        op = nc.tensor.matmul(round_nodes(n, k)[0:wide, c % 4, :], sums_t[:, k % 2, (c % 4) * P:(c % 4) * P + wide], join[:, :],
                                              start=True, stop=True)
                    op.then_inc(ev("sums_nodes"), 1)

                for k in range(ROUNDS):
                    cols = min(4 * P, WIDE - 4 * k * P)
                    if n * ROUNDS + k >= 2:
                        pe.wait_ge(ev("sums_t"), n * ROUNDS + k - 1)
                    for s in range(NC):
                        op = nc.tensor.matmul(seg[:, 2 + k % 2, 0:cols], parts[:, s, :, :], A[:, s, 4 * k * P:4 * k * P + cols],
                                              start=(s == 0), stop=(s == NC - 1))
                    op.then_inc(ev("sums_ps"), 1)
                    if k:
                        turn_round(k - 1)
                turn_round(ROUNDS - 1)

            for n in range(3):
                dense_sums(n)

            pe.wait_ge(ev("conv1_in"), 1)
            for c in range(NC):
                nc.tensor.transpose(seg[0:D, 0, 0:P], cur[:, c, :], ident[:, :]).then_inc(ev("turn1_ps"), 1)
                pe.wait_ge(ev("turn1_ready"), c + 1)
                nc.tensor.matmul(big_nodes[:, c, :], turn1, w1_sb[:, :], start=(c % 8 == 0), stop=True,
                                 skip_group_check=True).then_inc(ev("turn1_used"), 1)
                pe.wait_ge(ev("turn1_used"), c + 1)
            with pe.Fori(0, IT) as it:
                for q in range(Q):
                    pe.wait_ge(gathered[q], (it + 1) * (16 * G))
                    pe.wait_ge(onehot_ready[q], it + 1)
                    pe.wait_ge(acc_step, it * (Q * G) + (q + 1) * G)
                    for j in range(G):
                        op = nc.tensor.matmul(seg[0:D, q, j * W:(j + 1) * W], rows1[:, q, j, :], onehot1[:, q, j, :],
                                              start=True, stop=True)
                    op.then_inc(seg_done[q], 1)
            pe.wait_ge(acc_step, Q * G + T)
            for c in range(NC):
                op = nc.tensor.matmul(big_nodes[:, c, :], acc_t[:, c * P:(c + 1) * P], w1_sb[:, :], start=False, stop=True,
                                      skip_group_check=True)
            op.then_inc(ev("conv1_out"), 1)

            dense_sums(3)
            pe.sem_inc(ev("adjacency_over_pe"), 1)
            pe.wait_ge(ev("nb_ready"), 1)
            for k in range(ROUNDS + 1):
                if k < ROUNDS:
                    if k >= 2:
                        pe.wait_ge(ev("turn2_ready"), k - 1)
                    for c in range(4 * k, min(4 * k + 4, NC)):
                        op = nc.tensor.transpose(seg[:, k % 2, (c % 4) * P:(c % 4 + 1) * P], h_nb[:, c, :], ident[:, :])
                    op.then_inc(ev("turn2_ps"), 1)
                if k >= 1:
                    pe.wait_ge(ev("turn2_ready"), k)
                    for c in range(4 * k - 4, min(4 * k, NC)):
                        op = nc.tensor.matmul(big_nodes[:, c, :], turn2_ring[:, (k - 1) % 2, (c % 4) * P:(c % 4 + 1) * P], w2_t[:, :],
                                              start=True, stop=True)
                    op.then_inc(ev("turn2_used"), 1)

            pe.wait_ge(ev("h_L3"), 1)
            for k in range(ROUNDS):
                if k >= 4:
                    pe.wait_ge(ev("h_t"), k - 3)
                for c in range(4 * k, min(4 * k + 4, NC)):
                    op = nc.tensor.transpose(seg[0:D, k % 4, (c % 4) * P:(c % 4 + 1) * P], hs[:, c, :], ident[:, :])
                op.then_inc(ev("h_ps"), 1)
            for k in range(ROUNDS):
                pe.wait_ge(ev("h_t"), k + 1)
                if k >= 4:
                    pe.wait_ge(ev("pr_copied"), k - 3)
                for c in range(4 * k, min(4 * k + 4, NC)):
                    op = nc.tensor.matmul(big[:, k % 4, (c % 4) * HID:(c % 4 + 1) * HID], h_t[:, c * P:(c + 1) * P], mw1_r[:, :], start=True, stop=True)
                op.then_inc(ev("pr_ps"), 1)
            pe.wait_ge(ev("pr_copied"), ROUNDS)
            pe.wait_ge(ld_l3, 15 * 16)
            pe.wait_ge(ev("mb2_ready"), 1)
            with pe.Fori(0, IT) as it:
                for s in range(Q + 3):
                    if s < Q:
                        r, k = s % 2, it * 2 + s // 2
                        pe.wait_ge(gathered[s], (it + (IT + 1)) * (16 * G))
                        pe.wait_ge(edges_loaded[s], (it + 1) * 16)
                        pe.wait_ge(x_t_ready[r], 1 + k)
                        for j in range(G):
                            op = nc.tensor.transpose(big[:, r, j * P:(j + 1) * P], X[:, s, j, :], ident[:, :])
                        op.then_inc(transposed[r], 1)
                    if 1 <= s <= Q:
                        q = s - 1
                        r, k = q % 2, it * 2 + q // 2
                        pe.wait_ge(x_t_ready[r], k + 2)
                        pe.wait_ge(hid_ready[r], 1 + k)
                        pe.wait_ge(onehot_t_ready[q], it + 1)
                        pe.wait_ge(prw_loaded[q], (it + 1) * (16 * G))
                        nc.tensor.matmul(big[:, 2 + r, :], mw1_se, x_t[:, r, :], start=True, stop=True)
                        for j in range(G):
                            op = nc.tensor.matmul(big[:, 2 + r, j * P:(j + 1) * P], prw[:, q, j, :],
                                                  onehot_t[:, q, j * P:(j + 1) * P], start=False, stop=True,
                                                  skip_group_check=True)
                        op.then_inc(hid_done[r], 1)
                    if 2 <= s <= Q + 1:
                        q = s - 2
                        r, k = q % 2, it * 2 + q // 2
                        pe.wait_ge(hid_ready[r], k + 2)
                        pe.wait_ge(msg_ready[r], 1 + k)
                        for part in range(3):
                            nc.tensor.matmul(seg[:, 2 + r, 0:G * D], ones_row[:, :], mb2_parts[:, part, :], start=(part == 0), stop=(part == 2))
                        for j in range(G):
                            op = nc.tensor.matmul(seg[:, 2 + r, j * D:(j + 1) * D], hid_t[:, r, j * P:(j + 1) * P],
                                                  mw2_sb, start=False, stop=True, skip_group_check=True)
                        op.then_inc(msg_done[r], 1)
                    if s >= 3:
                        q = s - 3
                        r, k = q % 2, it * 2 + q // 2
                        pe.wait_ge(msg_ready[r], k + 2)
                        pe.wait_ge(onehot_ready[q], IT + it + 1)
                        pe.wait_ge(acc_step, Q * G - G + T + it * (Q * G) + q * G)
                        for j in range(G):
                            op = nc.tensor.matmul(seg[0:D, r, j * W:(j + 1) * W], msg[:, r, j, :], onehot3[:, q, j, :],
                                                  start=True, stop=True)
                        op.then_inc(seg_done[q], 1)
            pe.wait_ge(acc_step, Q * G + 2 * T)
            for k in range(ROUNDS + 1):
                if k < ROUNDS:
                    n = min(4, NC - 4 * k) * P
                    cols = slice(4 * k * P, 4 * k * P + n)
                    if k >= 4:
                        pe.wait_ge(ev("y1_ready"), k - 3)
                    nc.tensor.matmul(seg[:, k % 4, 0:n], nw1_h, h_t[:, cols], start=True, stop=False)
                    nc.tensor.matmul(seg[:, k % 4, 0:n], nw1_a, acc_t[:, cols], start=False, stop=True).then_inc(ev("y1_ps"), 1)
                if k >= 1:
                    pe.wait_ge(ev("y1_ready"), k)
                    for c in range(4 * k - 4, min(4 * k, NC)):
                        op = nc.tensor.matmul(big_nodes[:, c, :], y1_t[:, (k - 1) % 2, (c % 4) * P:(c % 4 + 1) * P], nw2_sb,
                                              start=True, stop=True)
                    op.then_inc(ev("y1_used"), 1)

        def on_vector(dve):
            dve.sem_inc(acc_step, Q * G)
            links = [0]
            pows = [0]

            def link(op):
                links[0] += 1
                op.then_inc(dve_chain, 1)
                dve.wait_ge(dve_chain, links[0])

            def per_node(v):
                return v[:, :].rearrange("p (c a) -> p c a", a=1).broadcast_to([P, NC, D])

            def per_feature(v):
                return v.rearrange("p (a d) -> p a d", a=1).broadcast_to([P, NC, D])

            def invsqrt():
                pows[0] += 1
                dve.wait_ge(rstd_out, pows[0])

            def normalize(dst_, src_, tmp=ln_tmp):
                link(dve.tensor_reduce(st_a[:, :], src_, AX.X, ALU.add))
                link(dve.tensor_scalar(st_c[:, :], st_a[:, :], 1.0 / D, None, ALU.mult))
                link(dve.tensor_tensor(dst_, src_, per_node(st_c), ALU.subtract))
                link(dve.tensor_tensor(tmp, dst_, dst_, ALU.mult))
                link(dve.tensor_reduce(st_c[:, :], tmp, AX.X, ALU.add))
                dve.tensor_scalar(st_a[:, :], st_c[:, :], 1.0 / D, EPS, ALU.mult, ALU.add).then_inc(rstd_in, 1)
                invsqrt()
                link(dve.tensor_tensor(dst_, dst_, per_node(st_b), ALU.mult))

            def pre_ln(h):
                normalize(h, xs[:, :, :])
                link(dve.tensor_scalar(h, h, 0.0, None, ALU.max))

            def split3(value, parts, rest):
                link(dve.tensor_copy(parts(0), value))
                link(dve.tensor_tensor(rest, value, parts(0), ALU.subtract))
                link(dve.tensor_copy(parts(1), rest))
                link(dve.tensor_tensor(rest, rest, parts(1), ALU.subtract))
                link(dve.tensor_copy(parts(2), rest))

            def edge_pass(n, onehot, weighted=False, l3=False):
                with dve.Fori(0, IT) as it:
                    for q in range(Q):
                        base = it * (Q * G) + q * G
                        dve.wait_ge(seg_done[q], 1 + n * IT + it)
                        for j in range(G):
                            t = base + j
                            if weighted:
                                op = dve.tensor_scalar(onehot[:, q, j, :], iota_row[:, :], drel[:, bass.ds(t, 1)], wcol[:, bass.ds(t, 1)],
                                                       ALU.is_equal, ALU.mult)
                            else:
                                op = dve.tensor_scalar(onehot[:, q, j, :], iota_row[:, :], drel[:, bass.ds(t, 1)], None, ALU.is_equal)
                        op.then_inc(onehot_ready[q], 1)
                        if l3:
                            dve.wait_ge(drel_loaded[q], (it + 1) * 16)
                            dve.tensor_scalar(onehot_t[:, q, :], drel_bc[:, q, :], iota_p[:, 0:1], None, ALU.is_equal).then_inc(onehot_t_ready[q], 1)
                    for q in range(Q):
                        base = it * (Q * G) + q * G
                        bank = q % 2 if l3 else q
                        nodes = load_nodes(dve, base_row, base, G, N - 1)
                        dve.wait_ge(seg_done[q], 2 + n * IT + it)
                        for j in range(G):
                            dve.wait_ge(acc_step, Q * G + n * T + base + j)
                            window = acc_t[:, bass.ds(nodes[j], W)]
                            dve.tensor_tensor(window, window, seg[0:D, bank, j * W:(j + 1) * W], ALU.add).then_inc(acc_step, 1)

            dve.wait_ge(ld_edges, 9 * 16)
            dve.wait_ge(fills, 9)
            link(dve.tensor_copy(join[0:D, :], ident[0:D, 0:D]))
            link(dve.tensor_scalar(join[D:2 * D, :], ident[D:2 * D, D:2 * D], 1.0 / LOW, None, ALU.mult))
            dve.tensor_scalar(dst_hi, raw_dst, 4, 7, ALU.logical_shift_right, ALU.logical_shift_left)
            dve.tensor_scalar(dst_lo, raw_dst, B - 1, None, ALU.bitwise_and)
            dve.tensor_scalar(src_hi, raw_src, 7, 4, ALU.logical_shift_right, ALU.logical_shift_left)
            link(dve.tensor_scalar(src_lo, raw_src, P - 1, None, ALU.bitwise_and))
            link(dve.tensor_copy(dst_t, raw_dst))
            dve.sem_inc(ev("dst_t_ready"), 1)
            dve.tensor_tensor(key_r_t, src_hi, dst_lo, ALU.add).then_inc(ev("key_r_t_ready"), 1)
            dve.tensor_tensor(key_l_t, src_lo, dst_hi, ALU.add).then_inc(ev("key_l_t_ready"), 1)
            dve.tensor_tensor(drel_t.rearrange("p (c e) -> p c e", e=P), raw_dst.rearrange("p (c e) -> p c e", e=P),
                              raw_dst.rearrange("p (c e) -> p c e", e=P)[:, :, 0:1].broadcast_to([P, 4, P]), ALU.subtract).then_inc(ev("drel_t_ready"), 1)
            dve.tensor_copy(src_t, raw_src).then_inc(ev("src_t_ready"), 1)
            for c in range(4):
                op = dve.tensor_scalar(below[:, c * THR:(c + 1) * THR], starts, dst_t[:, c * P:c * P + 1], None, ALU.is_gt)
            op.then_inc(ev("below_ready"), 1)
            dve.wait_ge(ev("cols_ps"), 6)
            for b, t in enumerate((dst_c, key_r, key_l, drel[:, :], src_i[:, :], wcol[:, :])):
                link(dve.tensor_copy(t, banks[b]))
            link(dve.memset(w_parts, 1.0))
            split3(wcol[:, :], lambda k: w_parts[:, :, 1 + k], w_res)
            dve.wait_ge(ev("w2_ps"), 1)
            link(dve.tensor_copy(w2_t[:, :], banks[7][:, 0:D]))
            dve.sem_inc(ev("keys_ready"), 1)
            dve.wait_ge(ev("counts_ps"), 1)
            link(dve.tensor_scalar(first_row[:, :], banks[6][0:1, 0:THR], 1.0, 0.0, ALU.subtract, ALU.max))
            dve.sem_inc(ev("ranges_ready"), 1)
            dve.wait_ge(ld_x, 32)
            normalize(total, xs[:, :, :], tmp=scratch)
            link(dve.tensor_scalar(total, total, 0.0, None, ALU.max))

            def block_hots(c, blocks):
                firsts = load_nodes(dve, first_row, c * BC, blocks, T)

                def equal_four(out_, four):
                    return dve.tensor_tensor(out_, four.rearrange("p (a k) -> p a k", a=1).broadcast_to([P, P, 4]), iota_4[:, :, :], ALU.is_equal)

                dve.wait_ge(hot_d_used[KG - 1], 1 + c)
                dve.tensor_scalar(chunk_rel[:, :], dst_c[:, bass.ds(firsts[0], KC)], chunk_start[:, bass.ds(c, 1)], None,
                                  ALU.subtract).then_inc(chunk_rel_ready, 1)
                groups = 0
                for j in range(blocks):
                    b = j % 2
                    dve.wait_ge(block_built[b], c * (BC // 2) + j // 2 + 1)
                    dve.tensor_scalar(block_rel[:, b, :], key_l[:, bass.ds(firsts[j], KB)], block_key[:, bass.ds(c * BC + j, 1)], None,
                                      ALU.subtract).then_inc(block_rel_ready, 1)
                    for k in range(KB):
                        dve.tensor_scalar(hot_r[:, b, k, :], iota_r[:, :], key_r[:, bass.ds(firsts[j] + k, 1)], None, ALU.is_equal)
                    dve.wait_ge(block_rel_ready, c * BC + j + 1)
                    equal_four(hot_l[:, b, :, :], block_rel[:, b, :]).then_inc(hots_ready[b], 1)
                    while groups < (j + 1) * KG // blocks:
                        dve.wait_ge(chunk_rel_ready, c + 1)
                        dve.wait_ge(hot_d_used[groups], 1 + c)
                        equal_four(hot_d[:, groups, :, :], chunk_rel[:, 4 * groups:4 * groups + 4]).then_inc(hot_d_ready[groups], 1)
                        groups += 1

            with dve.Fori(0, NC - 1) as c:
                block_hots(c, BC)
            block_hots(NC - 1, LASTB)

            dve.wait_ge(ev("degrees_ps"), 1)
            for g in range(KG):
                dve.wait_ge(hot_d_used[g], 1 + NC)
            link(dve.tensor_copy(deg[:, :, :], seg[:, 0, 0:4 * NC].rearrange("p (c a) -> p c a", a=4)))
            link(dve.tensor_scalar(rdeg[:, :], deg[:, :, 0], 1.0, None, ALU.max))
            dve.tensor_copy(st_a[:, :], rdeg[:, :]).then_inc(rstd_in, 1)
            link(dve.tensor_scalar(st_c[:, :], deg[:, :, 0], 0.0, None, ALU.is_gt))
            invsqrt()
            link(dve.tensor_tensor(dinv0[:, :], st_b[:, :], st_c[:, :], ALU.mult))
            link(dve.tensor_tensor(dinv0sq[:, :], dinv0[:, :], dinv0[:, :], ALU.mult))
            link(dve.reciprocal(rdeg[:, :], rdeg[:, :]))
            link(dve.tensor_reduce(st_c[:, :], deg[:, :, 1:4], AX.X, ALU.add))
            link(dve.tensor_scalar(deg[:, :, 1], st_c[:, :], 1.0, None, ALU.add))
            link(dve.tensor_scalar(dinv1[:, :], deg[:, :, 1], 0.0, None, ALU.is_gt))
            link(dve.tensor_tensor(st_c[:, :], deg[:, :, 1], dinv1[:, :], ALU.mult))
            link(dve.tensor_tensor(st_c[:, :], st_c[:, :], dinv1[:, :], ALU.subtract))
            dve.tensor_scalar(st_a[:, :], st_c[:, :], 1.0, None, ALU.add).then_inc(rstd_in, 1)
            invsqrt()
            link(dve.tensor_tensor(dinv1[:, :], dinv1[:, :], st_b[:, :], ALU.mult))

            def split_features(buf, value, rest, cols=slice(0, NC)):
                parts = x_parts[buf]
                link(dve.tensor_copy(parts[:, cols, 0, :], value))
                link(dve.tensor_tensor(rest, value, parts[:, cols, 0, :], ALU.subtract))
                link(dve.tensor_scalar(parts[:, cols, 1, :], rest, LOW, None, ALU.mult))

            link(dve.tensor_tensor(cur[:, :, :], total, per_node(dinv0), ALU.mult))
            split_features(0, cur[:, :, :], hop)
            dve.sem_inc(ev("parts_ready"), 1)
            for n in range(3):
                for k in range(ROUNDS):
                    cols = slice(4 * k, min(4 * k + 4, NC))
                    rows = slice(0, LASTB * B if k == ROUNDS - 1 else P)
                    wide = cols.stop - cols.start
                    sums = round_nodes(n, k)[rows, 0:wide, :]
                    dve.wait_ge(ev("sums_nodes"), n * ROUNDS + k + 1)
                    link(dve.tensor_tensor(cur[rows, cols, :], sums, per_node(dinv0)[rows, cols, :], ALU.mult))
                    link(dve.tensor_tensor(total[rows, cols, :], total[rows, cols, :], cur[rows, cols, :], ALU.add))
                    if n < 2:
                        parts = x_parts[(n + 1) % 2]
                        link(dve.tensor_tensor(cur[rows, cols, :], sums, per_node(dinv0sq)[rows, cols, :], ALU.mult))
                        dve.sem_inc(ev("sums_read"), 1)
                        link(dve.tensor_copy(parts[rows, cols, 0, :], cur[rows, cols, :]))
                        link(dve.tensor_tensor(cur[rows, cols, :], cur[rows, cols, :], parts[rows, cols, 0, :], ALU.subtract))
                        link(dve.tensor_scalar(parts[rows, cols, 1, :], cur[rows, cols, :], LOW, None, ALU.mult))
                        dve.sem_inc(ev("parts_ready"), 1)
                    else:
                        dve.sem_inc(ev("sums_read"), 1)
            link(dve.tensor_scalar(total, total, 0.25, None, ALU.mult))
            link(dve.tensor_tensor(xs[:, :, :], xs[:, :, :], total, ALU.add))

            pre_ln(cur[:, :, :])
            link(dve.tensor_tensor(cur[:, :, :], cur[:, :, :], per_node(dinv1), ALU.mult))
            link(dve.memset(acc_t, 0.0))
            dve.sem_inc(table_ready, 1)
            dve.sem_inc(ev("conv1_in"), 1)
            edge_pass(0, onehot1, weighted=True)
            dve.wait_ge(ev("conv1_out"), 1)
            link(dve.tensor_tensor(hop, big_nodes, per_node(dinv1), ALU.mult))
            link(dve.tensor_tensor(hop, hop, per_feature(b1_bc[:, :]), ALU.add))
            link(dve.scalar_tensor_tensor(xs[:, :, :], hop, 0.0, xs[:, :, :], ALU.max, ALU.add))

            pre_ln(hs)
            dve.wait_ge(table_stored, 16)
            split_features(0, hs, cur[:, :, :])
            dve.sem_inc(ev("parts_ready"), 1)
            link(dve.memset(nb[:, NC - 1, :], 0.0))
            for k in range(ROUNDS):
                cols = slice(4 * k, min(4 * k + 4, NC))
                rows = slice(0, LASTB * B if k == ROUNDS - 1 else P)
                dve.wait_ge(ev("sums_nodes"), 3 * ROUNDS + k + 1)
                link(dve.tensor_tensor(nb[rows, cols, :], round_nodes(3, k)[rows, 0:cols.stop - cols.start, :],
                                       per_node(rdeg)[rows, cols, :], ALU.mult))
                dve.sem_inc(ev("sums_read"), 1)
            dve.sem_inc(ev("nb_ready"), 1)
            dve.wait_ge(ev("turn2_used"), ROUNDS)
            link(dve.tensor_tensor(xs[:, :, :], xs[:, :, :], big_nodes, ALU.add))

            dve.sem_inc(ev("adjacency_over"), 1)
            pre_ln(hs)
            link(dve.memset(acc_t, 0.0))
            link(dve.memset(X, 0.0))
            dve.sem_inc(table_ready, 1)
            dve.sem_inc(ev("h_L3"), 1)
            dve.wait_ge(ld_l3, 15 * 16)
            split3(mb2_row, lambda k: mb2_parts[:, k, :], mb2_rest)
            dve.sem_inc(ev("mb2_ready"), 1)
            edge_pass(1, onehot3, l3=True)
            dve.wait_ge(ev("y1_used"), ROUNDS)
            dve.wait_ge(ld_l3, 15 * 16)
            link(dve.tensor_tensor(nb, big_nodes, per_feature(nb2_bc), ALU.add))
            normalize(cur[:, :, :], nb, tmp=scratch)
            link(dve.tensor_tensor(cur[:, :, :], cur[:, :, :], per_feature(scale_bc), ALU.mult))
            link(dve.tensor_tensor(cur[:, :, :], cur[:, :, :], per_feature(offset_bc), ALU.add))
            link(dve.tensor_tensor(hs, hs, cur[:, :, :], ALU.add))
            dve.tensor_tensor(xs[:, :, :], xs[:, :, :], hs, ALU.add).then_inc(ev("out_ready"), 1)

        return {'sync': on_sync, 'gpsimd': on_gpsimd, 'scalar': on_scalar, 'tensor': on_tensor, 'vector': on_vector}


def build(nc, *args):
    dst = args[2]
    with ExitStack() as ctx:
        sems = {}

        def sem(name):
            if name not in sems:
                sems[name] = ctx.enter_context(nc.semaphore(name))
            return sems[name]

        base_row = ctx.enter_context(nc.sbuf_tensor("base_row", [1, T], I32))
        crowded = ctx.enter_context(nc.sbuf_tensor("crowded", [1, 1], I32))
        base_loaded, base_steps, crowded_ready = sem("base_loaded"), sem("base_steps"), sem("crowded_ready")
        with nc.sbuf_tensor("tile_block", [1, 2, T], I32) as tile_block, nc.sbuf_tensor("same", [1, 2, T], F32) as same:
            pass
        general = general_path(nc, sem, base_row[:, :], *args)
        dense = dense_path(nc, sem, base_row[:, :], *args)
        block = ctx.enter_context(nc.Block())

        def is_crowded(eng):
            eng.wait_ge(crowded_ready, 1)
            _, v = nc.values_load_multi_w_load_instructions(
                crowded[0:1, 0:1], engines=[eng.engine], min_val=0, max_val=1,
                skip_runtime_bounds_check_because="a comparison's result")
            return v[0] != 0

        @block.sync
        def _(sp):
            sp.dma_start(base_row[:, 0:FULL], dst[0:FULL * P].rearrange("(a t e) -> a t e", a=1, e=P)[:, :, 0],
                         allow_slow_non_contiguous=True).then_inc(base_loaded, 16)
            sp.dma_start(base_row[:, FULL:T], dst[FULL * P:FULL * P + 1].rearrange("(a t) -> a t", a=1)).then_inc(base_loaded, 16)
            with sp.If(is_crowded(sp)):
                general["sync"](sp)
            with sp.Else():
                dense["sync"](sp)

        @block.gpsimd
        def _(pool):
            with pool.If(is_crowded(pool)):
                general["gpsimd"](pool)
            with pool.Else():
                dense["gpsimd"](pool)

        @block.scalar
        def _(act):
            with act.If(is_crowded(act)):
                general["scalar"](act)
            with act.Else():
                dense["scalar"](act)

        @block.tensor
        def _(pe):
            with pe.If(is_crowded(pe)):
                general["tensor"](pe)
            with pe.Else():
                dense["tensor"](pe)

        @block.vector
        def _(dve):
            dve.wait_ge(base_loaded, 32)
            dve.tensor_scalar(tile_block[:, 0, :], base_row[:, :], 4, None, ALU.logical_shift_right).then_inc(base_steps, 1)
            dve.tensor_scalar(tile_block[:, 1, :], base_row[:, :], 7, None, ALU.logical_shift_right).then_inc(base_steps, 1)
            dve.memset(same[:, :, :], 0.0).then_inc(base_steps, 1)
            dve.wait_ge(base_steps, 3)
            for k, span in ((0, KB - 1), (1, KC - 1)):
                dve.tensor_tensor(same[:, k, 0:T - span], tile_block[:, k, 0:T - span], tile_block[:, k, span:T],
                                  ALU.is_equal).then_inc(base_steps, 1)
            dve.wait_ge(base_steps, 5)
            dve.tensor_reduce(crowded[:, :], same[:, :, :].rearrange("a k t -> a (k t)"), AX.X, ALU.max).then_inc(crowded_ready, 1)
            with dve.If(is_crowded(dve)):
                general["vector"](dve)
            with dve.Else():
                dense["vector"](dve)


_INS = ['x', 'src', 'dst', 'edge_attr_64', 'edge_weight', 'L1_gnn_W', 'L1_gnn_b', 'L2_gnn_W_self', 'L2_gnn_W_neigh',
        'L3_gnn_msg_W1', 'L3_gnn_msg_b1', 'L3_gnn_msg_W2', 'L3_gnn_msg_b2', 'L3_gnn_node_W1', 'L3_gnn_node_b1',
        'L3_gnn_node_W2', 'L3_gnn_node_b2', 'L3_gnn_ln_scale', 'L3_gnn_ln_offset']
_OUTS = [((N, D), 'float32')]


def kernel(**inputs):
    import numpy as _np
    import concourse.bacc as _bacc
    from concourse import mybir as _mybir
    from concourse.bass_utils import run_bass_kernel_spmd as _run

    nc = _bacc.Bacc("TRN2", target_bir_lowering=False, num_devices=1)
    arrays, args = {}, []
    for name in _INS:
        a = _np.ascontiguousarray(inputs[name])
        arrays[f"in_{name}_dram"] = a
        args.append(nc.dram_tensor(f"in_{name}_dram", a.shape, _mybir.dt.from_np(a.dtype), kind="ExternalInput").ap())
    for i, (shape, dtype) in enumerate(_OUTS):
        dt = _mybir.dt.from_np(_np.dtype(dtype))
        args.append(nc.dram_tensor(f"out_{i}_dram", shape, dt, kind="ExternalOutput").ap())
    build(nc, *args)
    r = _run(nc, [arrays], core_ids=[0])
    got = tuple(r.results[0][f"out_{i}_dram"] for i in range(len(_OUTS)))
    return got[0]
```

```python
from contextlib import ExitStack

import concourse.bass as bass
from concourse import mybir

F32 = mybir.dt.float32
F16 = mybir.dt.float16
BF16 = mybir.dt.bfloat16
I32 = mybir.dt.int32
ALU = mybir.AluOpType
ACT = mybir.ActivationFunctionType
AX = mybir.AxisListType

N = 3125
E = 53125
D = 64
HID = 128
P = 128
NC = -(-N // P)
NPAD = NC * P
LASTN = N - (NC - 1) * P
T = -(-E // P)
FULL = E // P
TAIL = E - FULL * P
G = 4
Q = 4
IT = T // (G * Q)
ROUNDS = -(-NC // 4)
LAST_GROUP = T // G - 1
LAST_EDGES = E - LAST_GROUP * G * P
EPS = 1e-5
W = 128
assert T == G * Q * IT

B = 16
NB = -(-N // B)
WIDE = NB * B
KB = 4
BC = P // B
LASTB = NB - (NC - 1) * BC
KP = 6
KC, KG = 20, 5
TK = T + KC
LOW = 2048.0
NOWHERE = 4000
GW = 64
GROUPS = T // G
EARLY = 3 * 4 * P + 4
HALVES = (slice(0, 12), slice(12, NC))
THR = 208

GP = 125
PASS_DEG, PASS_L0, PASS_L1, PASS_L2, PASS_L3 = 0, 1, 4, 5, 6
NPASS = 7


def general_path(nc, sem, base_row, x, src, dst, edge_attr, edge_weight, w1, b1, w2s, w2n, mw1, mb1, mw2, mb2,
                 nw1, nb1, nw2, nb2, ln_scale, ln_offset, out):
    with ExitStack() as ctx:
        def sb(name, shape, dt=F32):
            return ctx.enter_context(nc.sbuf_tensor(name, shape, dt))

        table = nc.dram_tensor("general_table", [N, D], F32, kind="Internal").ap()
        pr_table = nc.dram_tensor("general_pr_table", [N + W, HID], F32, kind="Internal").ap()
        drel_flat = nc.dram_tensor("general_drel_flat", [T * P], F32, kind="Internal").ap()

        raw_dst = sb("general_raw_dst", [P, 4, P], I32)
        raw_src = sb("general_raw_src", [P, 4, P], I32)
        raw_w = sb("general_raw_w", [P, 4, P])
        drel_t = sb("general_drel_t", [P, 4, P])
        src_t = sb("general_src_t", [P, 4, P])
        drel = sb("general_drel", [P, 4 * P])
        src_i = sb("general_src_i", [P, 4 * P], I32)
        wcol = sb("general_wcol", [P, 4 * P])
        ident = sb("general_ident", [P, P])
        iota_i = sb("general_iota_i", [P, P], I32)
        iota_row = sb("general_iota_row", [P, P])
        iota_ip = sb("general_iota_ip", [P, 1], I32)
        iota_p = sb("general_iota_p", [P, 1])
        ones_row = sb("general_ones_row", [1, P])
        neg_half = sb("general_neg_half", [P, NC])
        w1_sb = sb("general_w1_sb", [D, D])
        w2s_sb = sb("general_w2s_sb", [D, D])
        w2n_sb = sb("general_w2n_sb", [D, D])
        w2s_t = sb("general_w2s_t", [D, D])
        w2n_t = sb("general_w2n_t", [D, D])
        mw1_se = sb("general_mw1_se", [P, HID])
        mw1_r = sb("general_mw1_r", [D, HID])
        mb1_sb = sb("general_mb1_sb", [HID, 1])
        mw2_sb = sb("general_mw2_sb", [HID, D])
        mb2_row = sb("general_mb2_row", [1, G, D])
        nw1_h = sb("general_nw1_h", [D, HID])
        nw1_a = sb("general_nw1_a", [D, HID])
        nb1_sb = sb("general_nb1_sb", [HID, 1])
        nw2_sb = sb("general_nw2_sb", [HID, D])
        b1_bc = sb("general_b1_bc", [P, D])
        nb2_bc = sb("general_nb2_bc", [P, D])
        scale_bc = sb("general_scale_bc", [P, D])
        offset_bc = sb("general_offset_bc", [P, D])
        xs = sb("general_xs", [GP, NC, D])
        hs = sb("general_hs", [GP, NC, D])
        cur = sb("general_cur", [GP, NC, D])
        tmp = sb("general_tmp", [GP, NC, D])
        total = sb("general_total", [GP, NC, D])
        st_a = sb("general_st_a", [GP, NC])
        st_b = sb("general_st_b", [GP, NC])
        st_c = sb("general_st_c", [GP, NC])
        deg = sb("general_deg", [GP, NC, 2])
        dinv0 = sb("general_dinv0", [GP, NC])
        dinv0sq = sb("general_dinv0sq", [GP, NC])
        dinv1 = sb("general_dinv1", [GP, NC])
        rdeg = sb("general_rdeg", [GP, NC])
        h_t = sb("general_h_t", [D, NC, GP])
        acc_t = sb("general_acc_t", [D, N + W])
        acc_deg = sb("general_acc_deg", [2, N + W])
        pr_sb = sb("general_pr_sb", [GP, NC, HID])
        y1_t = sb("general_y1_t", [HID, 2, 4 * GP])
        X = sb("general_X", [P, Q, G, 2 * D])
        idx = sb("general_idx", [P, Q, G], I32)
        ow = sb("general_ow", [P, Q, G, 2])
        onehot = sb("general_onehot", [P, Q, G, W])
        onehot_t = sb("general_onehot_t", [P, Q, G * P])
        drel_bc = sb("general_drel_bc", [P, Q, G * P])
        prw = sb("general_prw", [W, Q, G, HID])
        x_t = sb("general_x_t", [P, 2, G * P])
        hid_t = sb("general_hid_t", [HID, 2, G * P])
        msg = sb("general_msg", [P, 2, G, D])

        big = ctx.enter_context(nc.psum_tensor("general_big", [P, 4, 512], F32))
        seg = ctx.enter_context(nc.psum_tensor("general_seg", [P, 4, 512], F32))
        big_nodes = big[:, :, :].rearrange("p a b -> p (a b)")[0:GP, 0:NC * D].rearrange("p (c d) -> p c d", d=D)

        ld_edges, ld_x, ld_w = sem("ld_edges"), sem("ld_x"), sem("ld_w")
        fills = sem("fills")
        pads = sem("pads")
        drel_stored = sem("drel_stored")
        gathered = [sem(f"gathered{q}") for q in range(Q)]
        idx_ready = [sem(f"idx_ready{q}") for q in range(Q)]
        onehot_ready = [sem(f"onehot_ready{q}") for q in range(Q)]
        seg_done = [sem(f"seg_done{q}") for q in range(Q)]
        edges_loaded = [sem(f"edges_loaded{q}") for q in range(Q)]
        drel_loaded = [sem(f"drel_loaded{q}") for q in range(Q)]
        prw_loaded = [sem(f"prw_loaded{q}") for q in range(Q)]
        onehot_t_ready = [sem(f"onehot_t_ready{q}") for q in range(Q)]
        transposed = [sem(f"transposed{r}") for r in range(2)]
        x_t_ready = [sem(f"x_t_ready{r}") for r in range(2)]
        hid_done = [sem(f"hid_done{r}") for r in range(2)]
        hid_ready = [sem(f"hid_ready{r}") for r in range(2)]
        msg_done = [sem(f"msg_done{r}") for r in range(2)]
        msg_ready = [sem(f"msg_ready{r}") for r in range(2)]
        acc_step = sem("acc_step")
        dve_chain = sem("dve_chain")
        pool_chain = sem("pool_chain")
        acc_cleared = sem("acc_cleared")
        table_ready, table_stored = sem("table_ready"), sem("table_stored")
        rstd_in, rstd_out = sem("rstd_in"), sem("rstd_out")
        gathers_begun = sem("gathers_begun")
        tail_loaded = sem("tail_loaded")
        ev = sem

        def on_sync(sp):
            sp.dma_start(xs[:, :, :], x.rearrange("(p c) d -> p c d", c=NC)).then_inc(ld_x, 16)
            sp.wait_ge(pads, 3)
            for raw, flat in ((raw_dst, dst), (raw_src, src), (raw_w, edge_weight)):
                sp.dma_start(raw[:, 0:3, :], flat[0:3 * P * P].rearrange("(c p e) -> p c e", p=P, e=P)).then_inc(ld_edges, 16)
                sp.dma_start(raw[0:FULL - 3 * P, 3, :], flat[3 * P * P:FULL * P].rearrange("(p e) -> p e", e=P)).then_inc(ld_edges, 16)
                sp.dma_start(raw[FULL - 3 * P:T - 3 * P, 3, 0:TAIL], flat[FULL * P:E].rearrange("(p e) -> p e", p=1)).then_inc(ld_edges, 16)
            loads = [(w1_sb[:, :], w1), (w2s_sb[:, :], w2s), (w2n_sb[:, :], w2n),
                     (mw1_se[0:D, :], mw1[0:D, :]), (mw1_se[D:2 * D, :], mw1[2 * D:3 * D, :]), (mw1_r[:, :], mw1[D:2 * D, :]),
                     (mb1_sb[:, :], mb1.rearrange("(p a) -> p a", a=1)), (mw2_sb[:, :], mw2),
                     (nw1_h[:, :], nw1[0:D, :]), (nw1_a[:, :], nw1[D:2 * D, :]),
                     (nb1_sb[:, :], nb1.rearrange("(p a) -> p a", a=1)), (nw2_sb[:, :], nw2),
                     (b1_bc[:, :], b1.partition_broadcast(P)), (nb2_bc[:, :], nb2.partition_broadcast(P)),
                     (scale_bc[:, :], ln_scale.partition_broadcast(P)), (offset_bc[:, :], ln_offset.partition_broadcast(P))]
            loads += [(mb2_row[:, j, :], mb2.rearrange("(a d) -> a d", a=1)) for j in range(G)]
            for a, b in loads:
                sp.dma_start(a, b).then_inc(ld_w, 16)
            sp.wait_ge(ev("drel_t_ready"), 1)
            sp.dma_start(drel_flat[0:3 * P * P].rearrange("(c p e) -> p c e", p=P, e=P), drel_t[:, 0:3, :]).then_inc(drel_stored, 16)
            sp.dma_start(drel_flat[3 * P * P:T * P].rearrange("(p e) -> p e", e=P), drel_t[0:T - 3 * P, 3, :]).then_inc(drel_stored, 16)

            sp.wait_ge(fills, 7)
            sp.dma_start(pr_table[N:N + W, :], ident[:, :]).then_inc(ev("pr_stored"), 16)

            for k in range(6):
                sp.wait_ge(table_ready, k + 1)
                sp.dma_start(table.rearrange("(p c) d -> p c d", c=NC), cur[:, :, :]).then_inc(table_stored, 16)
            sp.wait_ge(ev("pr_ready"), 1)
            sp.dma_start(pr_table[0:N, :].rearrange("(p c) h -> p c h", c=NC), pr_sb[:, :, :]).then_inc(ev("pr_stored"), 16)
            sp.wait_ge(ev("pr_stored"), 32)
            sp.wait_ge(drel_stored, 32)

            def l3_loads(it, q, base, edges):
                sp.wait_ge(seg_done[q], 1 + PASS_L3 * IT + it)
                if edges == G * P:
                    sp.dma_start(X[:, q, :, D:2 * D],
                                 edge_attr[bass.ds(base * P, G * P), :].rearrange("(j e) d -> e j d", e=P)).then_inc(edges_loaded[q], 16)
                else:
                    whole = edges // P
                    sp.dma_start(X[:, q, 0:whole, D:2 * D],
                                 edge_attr[base * P:(base + whole) * P, :].rearrange("(j e) d -> e j d", e=P)).then_inc(tail_loaded, 16)
                    sp.wait_ge(tail_loaded, 16)
                    sp.dma_start(X[0:edges - whole * P, q, whole, D:2 * D],
                                 edge_attr[(base + whole) * P:E, :]).then_inc(edges_loaded[q], 16)
                sp.dma_start(drel_bc[:, q, :], drel_flat[bass.ds(base * P, G * P)].partition_broadcast(P)).then_inc(drel_loaded[q], 16)
                _, nodes = nc.values_load_multi_w_load_instructions(
                    base_row[0:1, bass.ds(base, G)], engines=[sp.engine], min_val=0, max_val=N - 1,
                    skip_runtime_bounds_check_because="dst holds node numbers")
                for j in range(G):
                    sp.dma_start(prw[:, q, j, :], pr_table[bass.ds(nodes[j], W), :]).then_inc(prw_loaded[q], 16)

            with sp.Fori(0, IT - 1) as it:
                for q in range(Q):
                    l3_loads(it, q, it * (Q * G) + q * G, G * P)
            for q in range(Q):
                l3_loads(IT - 1, q, (IT - 1) * Q * G + q * G, G * P if q < Q - 1 else LAST_EDGES)
            sp.wait_ge(ev("out_ready"), 1)
            sp.dma_start(out.rearrange("(p c) d -> p c d", c=NC), xs[:, :, :]).then_inc(ev("out_stored"), 16)
            sp.wait_ge(ev("out_stored"), 16)

        def on_gpsimd(pool):
            pool.memset(raw_dst[:, 3, :], 1000000).then_inc(pads, 1)
            pool.memset(raw_src[:, 3, :], 0).then_inc(pads, 1)
            pool.memset(raw_w[:, 3, :], 0.0).then_inc(pads, 1)
            pool.memset(ident[:, :], 0.0).then_inc(pool_chain, 1)
            pool.iota(iota_i[:, :], [[1, P]], base=0, channel_multiplier=0).then_inc(pool_chain, 1)
            pool.iota(iota_ip[:, :], [[1, 1]], base=0, channel_multiplier=1).then_inc(pool_chain, 1)
            pool.wait_ge(pool_chain, 3)
            pool.affine_select(out=ident[:, :], in_=ident[:, :], compare_op=ALU.not_equal, fill=1.0,
                               base=0, pattern=[[-1, P]], channel_multiplier=1).then_inc(fills, 1)
            pool.tensor_copy(iota_row[:, :], iota_i[:, :]).then_inc(fills, 1)
            pool.tensor_copy(iota_p[:, :], iota_ip[:, :]).then_inc(fills, 1)
            pool.memset(ones_row[:, :], 1.0).then_inc(fills, 1)
            pool.memset(neg_half[:, :], -0.5).then_inc(fills, 1)
            pool.memset(ow[:, :, :, :], 1.0).then_inc(fills, 1)
            pool.memset(X[:, :, :, :], 0.0).then_inc(fills, 1)

            def powers(k):
                pool.wait_ge(rstd_in, k)
                pool.tensor_tensor(st_b[:, :], st_a[:, :], neg_half[0:GP, :], ALU.pow).then_inc(rstd_out, 1)

            def gathers(g):
                pool.wait_ge(table_stored, 16 * (g + 1))
                with pool.Fori(0, IT) as it:
                    for q in range(Q):
                        pool.wait_ge(idx_ready[q], g * IT + it + 1)
                        pool.wait_ge(seg_done[q], 1 + (g + 1) * IT + it)
                        pool.sem_inc(gathers_begun, 1)
                        for j in range(G):
                            pool.indirect_dma_start(
                                out=X[:, q, j, 0:D], out_offset=None, in_=table,
                                in_offset=bass.IndirectOffsetOnAxis(ap=idx[:, q, j:j + 1], axis=0)).then_inc(gathered[q], 16)

            pool.wait_ge(fills, 7)
            powers(1)
            powers(2)
            powers(3)
            for g in range(3):
                gathers(g)
            powers(4)
            gathers(3)
            powers(5)
            gathers(4)
            powers(6)
            gathers(5)
            powers(7)

        def evacuate_h(act, layer):
            for k in range(ROUNDS):
                chunks = min(4, NC - 4 * k)
                act.wait_ge(ev(f"h_ps_{layer}"), k + 1)
                nc.scalar.copy(h_t[:, 4 * k:4 * k + chunks, :],
                               seg[0:D, k % 4, 0:chunks * GP].rearrange("d (c p) -> d c p", p=GP)).then_inc(ev(f"h_t_{layer}"), 1)

        def on_scalar(act):
            for free in x_t_ready + hid_ready + msg_ready:
                act.sem_inc(free, 1)

            def copy_idx(n, g, it, q):
                act.wait_ge(seg_done[q], 1 + n)
                nc.scalar.copy(idx[:, q, :], src_i[:, bass.ds(it * (Q * G) + q * G, G)]).then_inc(idx_ready[q], 1)

            act.wait_ge(ev("edge_cols"), 3)
            act.wait_ge(fills, 7)
            with act.Fori(0, IT) as it:
                for q in range(Q):
                    act.wait_ge(seg_done[q], 1 + it)
                    nc.scalar.copy(ow[:, q, :, 1], wcol[:, bass.ds(it * (Q * G) + q * G, G)]).then_inc(ev(f"ow_ready{q}"), 1)
            for g in range(5):
                with act.Fori(0, IT) as it:
                    for q in range(Q):
                        copy_idx((g + 1) * IT + it, g, it, q)
                if g == 3:
                    evacuate_h(act, "L2")
            evacuate_h(act, "L3")
            for k in range(ROUNDS):
                chunks = min(4, NC - 4 * k)
                act.wait_ge(ev("pr_ps"), k + 1)
                op = nc.scalar.copy(pr_sb[:, 4 * k:4 * k + chunks, :],
                                    big[0:GP, k % 4, 0:chunks * HID].rearrange("p (c h) -> p c h", h=HID))
                op.then_inc(ev("pr_copied"), 1)
            act.wait_ge(ev("pr_copied"), ROUNDS)
            act.sem_inc(ev("pr_ready"), 1)
            with act.Fori(0, IT) as it:
                for q in range(Q):
                    copy_idx(PASS_L3 * IT + it, 5, it, q)
                for s in range(Q + 2):
                    if s < Q:
                        r, k = s % 2, it * 2 + s // 2
                        act.wait_ge(transposed[r], k + 1)
                        act.wait_ge(hid_done[r], 1 + k)
                        nc.scalar.copy(x_t[:, r, :], big[:, r, :]).then_inc(x_t_ready[r], 1)
                    if 1 <= s <= Q:
                        r, k = (s - 1) % 2, it * 2 + (s - 1) // 2
                        act.wait_ge(hid_done[r], 1 + k + 1)
                        act.wait_ge(msg_done[r], 1 + k)
                        nc.scalar.activation(hid_t[:, r, :], big[:, 2 + r, :], ACT.Relu, bias=mb1_sb[:, 0:1]).then_inc(hid_ready[r], 1)
                    if s >= 2:
                        q = s - 2
                        r, k = q % 2, it * 2 + q // 2
                        act.wait_ge(msg_done[r], 1 + k + 1)
                        if q >= 2:
                            act.wait_ge(seg_done[q - 2], 1 + PASS_L3 * IT + it + 1)
                        else:
                            act.wait_ge(seg_done[q + 2], 1 + PASS_L3 * IT + it)
                        nc.scalar.activation(msg[:, r, :, :], seg[:, 2 + r, 0:G * D].rearrange("p (j d) -> p j d", d=D),
                                             ACT.Relu).then_inc(msg_ready[r], 1)
            for k in range(ROUNDS):
                cols = min(4, NC - 4 * k) * GP
                act.wait_ge(ev("y1_ps"), k + 1)
                if k >= 2:
                    act.wait_ge(ev("y1_used"), k - 1)
                nc.scalar.activation(y1_t[:, k % 2, 0:cols], seg[:, k % 4, 0:cols], ACT.Relu, bias=nb1_sb[:, 0:1]).then_inc(ev("y1_ready"), 1)

        def on_tensor(pe):
            for free in seg_done + hid_done + msg_done:
                pe.sem_inc(free, 1)

            def edge_pass(n0, lhs, more=None):
                with pe.Fori(0, IT) as it:
                    for q in range(Q):
                        more(it, q)
                        pe.wait_ge(onehot_ready[q], n0 + it + 1)
                        pe.wait_ge(acc_step, n0 * (Q * G) + it * (Q * G) + (q + 1) * G)
                        for j in range(G):
                            a = lhs(q, j)
                            op = nc.tensor.matmul(seg[0:a.shape[1], q, j * W:(j + 1) * W], a, onehot[:, q, j, :],
                                                  start=True, stop=True)
                        op.then_inc(seg_done[q], 1)

            def wait_rows(g):
                def f(it, q):
                    pe.wait_ge(gathered[q], 16 * G * (g * IT + it + 1))
                return f

            def wait_ow(it, q):
                pe.wait_ge(ev(f"ow_ready{q}"), it + 1)

            def turn_acc(name):
                pe.wait_ge(acc_step, Q * G + turn_acc.passes * T)
                for c in range(NC):
                    op = nc.tensor.transpose(big_nodes[:, c, :], acc_t[:, c:N:NC], ident[0:D, 0:D])
                op.then_inc(ev(name), 1)

            def turn_h(layer):
                pe.wait_ge(ev(f"h_{layer}"), 1)
                for k in range(ROUNDS):
                    if k >= 4:
                        pe.wait_ge(ev(f"h_t_{layer}"), k - 3)
                    for c in range(4 * k, min(4 * k + 4, NC)):
                        op = nc.tensor.transpose(seg[0:D, k % 4, (c % 4) * GP:(c % 4 + 1) * GP], hs[:, c, :], ident[0:GP, 0:GP])
                    op.then_inc(ev(f"h_ps_{layer}"), 1)

            pe.wait_ge(fills, 7)
            pe.wait_ge(ev("drel_t_ready"), 1)
            pe.wait_ge(ev("src_t_ready"), 1)
            for b, t in enumerate((drel_t, src_t, raw_w)):
                for c in range(4):
                    op = nc.tensor.transpose(big[:, b, c * P:(c + 1) * P], t[:, c, :], ident[:, :])
                op.then_inc(ev("cols_ps"), 1)
            pe.wait_ge(ld_w, 16 * 20)
            nc.tensor.transpose(big[0:D, 3, 0:D], w2s_sb[:, :], ident[0:D, 0:D])
            nc.tensor.transpose(big[0:D, 3, D:2 * D], w2n_sb[:, :], ident[0:D, 0:D]).then_inc(ev("w2_ps"), 1)

            edge_pass(0, lambda q, j: ow[:, q, j, :], wait_ow)
            pe.wait_ge(acc_step, Q * G + T)
            pe.wait_ge(ev("w2_t"), 2)
            for c in range(NC):
                op = nc.tensor.transpose(big[0:GP, 0, 2 * c:2 * c + 2], acc_deg[:, c:N:NC], ident[0:2, 0:2])
            op.then_inc(ev("deg_ps"), 1)
            rows = lambda q, j: X[:, q, j, 0:D]
            for g in range(3):
                edge_pass((g + 1) * IT, rows, wait_rows(g))
                turn_acc.passes = g + 2
                turn_acc(f"sum_ps{g}")
            edge_pass(PASS_L1 * IT, rows, wait_rows(3))
            turn_acc.passes = 5
            turn_acc("sum_ps3")
            pe.wait_ge(ev("conv1_in"), 1)
            for k in range(ROUNDS):
                if k >= 4:
                    pe.wait_ge(ev("conv1_t"), k - 3)
                for c in range(4 * k, min(4 * k + 4, NC)):
                    op = nc.tensor.transpose(seg[0:D, k % 4, (c % 4) * GP:(c % 4 + 1) * GP], cur[:, c, :], ident[0:GP, 0:GP])
                op.then_inc(ev("conv1_ps"), 1)
            pe.wait_ge(ev("conv1_t"), ROUNDS)
            for c in range(NC):
                op = nc.tensor.matmul(big_nodes[:, c, :], h_t[:, c, :], w1_sb[:, :], start=True, stop=True)
            op.then_inc(ev("conv1_out"), 1)
            turn_h("L2")
            pe.wait_ge(ev("h_t_L2"), ROUNDS)
            for c in range(NC):
                op = nc.tensor.matmul(big_nodes[:, c, :], h_t[:, c, :], w2s_t[:, :], start=True, stop=True)
            op.then_inc(ev("self_out"), 1)
            edge_pass(PASS_L2 * IT, rows, wait_rows(4))
            pe.wait_ge(acc_step, Q * G + 6 * T)
            pe.wait_ge(ev("self_kept"), 1)
            for c in range(NC):
                op = nc.tensor.matmul(big_nodes[:, c, :], acc_t[:, c:N:NC], w2n_t[:, :], start=True, stop=True)
            op.then_inc(ev("neigh_out"), 1)
            turn_h("L3")
            pe.wait_ge(ev("h_t_L3"), ROUNDS)
            for k in range(ROUNDS):
                if k >= 4:
                    pe.wait_ge(ev("pr_copied"), k - 3)
                for c in range(4 * k, min(4 * k + 4, NC)):
                    op = nc.tensor.matmul(big[0:GP, k % 4, (c % 4) * HID:(c % 4 + 1) * HID], h_t[:, c, :], mw1_r[:, :], start=True, stop=True)
                op.then_inc(ev("pr_ps"), 1)
            pe.wait_ge(ev("pr_copied"), ROUNDS)
            n0 = PASS_L3 * IT
            with pe.Fori(0, IT) as it:
                for s in range(Q + 3):
                    if s < Q:
                        r, k = s % 2, it * 2 + s // 2
                        pe.wait_ge(gathered[s], 16 * G * (5 * IT + it + 1))
                        pe.wait_ge(edges_loaded[s], (it + 1) * 16)
                        pe.wait_ge(x_t_ready[r], 1 + k)
                        for j in range(G):
                            op = nc.tensor.transpose(big[:, r, j * P:(j + 1) * P], X[:, s, j, :], ident[:, :])
                        op.then_inc(transposed[r], 1)
                    if 1 <= s <= Q:
                        q = s - 1
                        r, k = q % 2, it * 2 + q // 2
                        pe.wait_ge(x_t_ready[r], 1 + k + 1)
                        pe.wait_ge(hid_ready[r], 1 + k)
                        pe.wait_ge(onehot_t_ready[q], it + 1)
                        pe.wait_ge(prw_loaded[q], (it + 1) * (16 * G))
                        nc.tensor.matmul(big[:, 2 + r, :], mw1_se[:, :], x_t[:, r, :], start=True, stop=True)
                        for j in range(G):
                            op = nc.tensor.matmul(big[:, 2 + r, j * P:(j + 1) * P], prw[:, q, j, :],
                                                  onehot_t[:, q, j * P:(j + 1) * P], start=False, stop=True,
                                                  skip_group_check=True)
                        op.then_inc(hid_done[r], 1)
                    if 2 <= s <= Q + 1:
                        q = s - 2
                        r, k = q % 2, it * 2 + q // 2
                        pe.wait_ge(hid_ready[r], 1 + k + 1)
                        pe.wait_ge(msg_ready[r], 1 + k)
                        nc.tensor.matmul(seg[:, 2 + r, 0:G * D], ones_row[:, :], mb2_row[:, :, :].rearrange("a j d -> a (j d)"),
                                         start=True, stop=True)
                        for j in range(G):
                            op = nc.tensor.matmul(seg[:, 2 + r, j * D:(j + 1) * D], hid_t[:, r, j * P:(j + 1) * P],
                                                  mw2_sb[:, :], start=False, stop=True, skip_group_check=True)
                        op.then_inc(msg_done[r], 1)
                    if s >= 3:
                        q = s - 3
                        r, k = q % 2, it * 2 + q // 2
                        pe.wait_ge(msg_ready[r], 1 + k + 1)
                        pe.wait_ge(onehot_ready[q], n0 + it + 1)
                        pe.wait_ge(acc_step, Q * G - G + PASS_L3 * T + it * (Q * G) + q * G)
                        for j in range(G):
                            op = nc.tensor.matmul(seg[0:D, r, j * W:(j + 1) * W], msg[:, r, j, :], onehot[:, q, j, :],
                                                  start=True, stop=True)
                        op.then_inc(seg_done[q], 1)
            pe.wait_ge(acc_step, Q * G + NPASS * T)
            for k in range(ROUNDS + 1):
                if k < ROUNDS:
                    n = min(4, NC - 4 * k)
                    if k >= 4:
                        pe.wait_ge(ev("y1_ready"), k - 3)
                    nc.tensor.matmul(seg[:, k % 4, 0:n * GP], nw1_h[:, :], h_t[:, 4 * k:4 * k + n, :], start=True, stop=False)
                    nc.tensor.matmul(seg[:, k % 4, 0:n * GP], nw1_a[:, :],
                                     acc_t[:, 0:N].rearrange("d (p c) -> d c p", c=NC)[:, 4 * k:4 * k + n, :],
                                     start=False, stop=True).then_inc(ev("y1_ps"), 1)
                if k >= 1:
                    pe.wait_ge(ev("y1_ready"), k)
                    for c in range(4 * k - 4, min(4 * k, NC)):
                        op = nc.tensor.matmul(big_nodes[:, c, :], y1_t[:, (k - 1) % 2, (c % 4) * GP:(c % 4 + 1) * GP], nw2_sb[:, :],
                                              start=True, stop=True)
                    op.then_inc(ev("y1_used"), 1)

        def on_vector(dve):
            dve.sem_inc(acc_step, Q * G)
            links = [0]
            pows = [0]

            def link(op):
                links[0] += 1
                op.then_inc(dve_chain, 1)
                dve.wait_ge(dve_chain, links[0])

            def per_node(v):
                return v[:, :].rearrange("p (c a) -> p c a", a=1).broadcast_to([GP, NC, D])

            def per_feature(v):
                return v[0:GP, :].rearrange("p (a d) -> p a d", a=1).broadcast_to([GP, NC, D])

            def invsqrt():
                pows[0] += 1
                dve.wait_ge(rstd_out, pows[0])

            def normalize(dst_, src_):
                link(dve.tensor_reduce(st_a[:, :], src_, AX.X, ALU.add))
                link(dve.tensor_scalar(st_c[:, :], st_a[:, :], 1.0 / D, None, ALU.mult))
                link(dve.tensor_tensor(dst_, src_, per_node(st_c), ALU.subtract))
                link(dve.tensor_tensor(tmp[:, :, :], dst_, dst_, ALU.mult))
                link(dve.tensor_reduce(st_c[:, :], tmp[:, :, :], AX.X, ALU.add))
                dve.tensor_scalar(st_a[:, :], st_c[:, :], 1.0 / D, EPS, ALU.mult, ALU.add).then_inc(rstd_in, 1)
                invsqrt()
                link(dve.tensor_tensor(dst_, dst_, per_node(st_b), ALU.mult))

            def pre_ln():
                normalize(hs[:, :, :], xs[:, :, :])
                link(dve.tensor_scalar(hs[:, :, :], hs[:, :, :], 0.0, None, ALU.max))

            def clear_acc():
                link(dve.memset(acc_t[:, :], 0.0))

            def edge_pass(n, weighted=False, acc=acc_t, rows=D, l3=False):
                with dve.Fori(0, IT) as it:
                    for q in range(Q):
                        base = it * (Q * G) + q * G
                        dve.wait_ge(seg_done[q], 1 + n * IT + it)
                        for j in range(G):
                            t = base + j
                            if weighted:
                                op = dve.tensor_scalar(onehot[:, q, j, :], iota_row[:, :], drel[:, bass.ds(t, 1)], wcol[:, bass.ds(t, 1)],
                                                       ALU.is_equal, ALU.mult)
                            else:
                                op = dve.tensor_scalar(onehot[:, q, j, :], iota_row[:, :], drel[:, bass.ds(t, 1)], None, ALU.is_equal)
                        op.then_inc(onehot_ready[q], 1)
                        if l3:
                            dve.wait_ge(drel_loaded[q], (it + 1) * 16)
                            dve.tensor_scalar(onehot_t[:, q, :], drel_bc[:, q, :], iota_p[:, 0:1], None, ALU.is_equal).then_inc(onehot_t_ready[q], 1)
                    for q in range(Q):
                        base = it * (Q * G) + q * G
                        bank = q % 2 if l3 else q
                        _, nodes = nc.values_load_multi_w_load_instructions(
                            base_row[0:1, bass.ds(base, G)], engines=[dve.engine], min_val=0, max_val=N - 1,
                            skip_runtime_bounds_check_because="dst holds node numbers")
                        dve.wait_ge(seg_done[q], 1 + n * IT + it + 1)
                        for j in range(G):
                            dve.wait_ge(acc_step, Q * G + n * T + base + j)
                            window = acc[:, bass.ds(nodes[j], W)]
                            dve.tensor_tensor(window, window, seg[0:rows, bank, j * W:(j + 1) * W], ALU.add).then_inc(acc_step, 1)

            dve.wait_ge(ld_edges, 9 * 16)
            dve.tensor_copy(src_t[:, :, :], raw_src[:, :, :]).then_inc(ev("src_t_ready"), 1)
            dve.tensor_tensor(drel_t[:, :, :], raw_dst[:, :, :], raw_dst[:, :, 0:1].broadcast_to([P, 4, P]), ALU.subtract).then_inc(ev("drel_t_ready"), 1)
            dve.wait_ge(ev("cols_ps"), 3)
            dve.tensor_copy(drel[:, :], big[:, 0, :]).then_inc(ev("edge_cols"), 1)
            dve.tensor_copy(src_i[:, :], big[:, 1, :]).then_inc(ev("edge_cols"), 1)
            dve.tensor_copy(wcol[:, :], big[:, 2, :]).then_inc(ev("edge_cols"), 1)
            dve.wait_ge(ev("edge_cols"), 3)
            dve.wait_ge(ev("w2_ps"), 1)
            dve.tensor_copy(w2s_t[:, :], big[0:D, 3, 0:D]).then_inc(ev("w2_t"), 1)
            dve.tensor_copy(w2n_t[:, :], big[0:D, 3, D:2 * D]).then_inc(ev("w2_t"), 1)
            dve.wait_ge(ev("w2_t"), 2)
            dve.wait_ge(ld_x, 16)
            dve.wait_ge(fills, 7)
            link(dve.memset(acc_deg[:, :], 0.0))
            pre_ln()
            edge_pass(PASS_DEG, acc=acc_deg, rows=2)
            dve.wait_ge(ev("deg_ps"), 1)
            link(dve.tensor_copy(deg[:, :, :], big[0:GP, 0, 0:2 * NC].rearrange("p (c a) -> p c a", a=2)))
            link(dve.tensor_scalar(rdeg[:, :], deg[:, :, 0], 1.0, None, ALU.max))
            dve.tensor_copy(st_a[:, :], rdeg[:, :]).then_inc(rstd_in, 1)
            link(dve.tensor_scalar(st_c[:, :], deg[:, :, 0], 0.0, None, ALU.is_gt))
            invsqrt()
            link(dve.tensor_tensor(dinv0[:, :], st_b[:, :], st_c[:, :], ALU.mult))
            link(dve.tensor_tensor(dinv0sq[:, :], dinv0[:, :], dinv0[:, :], ALU.mult))
            link(dve.reciprocal(rdeg[:, :], rdeg[:, :]))
            link(dve.tensor_scalar(deg[:, :, 1], deg[:, :, 1], 1.0, None, ALU.add))
            link(dve.tensor_scalar(dinv1[:, :], deg[:, :, 1], 0.0, None, ALU.is_gt))
            link(dve.tensor_tensor(st_c[:, :], deg[:, :, 1], dinv1[:, :], ALU.mult))
            link(dve.tensor_tensor(st_c[:, :], st_c[:, :], dinv1[:, :], ALU.subtract))
            dve.tensor_scalar(st_a[:, :], st_c[:, :], 1.0, None, ALU.add).then_inc(rstd_in, 1)
            invsqrt()
            link(dve.tensor_tensor(dinv1[:, :], dinv1[:, :], st_b[:, :], ALU.mult))

            link(dve.tensor_copy(total[:, :, :], hs[:, :, :]))
            link(dve.tensor_tensor(cur[:, :, :], hs[:, :, :], per_node(dinv0), ALU.mult))
            for g in range(3):
                clear_acc()
                dve.sem_inc(table_ready, 1)
                edge_pass(PASS_L0 + g)
                dve.wait_ge(ev(f"sum_ps{g}"), 1)
                link(dve.tensor_tensor(tmp[:, :, :], big_nodes, per_node(dinv0), ALU.mult))
                link(dve.tensor_tensor(total[:, :, :], total[:, :, :], tmp[:, :, :], ALU.add))
                if g < 2:
                    dve.wait_ge(table_stored, 16 * (g + 1))
                    link(dve.tensor_tensor(cur[:, :, :], big_nodes, per_node(dinv0sq), ALU.mult))
            link(dve.tensor_scalar(total[:, :, :], total[:, :, :], 0.25, None, ALU.mult))
            link(dve.tensor_tensor(xs[:, :, :], xs[:, :, :], total[:, :, :], ALU.add))

            pre_ln()
            link(dve.tensor_tensor(cur[:, :, :], hs[:, :, :], per_node(dinv1), ALU.mult))
            clear_acc()
            dve.sem_inc(table_ready, 1)
            edge_pass(PASS_L1, weighted=True)
            dve.wait_ge(ev("sum_ps3"), 1)
            dve.wait_ge(table_stored, 16 * 4)
            dve.tensor_tensor(cur[:, :, :], cur[:, :, :], big_nodes, ALU.add).then_inc(ev("conv1_in"), 1)
            for k in range(ROUNDS):
                chunks = min(4, NC - 4 * k)
                dve.wait_ge(ev("conv1_ps"), k + 1)
                dve.tensor_copy(h_t[:, 4 * k:4 * k + chunks, :],
                                seg[0:D, k % 4, 0:chunks * GP].rearrange("d (c p) -> d c p", p=GP)).then_inc(ev("conv1_t"), 1)
            dve.wait_ge(ev("conv1_out"), 1)
            link(dve.tensor_tensor(tmp[:, :, :], big_nodes, per_node(dinv1), ALU.mult))
            link(dve.tensor_tensor(tmp[:, :, :], tmp[:, :, :], per_feature(b1_bc), ALU.add))
            link(dve.scalar_tensor_tensor(xs[:, :, :], tmp[:, :, :], 0.0, xs[:, :, :], ALU.max, ALU.add))

            pre_ln()
            link(dve.tensor_copy(cur[:, :, :], hs[:, :, :]))
            clear_acc()
            dve.sem_inc(table_ready, 1)
            dve.sem_inc(ev("h_L2"), 1)
            dve.wait_ge(ev("self_out"), 1)
            dve.tensor_copy(total[:, :, :], big_nodes).then_inc(ev("self_kept"), 1)
            edge_pass(PASS_L2)
            dve.wait_ge(ev("self_kept"), 1)
            link(dve.tensor_tensor(xs[:, :, :], xs[:, :, :], total[:, :, :], ALU.add))
            dve.wait_ge(ev("neigh_out"), 1)
            link(dve.tensor_tensor(tmp[:, :, :], big_nodes, per_node(rdeg), ALU.mult))
            link(dve.tensor_tensor(xs[:, :, :], xs[:, :, :], tmp[:, :, :], ALU.add))

            pre_ln()
            dve.wait_ge(table_stored, 16 * 5)
            link(dve.tensor_copy(cur[:, :, :], hs[:, :, :]))
            clear_acc()
            dve.sem_inc(table_ready, 1)
            dve.sem_inc(ev("h_L3"), 1)
            edge_pass(PASS_L3, l3=True)
            dve.wait_ge(ev("y1_used"), ROUNDS)
            link(dve.tensor_tensor(total[:, :, :], big_nodes, per_feature(nb2_bc), ALU.add))
            normalize(cur[:, :, :], total[:, :, :])
            link(dve.tensor_tensor(cur[:, :, :], cur[:, :, :], per_feature(scale_bc), ALU.mult))
            link(dve.tensor_tensor(cur[:, :, :], cur[:, :, :], per_feature(offset_bc), ALU.add))
            link(dve.tensor_tensor(hs[:, :, :], hs[:, :, :], cur[:, :, :], ALU.add))
            dve.tensor_tensor(xs[:, :, :], xs[:, :, :], hs[:, :, :], ALU.add).then_inc(ev("out_ready"), 1)

        return {'sync': on_sync, 'gpsimd': on_gpsimd, 'scalar': on_scalar, 'tensor': on_tensor, 'vector': on_vector}


def dense_path(nc, sem, base_row, x, src, dst, edge_attr, edge_weight, w1, b1, w2s, w2n, mw1, mb1, mw2, mb2,
               nw1, nb1, nw2, nb2, ln_scale, ln_offset, out):
    with ExitStack() as ctx:
        def sb(name, shape, dt=F32):
            return ctx.enter_context(nc.sbuf_tensor(name, shape, dt))

        table = nc.dram_tensor("table", [NPAD, D], F32, kind="Internal").ap()
        pr_table = nc.dram_tensor("pr_table", [NPAD + GW, HID], F32, kind="Internal").ap()
        table_nodes = table.rearrange("(c p) d -> p c d", p=P)
        drel_flat = nc.dram_tensor("drel_flat", [T * P], F32, kind="Internal").ap()

        A = sb("A", [P, NC, WIDE], F16)
        a_words = A[:, :, :].rearrange("p s d -> p (s d)").bitcast(F32)
        carved = {"prep": 0, "l3": 0}

        def carve(phase, n):
            at = carved[phase]
            carved[phase] = at + n
            assert at + n <= NC * WIDE // 2
            return a_words[:, at:at + n]

        raw_dst, raw_src, raw_w = (carve("prep", 4 * P) for _ in range(3))
        group_base = carve("prep", 4).bitcast(I32)
        assert carved["prep"] <= EARLY
        raw_dst, raw_src = raw_dst.bitcast(I32), raw_src.bitcast(I32)
        src_lo, src_hi, dst_lo, dst_hi = (carve("prep", 4 * P).bitcast(I32) for _ in range(4))
        drel_t, src_t, dst_t, key_r_t, key_l_t = (carve("prep", 4 * P) for _ in range(5))
        below = carve("prep", 4 * THR)
        starts = carve("prep", THR)
        w_res = carve("prep", 4 * P)

        drel = sb("drel", [P, TK])
        src_i = sb("src_i", [P, TK], I32)
        wcol = sb("wcol", [P, TK])
        first_row = sb("first_row", [1, THR], I32)
        ident = sb("ident", [P, P])
        iota_row = sb("iota_row", [P, P])
        iota_p = sb("iota_p", [P, 1])
        iota_4 = sb("iota_4", [P, P, 4], F16)
        iota_r = sb("iota_r", [P, NC * B], F16)
        chunk_start = sb("chunk_start", [P, NC])
        ones = sb("ones", [P, 1])
        ones_bf = sb("ones_bf", [P, P], BF16)
        neg_half = sb("neg_half", [P, NC])
        join = sb("join", [P, D])
        w1_sb = sb("w1_sb", [D, D])
        w2_cat = sb("w2_cat", [D, 2 * D])
        w2_t = sb("w2_t", [2 * D, D])
        mw1_r = sb("mw1_r", [P, HID])[D:2 * D, :]
        b1_bc = sb("b1_bc", [P, D])
        xs = sb("xs", [P, NC, D])
        cur = sb("cur", [P, NC, D])
        pair = sb("pair", [P, NC * 2 * D])
        acc_mem = sb("acc_mem", [P, (2 * (KP * NC * B + KB * P + BC * KB + KC) + 4 * TK) // 2])
        st_a = sb("st_a", [P, NC])
        st_b = sb("st_b", [P, NC])
        st_c = sb("st_c", [P, NC])
        st_d = sb("st_d", [P, NC])
        deg = sb("deg", [P, NC, 4])
        dinv0 = sb("dinv0", [P, NC])
        dinv0sq = sb("dinv0sq", [P, NC])
        dinv1 = sb("dinv1", [P, NC])
        rdeg = sb("rdeg", [P, NC])
        idx = sb("idx", [P, Q, G], I32)

        key_r, key_l, dst_c = (pair[:, k * TK:(k + 1) * TK] for k in range(3))
        block_key = pair[:, 3 * TK:3 * TK + NC * BC]
        assert 3 * TK + NC * BC <= NC * D
        total = pair[:, NC * D:2 * NC * D].rearrange("p (c d) -> p c d", d=D)
        hop = pair[:, 0:NC * D].rearrange("p (c d) -> p c d", d=D)
        rows1 = pair[:, 0:Q * G * D].rearrange("p (q j d) -> p q j d", q=Q, j=G)
        onehot1 = pair[:, Q * G * D:Q * G * (D + GW)].rearrange("p (q j w) -> p q j w", q=Q, j=G)
        turn1 = pair[0:D, Q * G * (D + GW):Q * G * (D + GW) + 2 * 4 * P].rearrange("p (r e) -> p r e", r=2)
        h_nb = pair[:, :].rearrange("p (c d) -> p c d", d=2 * D)
        nb = h_nb[:, :, 0:D]
        hs = h_nb[:, :, D:2 * D]
        acc_h = acc_mem[:, :].bitcast(F16)
        hot_r = acc_h[:, 0:2 * KP * NC * B].rearrange("p (u k v) -> p u k v", u=2, k=KP)
        hot_l_at = 2 * KP * NC * B
        w_parts_at = hot_l_at + 2 * KB * P
        rel_at = w_parts_at + 4 * TK
        hot_l = acc_h[:, hot_l_at:w_parts_at].rearrange("p (b v k) -> p b v k", b=2, k=KB)
        w_parts = acc_mem[:, :].bitcast(BF16)[:, w_parts_at:rel_at].rearrange("p (t v) -> p t v", v=4)
        rel = acc_h[:, rel_at:rel_at + 2 * (BC * KB + KC)].rearrange("p (r v) -> p r v", r=2)
        half = NC * 2 * D
        x_parts = [m.bitcast(F16)[:, 0:half].rearrange("p (s k d) -> p s k d", k=2, d=D)
                   for m in (acc_mem[:, 0:half // 2], pair[:, 0:half // 2])]
        sums_t = acc_mem[:, half // 2:half // 2 + 2 * 4 * P].rearrange("p (r e) -> p r e", r=2)
        acc_t = acc_mem[0:D, :]
        h_t = acc_mem[D:2 * D, 0:NPAD]
        hot_d = cur[:, :, :].rearrange("p c d -> p (c d)").bitcast(F16)[:, 0:KG * 4 * P].rearrange("p (g v k) -> p g v k", g=KG, k=4)

        low, high = (cur[:, :, :].rearrange("p c d -> p (c d)")[:, at:at + NC // 5 * D // 2].rearrange("p (c d) -> p c d", d=D // 2)
                     for at in (KG * 4 * P // 2, KG * 4 * P // 2 + NC // 5 * D // 2))

        X = carve("l3", Q * G * 2 * D).rearrange("p (q j d) -> p q j d", q=Q, j=G)
        onehot3 = carve("l3", Q * G * GW).rearrange("p (q j w) -> p q j w", q=Q, j=G)
        onehot_t = carve("l3", Q * G * P)[0:GW, :].rearrange("p (q e) -> p q e", q=Q)
        drel_bc = carve("l3", Q * G * P)[0:GW, :].rearrange("p (q e) -> p q e", q=Q)
        prw = carve("l3", Q * HID)[0:GW, :].rearrange("p (q h) -> p q h", q=Q)
        x_t = carve("l3", 2 * G * P).rearrange("p (r e) -> p r e", r=2)
        hid_t = carve("l3", 2 * G * P).rearrange("p (r e) -> p r e", r=2)
        msg = carve("l3", 2 * G * D).rearrange("p (r j d) -> p r j d", r=2, j=G)
        pr_sb = carve("l3", NC * HID).rearrange("p (c h) -> p c h", h=HID)
        y1_t = carve("l3", 2 * 4 * P).rearrange("p (r e) -> p r e", r=2)
        mw1_se = carve("l3", HID)
        mb1_sb = carve("l3", 1)
        mw2_sb = carve("l3", D)
        mb2_bc = carve("l3", G * D)
        mb2_rest = carve("l3", G * D)
        mb2_parts = carve("l3", 3 * G * D // 2).bitcast(BF16).rearrange("p (k d) -> p k d", k=3)
        mb2_sum = carve("l3", G * D // 2).bitcast(BF16)
        nw1_ah = carve("l3", HID)
        nb1_sb = carve("l3", 1)
        nw2_sb = carve("l3", D)
        nb2_bc = carve("l3", D)
        scale_bc = carve("l3", D)
        offset_bc = carve("l3", D)
        turn2_ring = acc_mem[:, 0:2 * 4 * P].rearrange("p (r e) -> p r e", r=2)
        scratch = a_words[:, NC * WIDE // 2 - NC * D:NC * WIDE // 2].rearrange("p (c d) -> p c d", d=D)

        big = ctx.enter_context(nc.psum_tensor("big", [P, 4, 512], F32))
        seg = ctx.enter_context(nc.psum_tensor("seg", [P, 4, 512], F32))
        big_nodes = big[:, :, :].rearrange("p a b -> p (a b)")[:, 0:NC * D].rearrange("p (c d) -> p c d", d=D)
        banks = [big[:, b, :] for b in range(4)] + [seg[:, b, :] for b in range(4)]

        ld_edges, ld_x, ld_w, ld_l3 = sem("dense_ld_edges"), sem("ld_x"), sem("ld_w"), sem("ld_l3")
        fills = sem("fills")
        pads = sem("dense_pads")
        drel_stored = sem("drel_stored")
        hots_ready = [sem(f"hots_ready{b}") for b in range(2)]
        block_built = [sem(f"block_built{b}") for b in range(2)]
        block_kept = [sem(f"block_kept{b}") for b in range(2)]
        hot_d_ready = [sem(f"hot_d_ready{g}") for g in range(KG)]
        hot_d_used = [sem(f"hot_d_used{g}") for g in range(KG)]
        last_hot_ready = sem("last_hot_ready")
        distance_ready = sem("distance_ready")
        rel_ready = sem("rel_ready")
        gathered = [sem(f"gathered{q}") for q in range(Q)]
        idx_ready = [sem(f"idx_ready{q}") for q in range(Q)]
        onehot_ready = [sem(f"onehot_ready{q}") for q in range(Q)]
        seg_done = [sem(f"seg_done{q}") for q in range(Q)]
        edges_loaded = [sem(f"edges_loaded{q}") for q in range(Q)]
        drel_loaded = [sem(f"drel_loaded{q}") for q in range(Q)]
        prw_loaded = [sem(f"prw_loaded{q}") for q in range(Q)]
        onehot_t_ready = [sem(f"onehot_t_ready{q}") for q in range(Q)]
        transposed = [sem(f"transposed{r}") for r in range(2)]
        x_t_ready = [sem(f"x_t_ready{r}") for r in range(2)]
        hid_done = [sem(f"hid_done{r}") for r in range(2)]
        hid_ready = [sem(f"hid_ready{r}") for r in range(2)]
        msg_done = [sem(f"msg_done{r}") for r in range(2)]
        msg_ready = [sem(f"msg_ready{r}") for r in range(2)]
        acc_step = sem("acc_step")
        dve_chain = sem("dve_chain")
        pool_chain = sem("pool_chain")
        table_ready, table_stored = sem("table_ready"), sem("table_stored")
        waits_carried = sem("waits_carried")
        tail_loaded = sem("tail_loaded")
        ev = sem

        def round_nodes(n, k):
            return big[:, (n * ROUNDS + k) % 4, 0:4 * D].rearrange("p (c d) -> p c d", d=D)

        def per_node(v):
            return v[:, :].rearrange("p (c a) -> p c a", a=1).broadcast_to([P, NC, D])

        def load_nodes(eng, row, at, n, top):
            _, v = nc.values_load_multi_w_load_instructions(
                row[0:1, bass.ds(at, n)], engines=[eng.engine], min_val=0, max_val=top,
                skip_runtime_bounds_check_because="node or tile numbers, bounded where they were made")
            return v

        def load_edges(sp):
            sp.wait_ge(pads, 4)
            for raw, flat in ((raw_dst, dst), (raw_src, src), (raw_w, edge_weight)):
                raw = raw.rearrange("p (c e) -> p c e", e=P)
                sp.dma_start(raw[:, 0:3, :], flat[0:3 * P * P].rearrange("(c p e) -> p c e", p=P, e=P)).then_inc(ld_edges, 16)
                sp.dma_start(raw[0:FULL - 3 * P, 3, :], flat[3 * P * P:FULL * P].rearrange("(p e) -> p e", e=P)).then_inc(ld_edges, 16)
                sp.dma_start(raw[FULL - 3 * P:T - 3 * P, 3, 0:TAIL], flat[FULL * P:E].rearrange("(p e) -> p e", p=1)).then_inc(ld_edges, 16)
            for c in range(4):
                groups = min(P // G, GROUPS - c * P // G)
                sp.dma_start(group_base[0:groups * G, c:c + 1],
                             bass.AP(dst.tensor, c * P * P, [[G * P, groups], [0, G], [1, 1]]),
                             allow_slow_non_contiguous=True).then_inc(ld_edges, 16)

        def on_sync(sp):
            sp.dma_start(xs[:, 0:NC - 1, :], x[0:(NC - 1) * P, :].rearrange("(c p) d -> p c d", p=P)).then_inc(ld_x, 16)
            sp.wait_ge(ev("x_padded"), 1)
            sp.dma_start(xs[0:LASTN, NC - 1, :], x[(NC - 1) * P:N, :]).then_inc(ld_x, 16)
            for a, b in ((w1_sb[:, :], w1), (w2_cat[:, 0:D], w2n), (w2_cat[:, D:2 * D], w2s),
                         (mw1_r, mw1[D:2 * D, :]), (b1_bc[:, :], b1.partition_broadcast(P))):
                sp.dma_start(a, b).then_inc(ld_w, 16)
            sp.wait_ge(ev("drel_t_ready"), 1)
            flat_t = drel_t.rearrange("p (c e) -> p c e", e=P)
            sp.dma_start(drel_flat[0:3 * P * P].rearrange("(c p e) -> p c e", p=P, e=P), flat_t[:, 0:3, :]).then_inc(drel_stored, 16)
            sp.dma_start(drel_flat[3 * P * P:T * P].rearrange("(p e) -> p e", e=P), flat_t[0:T - 3 * P, 3, :]).then_inc(drel_stored, 16)
            sp.wait_ge(fills, 9)
            sp.dma_start(pr_table[NPAD:NPAD + GW, :], ident[0:GW, :]).then_inc(ev("pr_stored"), 16)

            for k, cols in enumerate(HALVES):
                sp.wait_ge(table_ready, k + 1)
                sp.dma_start(table_nodes[:, cols, :], cur[:, cols, :]).then_inc(table_stored, 16)

            sp.wait_ge(ev("adjacency_over"), 1)
            for a, b in ((mw1_se[0:D, :], mw1[0:D, :]), (mw1_se[D:2 * D, :], mw1[2 * D:3 * D, :]),
                         (mb1_sb, mb1.rearrange("(p a) -> p a", a=1)), (mw2_sb, mw2),
                         (nw1_ah[0:D, :], nw1[D:2 * D, :]), (nw1_ah[D:2 * D, :], nw1[0:D, :]),
                         (nb1_sb, nb1.rearrange("(p a) -> p a", a=1)), (nw2_sb, nw2),
                         (nb2_bc, nb2.partition_broadcast(P)),
                         (scale_bc, ln_scale.partition_broadcast(P)), (offset_bc, ln_offset.partition_broadcast(P)),
                         *((mb2_bc[:, j * D:(j + 1) * D], mb2.partition_broadcast(P)) for j in range(G))):
                sp.dma_start(a, b).then_inc(ld_l3, 16)
            for k, cols in enumerate(HALVES):
                sp.wait_ge(table_ready, k + 3)
                sp.dma_start(table_nodes[:, cols, :], hs[:, cols, :]).then_inc(table_stored, 16)
            sp.wait_ge(ev("pr_ready"), 1)
            sp.dma_start(pr_table[0:NPAD, :].rearrange("(c p) h -> p c h", p=P), pr_sb).then_inc(ev("pr_stored"), 16)
            sp.wait_ge(ev("pr_stored"), 32)
            sp.wait_ge(drel_stored, 32)

            def l3_loads(it, q, base, edges):
                sp.wait_ge(hid_done[q % 2], 1 + 2 * it + q // 2)
                if edges == G * P:
                    sp.dma_start(X[:, q, :, D:2 * D],
                                 edge_attr[bass.ds(base * P, G * P), :].rearrange("(j e) d -> e j d", e=P)).then_inc(edges_loaded[q], 16)
                else:
                    whole = edges // P
                    sp.dma_start(X[:, q, 0:whole, D:2 * D],
                                 edge_attr[base * P:(base + whole) * P, :].rearrange("(j e) d -> e j d", e=P)).then_inc(tail_loaded, 16)
                    sp.wait_ge(tail_loaded, 16)
                    sp.dma_start(X[0:edges - whole * P, q, whole, D:2 * D],
                                 edge_attr[(base + whole) * P:E, :]).then_inc(edges_loaded[q], 16)
                sp.dma_start(drel_bc[:, q, :], drel_flat[bass.ds(base * P, G * P)].partition_broadcast(GW)).then_inc(drel_loaded[q], 16)
                node = load_nodes(sp, base_row, base, 1, N - 1)[0]
                sp.dma_start(prw[:, q, :], pr_table[bass.ds(node, GW), :]).then_inc(prw_loaded[q], 16)

            with sp.Fori(0, IT - 1) as it:
                for q in range(Q):
                    l3_loads(it, q, it * (Q * G) + q * G, G * P)
            for q in range(Q):
                l3_loads(IT - 1, q, (IT - 1) * Q * G + q * G, G * P if q < Q - 1 else LAST_EDGES)
            for k, cols in enumerate(HALVES):
                sp.wait_ge(ev("out_ready"), k + 1)
                whole = min(cols.stop, NC - 1)
                sp.dma_start(out[cols.start * P:whole * P, :].rearrange("(c p) d -> p c d", p=P), xs[:, cols.start:whole, :]).then_inc(ev("out_stored"), 16)
            sp.dma_start(out[(NC - 1) * P:N, :], xs[0:LASTN, NC - 1, :]).then_inc(ev("out_stored"), 16)
            sp.wait_ge(ev("out_stored"), 48)

        def pad_edges(pool):
            pool.memset(raw_dst[:, 3 * P:4 * P], NOWHERE).then_inc(pads, 1)
            pool.memset(raw_src[:, 3 * P:4 * P], 0).then_inc(pads, 1)
            pool.memset(raw_w[:, 3 * P:4 * P], 0.0).then_inc(pads, 1)
            pool.memset(group_base, 0).then_inc(pads, 1)

        def on_gpsimd(pool):
            pool.memset(xs[:, NC - 1, :], 0.0).then_inc(ev("x_padded"), 1)
            pool.memset(ident[:, :], 0.0).then_inc(pool_chain, 1)
            pool.wait_ge(pool_chain, 1)
            pool.affine_select(out=ident[:, :], in_=ident[:, :], compare_op=ALU.not_equal, fill=1.0,
                               base=0, pattern=[[-1, P]], channel_multiplier=1).then_inc(fills, 1)
            for tile, pattern, per_partition in (
                    (iota_row[:, :], [[1, P]], 0), (iota_p[:, :], [[1, 1]], 1), (iota_4[:, :, :], [[1, P], [0, 4]], 0),
                    (iota_r[:, :], [[1, NC * B]], 0), (block_key, [[P, NC * BC]], 0), (chunk_start[:, :], [[P, NC]], 0),
                    (starts, [[B, THR]], 0)):
                pool.iota(tile, pattern, base=0, channel_multiplier=per_partition,
                          allow_small_or_imprecise_dtypes=True).then_inc(fills, 1)
            pool.memset(ones[:, :], 1.0)
            pool.memset(neg_half[:, :], -0.5)
            pool.memset(ones_bf[:, :], 1.0).then_inc(fills, 1)

            pool_links = [1]

            def pool_link(op):
                pool_links[0] += 1
                op.then_inc(pool_chain, 1)
                pool.wait_ge(pool_chain, pool_links[0])

            def gathers(g, rows, slot_free):
                pool.wait_ge(table_stored, 32 * (g + 1))
                with pool.Fori(0, IT) as it:
                    for q in range(Q):
                        pool.wait_ge(idx_ready[q], g * IT + it + 1)
                        slot_free(it, q)
                        pool.sem_inc(waits_carried, 1)
                        for j in range(G):
                            pool.indirect_dma_start(
                                out=rows[:, q, j, 0:D], out_offset=None, in_=table,
                                in_offset=bass.IndirectOffsetOnAxis(ap=idx[:, q, j:j + 1], axis=0)).then_inc(gathered[q], 16)

            def rows_summed(it, q):
                pool.wait_ge(seg_done[q], 1 + it)

            def rows_transposed(it, q):
                pool.wait_ge(transposed[q % 2], 1 + 2 * it + q // 2)

            pool.wait_ge(fills, 9)
            def relatives(c, blocks, slot):
                firsts = load_nodes(pool, first_row, c * BC, blocks, T)
                if not isinstance(c, int) or c >= 2:
                    pool.wait_ge(hot_d_used[KG - 1], c)
                for j in range(blocks):
                    pool.tensor_tensor(rel[:, slot, j * KB:(j + 1) * KB], key_l[:, bass.ds(firsts[j], KB)],
                                       block_key[:, bass.ds(c * BC + j, 1)].broadcast_to([P, KB]), ALU.subtract)
                pool.tensor_tensor(rel[:, slot, BC * KB:BC * KB + KC], dst_c[:, bass.ds(firsts[0], KC)],
                                   chunk_start[:, bass.ds(c, 1)].broadcast_to([P, KC]), ALU.subtract).then_inc(rel_ready, 1)

            def sum_pairs(a, b):
                width = D // 2
                while width:
                    pool_link(pool.tensor_tensor(low[:, :, 0:width], a[:, :, 0:width], b[:, :, 0:width], ALU.add))
                    width //= 2
                    a, b = low, low[:, :, width:D // 2]

            def ln0_fifth(k):
                cols = slice(k * NC // 5, (k + 1) * NC // 5)
                sum_pairs(xs[:, cols, 0:D // 2], xs[:, cols, D // 2:D])
                pool_link(pool.tensor_scalar(st_a[:, cols], low[:, :, 0], 1.0 / D, None, ALU.mult))
                pool_link(pool.tensor_tensor(total[:, cols, :], xs[:, cols, :], per_node(st_a)[:, cols, :], ALU.subtract))
                for half_sq, side in ((low, slice(0, D // 2)), (high, slice(D // 2, D))):
                    pool_link(pool.tensor_tensor(half_sq, total[:, cols, side], total[:, cols, side], ALU.mult))
                sum_pairs(low, high)
                pool_link(pool.tensor_scalar(st_a[:, cols], low[:, :, 0], 1.0 / D, EPS, ALU.mult, ALU.add))

            pool.wait_ge(ld_x, 32)
            pool.wait_ge(ev("keys_ready"), 1)
            pool.wait_ge(ev("ranges_ready"), 1)
            relatives(0, BC, 0)
            for k in range(5):
                relatives(k + 1, BC, (k + 1) % 2)
                ln0_fifth(k)
            relatives(6, BC, 0)
            pool_link(pool.tensor_tensor(st_a[:, :], st_a[:, :], neg_half[:, :], ALU.pow))
            relatives(7, BC, 1)
            pool_link(pool.tensor_tensor(total, total, per_node(st_a), ALU.mult))
            relatives(8, BC, 0)
            pool_link(pool.tensor_scalar(total, total, 0.0, None, ALU.max))
            pool.sem_inc(ev("h_L0"), 1)
            relatives(9, BC, 1)
            with pool.Fori(5, NC // 2) as two:
                relatives(two * 2, BC, 0)
                relatives(two * 2 + 1, BC, 1)
            relatives(NC - 1, LASTB, 0)
            gathers(0, rows1, rows_summed)
            gathers(1, X, rows_transposed)

        def steps(eng, stages):
            longest = max(lag for lag, _ in stages)
            peeled = -(-longest // Q)

            def one_step(it, s, first, last):
                for lag, f in stages:
                    if first <= s - lag < last:
                        f(it + (s - lag) // Q, (s - lag) % Q)

            for s in range(peeled * Q):
                one_step(0, s, 0, GROUPS)
            with eng.Fori(peeled, IT) as it:
                for s in range(Q):
                    one_step(it, s, -longest, Q)
            for s in range(longest):
                one_step(IT, s, -longest, 0)

        def copy_idx(it, q):
            nc.scalar.copy(idx[:, q, :], src_i[:, bass.ds(it * (Q * G) + q * G, G)]).then_inc(idx_ready[q], 1)

        def on_scalar(act):
            for free in x_t_ready + hid_ready + msg_ready:
                act.sem_inc(free, 1)
            for free in block_kept:
                act.sem_inc(free, 2)
            for b, t in ((3, drel[:, :]), (5, wcol[:, :])):
                act.wait_ge(ev("cols_ps"), b + 1)
                nc.scalar.copy(t, banks[b][:, 0:TK]).then_inc(ev("cols_kept"), 1)
            act.wait_ge(ev("w2_ps"), 1)
            nc.scalar.copy(w2_t[:, :], banks[7][:, 0:D]).then_inc(ev("cols_kept"), 1)
            act.wait_ge(ev("keys_ready"), 1)
            act.wait_ge(ev("ranges_ready"), 1)
            act.wait_ge(drel_stored, 32)

            def last_hot(c, p, first):
                pair_no = c * (BC // 2) + p
                hot = hot_r[:, p % 2, KP - 1, :]
                act.wait_ge(block_built[1], pair_no + 1)
                nc.scalar.activation(hot, iota_r[:, :], ACT.Abs, bias=key_r[:, bass.ds(first + (KP - 1), 1)],
                                     scale=-1.0).then_inc(distance_ready, 1)
                act.wait_ge(distance_ready, pair_no + 1)
                nc.scalar.activation(hot, hot, ACT.Relu, bias=ones[:, :], scale=-1.0).then_inc(last_hot_ready, 1)

            def keep_blocks(c, blocks):
                firsts = load_nodes(act, first_row, c * BC + 2, BC, T)
                for j in range(blocks):
                    b = j % 2
                    if b == 0 and (blocks == BC or j + 2 < blocks):
                        last_hot(c, j // 2 + 1, firsts[j])
                    act.wait_ge(block_built[b], c * (BC // 2) + (j // 2 + 2 + b))
                    nc.scalar.copy(A[:, :, bass.ds(c * P + j * B, B)],
                                   big[:, j % 4, 0:NC * B].rearrange("p (s d) -> p s d", d=B)).then_inc(block_kept[b], 1)

            last_hot(0, 0, load_nodes(act, first_row, 0, 1, T)[0])
            with act.Fori(0, NC - 1) as c:
                keep_blocks(c, BC)
            keep_blocks(NC - 1, LASTB)

            def copy_sums(n):
                for k in range(ROUNDS):
                    cols = min(4 * P, WIDE - 4 * k * P)
                    act.wait_ge(ev("sums_ps"), n * ROUNDS + k + 1)
                    if n * ROUNDS + k >= 2:
                        act.wait_ge(ev("sums_nodes"), n * ROUNDS + k - 1)
                    nc.scalar.copy(sums_t[:, k % 2, 0:cols], seg[:, 2 + k % 2, 0:cols]).then_inc(ev("sums_t"), 1)

            for n in range(3):
                copy_sums(n)

            for q in range(Q):
                copy_idx(0, q)
            for k in range(ROUNDS):
                n = min(4, NC - 4 * k) * P
                act.wait_ge(ev("turn1_ps"), k + 1)
                if k >= 2:
                    act.wait_ge(ev("turn1_used"), k - 1)
                nc.scalar.copy(turn1[:, k % 2, 0:n], seg[0:D, k % 2, 0:n]).then_inc(ev("turn1_ready"), 1)
            with act.Fori(1, IT) as it:
                for q in range(Q):
                    act.wait_ge(seg_done[q], 1 + it)
                    copy_idx(it, q)
            for q in range(Q):
                act.wait_ge(seg_done[q], 1 + IT)
                copy_idx(0, q)

            copy_sums(3)
            for k in range(ROUNDS):
                n = min(4, NC - 4 * k) * P
                act.wait_ge(ev("turn2_ps"), k + 1)
                if k >= 2:
                    act.wait_ge(ev("turn2_used"), k - 1)
                nc.scalar.copy(turn2_ring[:, k % 2, 0:n], seg[:, k % 2, 0:n]).then_inc(ev("turn2_ready"), 1)

            for k in range(ROUNDS):
                n = min(4, NC - 4 * k) * P
                act.wait_ge(ev("h_ps"), k + 1)
                nc.scalar.copy(h_t[:, 4 * k * P:4 * k * P + n], seg[D:2 * D, k % 4, 0:n]).then_inc(ev("h_t"), 1)
            for k in range(ROUNDS):
                chunks = min(4, NC - 4 * k)
                act.wait_ge(ev("pr_ps"), k + 1)
                nc.scalar.copy(pr_sb[:, 4 * k:4 * k + chunks, :],
                               big[:, k % 4, 0:chunks * HID].rearrange("p (c h) -> p c h", h=HID)).then_inc(ev("pr_copied"), 1)
            act.wait_ge(ev("pr_copied"), ROUNDS)
            act.sem_inc(ev("pr_ready"), 1)
            act.wait_ge(ld_l3, 15 * 16)

            def next_idx(it, q):
                if isinstance(it, int) and it == 0:
                    return
                act.wait_ge(transposed[q % 2], 1 + 2 * it + q // 2)
                copy_idx(it, q)

            def copy_rows(it, q):
                r, k = q % 2, it * 2 + q // 2
                act.wait_ge(transposed[r], k + 3)
                act.wait_ge(hid_done[r], k + 2)
                nc.scalar.copy(x_t[:, r, :], big[:, r, :]).then_inc(x_t_ready[r], 1)

            def hidden(it, q):
                r, k = q % 2, it * 2 + q // 2
                act.wait_ge(hid_done[r], k + 3)
                act.wait_ge(msg_done[r], k + 1)
                nc.scalar.activation(hid_t[:, r, :], big[:, 2 + r, :], ACT.Relu, bias=mb1_sb).then_inc(hid_ready[r], 1)

            def message(it, q):
                r, k = q % 2, it * 2 + q // 2
                act.wait_ge(msg_done[r], k + 2)
                if q >= 2:
                    act.wait_ge(seg_done[q - 2], 2 + IT + it)
                else:
                    act.wait_ge(seg_done[q + 2], 1 + IT + it)
                nc.scalar.activation(msg[:, r, :, :], seg[:, 2 + r, 0:G * D].rearrange("p (j d) -> p j d", d=D),
                                     ACT.Relu).then_inc(msg_ready[r], 1)

            steps(act, [(0, next_idx), (3, copy_rows), (4, hidden), (5, message)])
            for k in range(ROUNDS):
                n = min(4, NC - 4 * k) * P
                act.wait_ge(ev("y1_ps"), k + 1)
                if k >= 2:
                    act.wait_ge(ev("y1_used"), k - 1)
                nc.scalar.activation(y1_t[:, k % 2, 0:n], seg[:, k % 4, 0:n], ACT.Relu, bias=nb1_sb).then_inc(ev("y1_ready"), 1)

        def on_tensor(pe):
            for free in seg_done + hid_done + msg_done + hot_d_used + block_built:
                pe.sem_inc(free, 1)
            for free in (hid_done + block_built[1:]):
                pe.sem_inc(free, 1)
            for free in transposed:
                pe.sem_inc(free, 2)

            pe.wait_ge(fills, 9)
            for b, (t, name) in enumerate(((dst_t, "dst_t"), (key_r_t, "key_r_t"), (key_l_t, "key_l_t"),
                                           (drel_t, "drel_t"), (src_t, "src_t"), (raw_w, None))):
                if name:
                    pe.wait_ge(ev(name + "_ready"), 1)
                for c in range(4):
                    op = nc.tensor.transpose(banks[b][:, c * P:(c + 1) * P], t[:, c * P:(c + 1) * P], ident[:, :])
                op.then_inc(ev("cols_ps"), 1)
            pe.wait_ge(ev("below_ready"), 1)
            for c in range(4):
                op = nc.tensor.matmul(banks[6][0:1, 0:THR], ones[:, :], below[:, c * THR:(c + 1) * THR], start=(c == 0), stop=(c == 3))
            op.then_inc(ev("counts_ps"), 1)
            pe.wait_ge(ld_w, 16 * 5)
            nc.tensor.transpose(banks[7][:, 0:D], w2_cat[:, :], ident[0:D, 0:D]).then_inc(ev("w2_ps"), 1)
            pe.wait_ge(ev("cols_kept"), 3)
            pe.wait_ge(ev("keys_ready"), 1)
            pe.wait_ge(ev("ranges_ready"), 1)

            def blocks_and_degrees(c, blocks):
                firsts = load_nodes(pe, first_row, c * BC, blocks, T)
                first = firsts[0]
                degree_groups = 0
                for j in range(blocks):
                    b = j % 2
                    use = c * (BC // 2) + j // 2
                    pe.wait_ge(hots_ready[b], use + 1)
                    if b:
                        pe.wait_ge(last_hot_ready, use + 1)
                        at = (firsts[j] - firsts[j - 1]).with_bounds(min_val=0, max_val=KP - KB)
                    pe.wait_ge(block_kept[b], use + 1)
                    for k in range(KB):
                        sources = hot_r[:, j // 2 % 2, bass.ds(at + k, 1), :] if b else hot_r[:, j // 2 % 2, k, :]
                        op = nc.tensor.matmul(big[:, j % 4, 0:NC * B], hot_l[:, b, :, k], sources, start=(k == 0), stop=(k == KB - 1))
                    op.then_inc(block_built[b], 1)
                    while degree_groups < (j + 1) * KG // blocks:
                        g = degree_groups
                        pe.wait_ge(hot_d_ready[g], c + 1)
                        for k in range(4):
                            t = 4 * g + k
                            op = nc.tensor.matmul(seg[:, 0, bass.ds(c * 4, 4)], hot_d[:, g, :, k], w_parts[:, bass.ds(first + t, 1), :],
                                                  start=(t == 0), stop=(t == KC - 1))
                        op.then_inc(hot_d_used[g], 1)
                        degree_groups += 1

            with pe.Fori(0, NC - 1) as c:
                blocks_and_degrees(c, BC)
            blocks_and_degrees(NC - 1, LASTB)
            for b in range(2):
                pe.wait_ge(block_kept[b], 2 + NB // 2)
            pe.sem_inc(ev("degrees_ps"), 1)

            def dense_sums(n):
                parts = x_parts[n % 2 if n < 3 else 0]
                first_parts = [1, 2 + ROUNDS, 2 + 2 * ROUNDS, 3 + 2 * ROUNDS][n]
                pe.wait_ge(ev("parts_ready"), first_parts)

                def turn_round(k):
                    pe.wait_ge(ev("sums_t"), n * ROUNDS + k + 1)
                    if n * ROUNDS + k >= 4:
                        pe.wait_ge(ev("sums_read"), n * ROUNDS + k - 3)
                    for c in range(4 * k, min(4 * k + 4, NC)):
                        wide = min(P, WIDE - c * P)
                        op = nc.tensor.matmul(round_nodes(n, k)[0:wide, c % 4, :], sums_t[:, k % 2, (c % 4) * P:(c % 4) * P + wide], join[:, :],
                                              start=True, stop=True)
                    op.then_inc(ev("sums_nodes"), 1)

                for k in range(ROUNDS):
                    cols = min(4 * P, WIDE - 4 * k * P)
                    if n * ROUNDS + k >= 2:
                        pe.wait_ge(ev("sums_t"), n * ROUNDS + k - 1)
                    for s in range(NC):
                        if k == 0 and n in (0, 3) and s == HALVES[1].start:
                            pe.wait_ge(ev("parts_ready"), first_parts + 1)
                        op = nc.tensor.matmul(seg[:, 2 + k % 2, 0:cols], parts[:, s, :, :], A[:, s, 4 * k * P:4 * k * P + cols],
                                              start=(s == 0), stop=(s == NC - 1))
                    op.then_inc(ev("sums_ps"), 1)
                    if k:
                        turn_round(k - 1)
                turn_round(ROUNDS - 1)

            for n in range(3):
                dense_sums(n)

            pe.wait_ge(ev("conv1_in"), 1)
            for k in range(ROUNDS + 1):
                if k < ROUNDS:
                    if k >= 2:
                        pe.wait_ge(ev("turn1_ready"), k - 1)
                    for c in range(4 * k, min(4 * k + 4, NC)):
                        op = nc.tensor.transpose(seg[0:D, k % 2, (c % 4) * P:(c % 4 + 1) * P], cur[:, c, :], ident[:, :])
                    op.then_inc(ev("turn1_ps"), 1)
                if k >= 1:
                    pe.wait_ge(ev("turn1_ready"), k)
                    for c in range(4 * k - 4, min(4 * k, NC)):
                        op = nc.tensor.matmul(big_nodes[:, c, :], turn1[:, (k - 1) % 2, (c % 4) * P:(c % 4 + 1) * P], w1_sb[:, :],
                                              start=(c % 8 == 0), stop=True, skip_group_check=True)
                    op.then_inc(ev("turn1_used"), 1)
            pe.wait_ge(ev("turn1_used"), ROUNDS)
            with pe.Fori(0, IT) as it:
                for q in range(Q):
                    pe.wait_ge(gathered[q], (it + 1) * (16 * G))
                    pe.wait_ge(onehot_ready[q], it + 1)
                    pe.wait_ge(acc_step, it * Q + q + 1)
                    for j in range(G):
                        op = nc.tensor.matmul(seg[0:D, q, 0:GW], rows1[:, q, j, :], onehot1[:, q, j, :],
                                              start=(j == 0), stop=(j == G - 1))
                    op.then_inc(seg_done[q], 1)
            pe.wait_ge(acc_step, Q + GROUPS)
            for c in range(NC):
                op = nc.tensor.matmul(big_nodes[:, c, :], acc_t[:, c * P:(c + 1) * P], w1_sb[:, :], start=False, stop=True,
                                      skip_group_check=True)
                if c % 8 == 7 or c == NC - 1:
                    op.then_inc(ev("conv1_out"), 1)

            dense_sums(3)
            pe.sem_inc(ev("adjacency_over_pe"), 1)
            pe.wait_ge(ev("nb_ready"), 1)
            for k in range(ROUNDS + 1):
                if k < ROUNDS:
                    if k >= 2:
                        pe.wait_ge(ev("turn2_ready"), k - 1)
                    for c in range(4 * k, min(4 * k + 4, NC)):
                        op = nc.tensor.transpose(seg[:, k % 2, (c % 4) * P:(c % 4 + 1) * P], h_nb[:, c, :], ident[:, :])
                    op.then_inc(ev("turn2_ps"), 1)
                if k >= 1:
                    pe.wait_ge(ev("turn2_ready"), k)
                    for c in range(4 * k - 4, min(4 * k, NC)):
                        op = nc.tensor.matmul(big_nodes[:, c, :], turn2_ring[:, (k - 1) % 2, (c % 4) * P:(c % 4 + 1) * P], w2_t[:, :],
                                              start=True, stop=True)
                    op.then_inc(ev("turn2_used"), 1)

            pe.wait_ge(ev("h_L3"), 1)
            for k in range(ROUNDS):
                if k >= 4:
                    pe.wait_ge(ev("h_t"), k - 3)
                for c in range(4 * k, min(4 * k + 4, NC)):
                    op = nc.tensor.transpose(seg[:, k % 4, (c % 4) * P:(c % 4 + 1) * P], h_nb[:, c, :], ident[:, :])
                op.then_inc(ev("h_ps"), 1)
            for k in range(ROUNDS):
                pe.wait_ge(ev("h_t"), k + 1)
                if k >= 4:
                    pe.wait_ge(ev("pr_copied"), k - 3)
                for c in range(4 * k, min(4 * k + 4, NC)):
                    op = nc.tensor.matmul(big[:, k % 4, (c % 4) * HID:(c % 4 + 1) * HID], h_t[:, c * P:(c + 1) * P], mw1_r, start=True, stop=True)
                op.then_inc(ev("pr_ps"), 1)
            pe.wait_ge(ev("pr_copied"), ROUNDS)
            pe.wait_ge(ld_l3, 15 * 16)
            pe.wait_ge(ev("mb2_ready"), 1)

            def turn_rows(it, q):
                r, k = q % 2, it * 2 + q // 2
                pe.wait_ge(gathered[q], (it + (IT + 1)) * (16 * G))
                pe.wait_ge(edges_loaded[q], (it + 1) * 16)
                pe.wait_ge(x_t_ready[r], k + 1)
                for j in range(G):
                    op = nc.tensor.transpose(big[:, r, j * P:(j + 1) * P], X[:, q, j, :], ident[:, :])
                op.then_inc(transposed[r], 1)

            def hidden_sums(it, q):
                r, k = q % 2, it * 2 + q // 2
                pe.wait_ge(x_t_ready[r], k + 2)
                pe.wait_ge(hid_ready[r], k + 1)
                pe.wait_ge(onehot_t_ready[q], it + 1)
                pe.wait_ge(prw_loaded[q], (it + 1) * 16)
                nc.tensor.matmul(big[:, 2 + r, :], mw1_se, x_t[:, r, :], start=True, stop=False)
                nc.tensor.matmul(big[:, 2 + r, :], prw[:, q, :], onehot_t[:, q, :], start=False, stop=True).then_inc(hid_done[r], 1)

            def message_sums(it, q):
                r, k = q % 2, it * 2 + q // 2
                pe.wait_ge(hid_ready[r], k + 2)
                pe.wait_ge(msg_ready[r], k + 1)
                nc.tensor.matmul(seg[:, 2 + r, 0:G * D], ones_bf[:, :], mb2_sum, start=True, stop=True)
                for j in range(G):
                    op = nc.tensor.matmul(seg[:, 2 + r, j * D:(j + 1) * D], hid_t[:, r, j * P:(j + 1) * P],
                                          mw2_sb, start=False, stop=True, skip_group_check=True)
                op.then_inc(msg_done[r], 1)

            def window_sums(it, q):
                r, k = q % 2, it * 2 + q // 2
                pe.wait_ge(msg_ready[r], k + 2)
                pe.wait_ge(onehot_ready[q], it + (IT + 1))
                pe.wait_ge(acc_step, it * Q + (Q + GROUPS + q - 1))
                for j in range(G):
                    op = nc.tensor.matmul(seg[0:D, r, 0:GW], msg[:, r, j, :], onehot3[:, q, j, :],
                                          start=(j == 0), stop=(j == G - 1))
                op.then_inc(seg_done[q], 1)

            steps(pe, [(0, turn_rows), (1, hidden_sums), (2, message_sums), (3, window_sums)])
            pe.wait_ge(acc_step, Q + 2 * GROUPS)
            for k in range(ROUNDS + 1):
                if k < ROUNDS:
                    n = min(4, NC - 4 * k) * P
                    cols = slice(4 * k * P, 4 * k * P + n)
                    if k >= 4:
                        pe.wait_ge(ev("y1_ready"), k - 3)
                    nc.tensor.matmul(seg[:, k % 4, 0:n], nw1_ah, acc_mem[:, cols], start=True, stop=True).then_inc(ev("y1_ps"), 1)
                if k >= 1:
                    pe.wait_ge(ev("y1_ready"), k)
                    for c in range(4 * k - 4, min(4 * k, NC)):
                        op = nc.tensor.matmul(big_nodes[:, c, :], y1_t[:, (k - 1) % 2, (c % 4) * P:(c % 4 + 1) * P], nw2_sb,
                                              start=True, stop=True)
                    op.then_inc(ev("y1_used"), 1)

        def on_vector(dve):
            dve.sem_inc(acc_step, Q)
            links = [0]

            def link(op):
                links[0] += 1
                op.then_inc(dve_chain, 1)
                dve.wait_ge(dve_chain, links[0])

            def per_feature(v):
                return v.rearrange("p (a d) -> p a d", a=1).broadcast_to([P, NC, D])

            def invsqrt():
                guess = st_b[:, :].bitcast(I32)
                link(dve.tensor_scalar(guess, st_a[:, :].bitcast(I32), 1, None, ALU.logical_shift_right))
                link(dve.tensor_scalar(guess, guess, -1.0, float(0x5f3759df), ALU.mult, ALU.add))
                for _ in range(3):
                    link(dve.tensor_tensor(st_d[:, :], st_b[:, :], st_b[:, :], ALU.mult))
                    link(dve.scalar_tensor_tensor(st_d[:, :], st_d[:, :], -0.5, st_a[:, :], ALU.mult, ALU.mult))
                    link(dve.scalar_tensor_tensor(st_b[:, :], st_d[:, :], 1.5, st_b[:, :], ALU.add, ALU.mult))

            bank_cols = [slice(8 * m, min(8 * m + 8, NC)) for m in range(4)]

            def centre(dst_, src_, tmp, cols):
                link(dve.tensor_reduce(st_a[:, cols], src_[:, cols, :], AX.X, ALU.add))
                link(dve.tensor_scalar(st_c[:, cols], st_a[:, cols], 1.0 / D, None, ALU.mult))
                link(dve.tensor_tensor(dst_[:, cols, :], src_[:, cols, :], per_node(st_c)[:, cols, :], ALU.subtract))
                link(dve.tensor_tensor(tmp[:, cols, :], dst_[:, cols, :], dst_[:, cols, :], ALU.mult))
                link(dve.tensor_reduce(st_c[:, cols], tmp[:, cols, :], AX.X, ALU.add))
                link(dve.tensor_scalar(st_a[:, cols], st_c[:, cols], 1.0 / D, EPS, ALU.mult, ALU.add))

            def split3(value, parts, rest):
                link(dve.tensor_copy(parts(0), value))
                link(dve.tensor_tensor(rest, value, parts(0), ALU.subtract))
                link(dve.tensor_copy(parts(1), rest))
                link(dve.tensor_tensor(rest, rest, parts(1), ALU.subtract))
                link(dve.tensor_copy(parts(2), rest))

            def one_hots(n, onehot, weighted, it, q):
                dve.wait_ge(seg_done[q], it + (1 + n * IT))
                for j in range(G):
                    t = it * (Q * G) + (q * G + j)
                    if weighted:
                        op = dve.tensor_scalar(onehot[:, q, j, :], iota_row[:, 0:GW], drel[:, bass.ds(t, 1)], wcol[:, bass.ds(t, 1)],
                                               ALU.is_equal, ALU.mult)
                    else:
                        op = dve.tensor_scalar(onehot[:, q, j, :], iota_row[:, 0:GW], drel[:, bass.ds(t, 1)], None, ALU.is_equal)
                op.then_inc(onehot_ready[q], 1)

            def add_window(n, bank, it, q):
                node = load_nodes(dve, base_row, it * (Q * G) + q * G, 1, N - 1)[0]
                dve.wait_ge(seg_done[q], it + (2 + n * IT))
                dve.wait_ge(acc_step, it * Q + (Q + n * GROUPS + q))
                window = acc_t[:, bass.ds(node, GW)]
                dve.tensor_tensor(window, window, seg[0:D, bank, 0:GW], ALU.add).then_inc(acc_step, 1)

            def receivers(it, q):
                dve.wait_ge(hid_done[q % 2], 1 + 2 * it + q // 2)
                dve.wait_ge(drel_loaded[q], (it + 1) * 16)
                dve.tensor_scalar(onehot_t[:, q, :], drel_bc[:, q, :], iota_p[0:GW, 0:1], None, ALU.is_equal).then_inc(onehot_t_ready[q], 1)

            dve.wait_ge(ld_edges, 13 * 16)
            dve.wait_ge(fills, 9)
            link(dve.tensor_copy(join[0:D, :], ident[0:D, 0:D]))
            link(dve.tensor_scalar(join[D:2 * D, :], ident[D:2 * D, D:2 * D], 1.0 / LOW, None, ALU.mult))
            dve.tensor_scalar(dst_hi, raw_dst, 4, 7, ALU.logical_shift_right, ALU.logical_shift_left)
            dve.tensor_scalar(dst_lo, raw_dst, B - 1, None, ALU.bitwise_and)
            dve.tensor_scalar(src_hi, raw_src, 7, 4, ALU.logical_shift_right, ALU.logical_shift_left)
            link(dve.tensor_scalar(src_lo, raw_src, P - 1, None, ALU.bitwise_and))
            link(dve.tensor_copy(dst_t, raw_dst))
            dve.sem_inc(ev("dst_t_ready"), 1)
            dve.tensor_tensor(key_r_t, src_hi, dst_lo, ALU.add).then_inc(ev("key_r_t_ready"), 1)
            dve.tensor_tensor(key_l_t, src_lo, dst_hi, ALU.add).then_inc(ev("key_l_t_ready"), 1)
            dve.tensor_tensor(drel_t.rearrange("p (c e) -> p c e", e=P), raw_dst.rearrange("p (c e) -> p c e", e=P),
                              group_base.rearrange("p (c a) -> p c a", a=1).broadcast_to([P, 4, P]), ALU.subtract).then_inc(ev("drel_t_ready"), 1)
            dve.tensor_copy(src_t, raw_src).then_inc(ev("src_t_ready"), 1)
            for c in range(4):
                op = dve.tensor_scalar(below[:, c * THR:(c + 1) * THR], starts, dst_t[:, c * P:c * P + 1], None, ALU.is_gt)
            op.then_inc(ev("below_ready"), 1)
            dve.wait_ge(ev("cols_ps"), 6)
            for b, t in ((0, dst_c), (1, key_r), (2, key_l), (4, src_i[:, :])):
                dve.tensor_copy(t, banks[b][:, 0:TK])
            link(dve.memset(w_parts, 1.0))
            dve.wait_ge(ev("cols_kept"), 2)
            split3(wcol[:, :], lambda k: w_parts[:, :, 1 + k], w_res[:, 0:TK])
            dve.sem_inc(ev("keys_ready"), 1)
            dve.wait_ge(ev("counts_ps"), 1)
            link(dve.tensor_scalar(first_row[:, :], banks[6][0:1, 0:THR], 1.0, 0.0, ALU.subtract, ALU.max))
            pairs = first_row[:, :].rearrange("a (b two) -> a b two", two=2)
            link(dve.scalar_tensor_tensor(pairs[:, :, 1], pairs[:, :, 0], float(KP - KB), pairs[:, :, 1], ALU.add, ALU.min))
            dve.sem_inc(ev("ranges_ready"), 1)

            def block_hots(c, blocks, slot):
                firsts = load_nodes(dve, first_row, c * BC, blocks, T)

                def equal_four(out_, four):
                    return dve.tensor_tensor(out_, four.rearrange("p (a k) -> p a k", a=1).broadcast_to([P, P, 4]), iota_4[:, :, :], ALU.is_equal)

                dve.wait_ge(rel_ready, c + 1)
                groups = 0
                for j in range(blocks):
                    b = j % 2
                    pair_no = c * (BC // 2) + j // 2
                    if b == 0:
                        dve.wait_ge(block_built[1], pair_no + 1)
                    for k in range(KB) if b == 0 else range(KB, KP - 1):
                        dve.tensor_scalar(hot_r[:, j // 2 % 2, k, :], iota_r[:, :], key_r[:, bass.ds(firsts[j - b] + k, 1)], None, ALU.is_equal)
                    dve.wait_ge(block_built[b], pair_no + (1 + b))
                    equal_four(hot_l[:, b, :, :], rel[:, slot, j * KB:(j + 1) * KB]).then_inc(hots_ready[b], 1)
                    while groups < (j + 1) * KG // blocks:
                        dve.wait_ge(hot_d_used[groups], 1 + c)
                        equal_four(hot_d[:, groups, :, :], rel[:, slot, BC * KB + 4 * groups:BC * KB + 4 * groups + 4]).then_inc(hot_d_ready[groups], 1)
                        groups += 1

            with dve.Fori(0, NC // 2) as two:
                block_hots(two * 2, BC, 0)
                block_hots(two * 2 + 1, BC, 1)
            block_hots(NC - 1, LASTB, 0)

            dve.wait_ge(ev("h_L0"), 1)
            dve.wait_ge(ev("degrees_ps"), 1)
            for g in range(KG):
                dve.wait_ge(hot_d_used[g], 1 + NC)
            link(dve.tensor_copy(deg[:, :, :], seg[:, 0, 0:4 * NC].rearrange("p (c a) -> p c a", a=4)))
            link(dve.tensor_scalar(rdeg[:, :], deg[:, :, 0], 1.0, None, ALU.max))
            link(dve.tensor_copy(st_a[:, :], rdeg[:, :]))
            link(dve.tensor_scalar(st_c[:, :], deg[:, :, 0], 0.0, None, ALU.is_gt))
            invsqrt()
            link(dve.tensor_tensor(dinv0[:, :], st_b[:, :], st_c[:, :], ALU.mult))
            def split_features(buf, value, rest, cols):
                parts = x_parts[buf]
                link(dve.tensor_copy(parts[:, cols, 0, :], value))
                link(dve.tensor_tensor(rest, value, parts[:, cols, 0, :], ALU.subtract))
                link(dve.tensor_scalar(parts[:, cols, 1, :], rest, LOW, None, ALU.mult))

            for cols in HALVES:
                link(dve.tensor_tensor(cur[:, cols, :], total[:, cols, :], per_node(dinv0)[:, cols, :], ALU.mult))
                split_features(0, cur[:, cols, :], hop[:, cols, :], cols)
                dve.sem_inc(ev("parts_ready"), 1)
            link(dve.tensor_tensor(dinv0sq[:, :], dinv0[:, :], dinv0[:, :], ALU.mult))
            link(dve.reciprocal(rdeg[:, :], rdeg[:, :]))
            link(dve.tensor_reduce(st_c[:, :], deg[:, :, 1:4], AX.X, ALU.add))
            link(dve.tensor_scalar(deg[:, :, 1], st_c[:, :], 1.0, None, ALU.add))
            link(dve.tensor_scalar(dinv1[:, :], deg[:, :, 1], 0.0, None, ALU.is_gt))
            link(dve.tensor_tensor(st_c[:, :], deg[:, :, 1], dinv1[:, :], ALU.mult))
            link(dve.tensor_tensor(st_c[:, :], st_c[:, :], dinv1[:, :], ALU.subtract))
            link(dve.tensor_scalar(st_a[:, :], st_c[:, :], 1.0, None, ALU.add))
            invsqrt()
            link(dve.tensor_tensor(dinv1[:, :], dinv1[:, :], st_b[:, :], ALU.mult))
            for n in range(3):
                for k in range(ROUNDS):
                    cols = slice(4 * k, min(4 * k + 4, NC))
                    rows = slice(0, LASTB * B if k == ROUNDS - 1 else P)
                    wide = cols.stop - cols.start
                    sums = round_nodes(n, k)[rows, 0:wide, :]
                    dve.wait_ge(ev("sums_nodes"), n * ROUNDS + k + 1)
                    link(dve.tensor_tensor(cur[rows, cols, :], sums, per_node(dinv0)[rows, cols, :], ALU.mult))
                    link(dve.tensor_tensor(total[rows, cols, :], total[rows, cols, :], cur[rows, cols, :], ALU.add))
                    if n < 2:
                        parts = x_parts[(n + 1) % 2]
                        link(dve.tensor_tensor(cur[rows, cols, :], sums, per_node(dinv0sq)[rows, cols, :], ALU.mult))
                        dve.sem_inc(ev("sums_read"), 1)
                        link(dve.tensor_copy(parts[rows, cols, 0, :], cur[rows, cols, :]))
                        link(dve.tensor_tensor(cur[rows, cols, :], cur[rows, cols, :], parts[rows, cols, 0, :], ALU.subtract))
                        link(dve.tensor_scalar(parts[rows, cols, 1, :], cur[rows, cols, :], LOW, None, ALU.mult))
                        dve.sem_inc(ev("parts_ready"), 1)
                    else:
                        dve.sem_inc(ev("sums_read"), 1)
                        link(dve.scalar_tensor_tensor(xs[:, cols, :], total[:, cols, :], 0.25, xs[:, cols, :], ALU.mult, ALU.add))
                        centre(cur[:, :, :], xs[:, :, :], hop, cols)

            invsqrt()
            link(dve.tensor_tensor(st_b[:, :], st_b[:, :], dinv1[:, :], ALU.mult))
            for cols in HALVES:
                dve.scalar_tensor_tensor(cur[:, cols, :], cur[:, cols, :], 0.0, per_node(st_b)[:, cols, :],
                                         ALU.max, ALU.mult).then_inc(table_ready, 1)
            dve.wait_ge(table_ready, 2)
            link(dve.memset(acc_t, 0.0))
            dve.sem_inc(ev("conv1_in"), 1)
            steps(dve, [(0, lambda it, q: one_hots(0, onehot1, True, it, q)), (4, lambda it, q: add_window(0, q, it, q))])
            dve.wait_ge(table_stored, 32)
            for m, cols in enumerate(bank_cols):
                dve.wait_ge(ev("conv1_out"), m + 1)
                conv = cur[:, cols, :]
                link(dve.tensor_tensor(conv, big_nodes[:, cols, :], per_node(dinv1)[:, cols, :], ALU.mult))
                link(dve.tensor_tensor(conv, conv, per_feature(b1_bc[:, :])[:, cols, :], ALU.add))
                link(dve.scalar_tensor_tensor(xs[:, cols, :], conv, 0.0, xs[:, cols, :], ALU.max, ALU.add))
                centre(hs, xs[:, :, :], cur[:, :, :], cols)

            invsqrt()
            for cols in HALVES:
                link(dve.scalar_tensor_tensor(hs[:, cols, :], hs[:, cols, :], 0.0, per_node(st_b)[:, cols, :], ALU.max, ALU.mult))
                split_features(0, hs[:, cols, :], cur[:, cols, :], cols)
                dve.sem_inc(ev("parts_ready"), 1)
            link(dve.memset(nb[:, NC - 1, :], 0.0))
            for k in range(ROUNDS):
                cols = slice(4 * k, min(4 * k + 4, NC))
                rows = slice(0, LASTB * B if k == ROUNDS - 1 else P)
                dve.wait_ge(ev("sums_nodes"), 3 * ROUNDS + k + 1)
                link(dve.tensor_tensor(nb[rows, cols, :], round_nodes(3, k)[rows, 0:cols.stop - cols.start, :],
                                       per_node(rdeg)[rows, cols, :], ALU.mult))
                dve.sem_inc(ev("sums_read"), 1)
            dve.sem_inc(ev("nb_ready"), 1)
            dve.sem_inc(ev("adjacency_over"), 1)
            link(dve.memset(X[:, Q - 1, :, :], 0.0))
            for m, cols in enumerate(bank_cols):
                dve.wait_ge(ev("turn2_used"), min(2 * m + 2, ROUNDS))
                link(dve.tensor_tensor(xs[:, cols, :], xs[:, cols, :], big_nodes[:, cols, :], ALU.add))
                centre(hs, xs[:, :, :], cur[:, :, :], cols)

            invsqrt()
            for cols in HALVES:
                dve.scalar_tensor_tensor(hs[:, cols, :], hs[:, cols, :], 0.0, per_node(st_b)[:, cols, :],
                                         ALU.max, ALU.mult).then_inc(table_ready, 1)
            dve.wait_ge(table_ready, 4)
            dve.sem_inc(ev("h_L3"), 1)
            link(dve.memset(acc_t, 0.0))
            dve.wait_ge(ld_l3, 15 * 16)
            split3(mb2_bc, lambda k: mb2_parts[:, k, :], mb2_rest)
            link(dve.memset(mb2_sum, 0.0))
            for k in range(3):
                link(dve.tensor_copy(mb2_sum[32 * k:32 * k + 1, :], mb2_parts[32 * k:32 * k + 1, k, :]))
            dve.sem_inc(ev("mb2_ready"), 1)
            steps(dve, [(0, receivers), (0, lambda it, q: one_hots(1, onehot3, False, it, q)), (4, lambda it, q: add_window(1, q % 2, it, q))])
            link(dve.tensor_tensor(xs[:, :, :], xs[:, :, :], hs, ALU.add))
            link(dve.tensor_tensor(xs[:, :, :], xs[:, :, :], per_feature(offset_bc), ALU.add))
            for m, cols in enumerate(bank_cols):
                dve.wait_ge(ev("y1_used"), min(2 * m + 2, ROUNDS))
                link(dve.tensor_tensor(nb[:, cols, :], big_nodes[:, cols, :], per_feature(nb2_bc)[:, cols, :], ALU.add))
                centre(cur[:, :, :], nb, scratch, cols)
                link(dve.tensor_tensor(cur[:, cols, :], cur[:, cols, :], per_feature(scale_bc)[:, cols, :], ALU.mult))
            invsqrt()
            for cols in HALVES:
                link(dve.tensor_tensor(cur[:, cols, :], cur[:, cols, :], per_node(st_b)[:, cols, :], ALU.mult))
                dve.tensor_tensor(xs[:, cols, :], xs[:, cols, :], cur[:, cols, :], ALU.add).then_inc(ev("out_ready"), 1)

        return {'load_edges': load_edges, 'pad_edges': pad_edges, 'sync': on_sync, 'gpsimd': on_gpsimd, 'scalar': on_scalar, 'tensor': on_tensor, 'vector': on_vector}


def build(nc, *args):
    dst = args[2]
    with ExitStack() as ctx:
        sems = {}

        def sem(name):
            if name not in sems:
                sems[name] = ctx.enter_context(nc.semaphore(name))
            return sems[name]

        base_row = ctx.enter_context(nc.sbuf_tensor("base_row", [1, T + G], I32))
        crowded = ctx.enter_context(nc.sbuf_tensor("crowded", [1, 1], I32))
        base_loaded, base_steps, crowded_ready = sem("base_loaded"), sem("base_steps"), sem("crowded_ready")
        with nc.sbuf_tensor("early_loads", [P, EARLY], F32), \
                nc.sbuf_tensor("tile_block", [1, 3, T], I32) as tile_block, nc.sbuf_tensor("same", [1, 4, T], F32) as same:
            pass
        general = general_path(nc, sem, base_row[:, :], *args)
        dense = dense_path(nc, sem, base_row[:, :], *args)
        block = ctx.enter_context(nc.Block())

        def is_crowded(eng):
            eng.wait_ge(crowded_ready, 1)
            _, v = nc.values_load_multi_w_load_instructions(
                crowded[0:1, 0:1], engines=[eng.engine], min_val=0, max_val=1,
                skip_runtime_bounds_check_because="a comparison's result")
            return v[0] != 0

        @block.sync
        def _(sp):
            sp.dma_start(base_row[:, 0:FULL], dst[0:FULL * P].rearrange("(a t e) -> a t e", a=1, e=P)[:, :, 0],
                         allow_slow_non_contiguous=True).then_inc(base_loaded, 16)
            sp.dma_start(base_row[:, FULL:T], dst[FULL * P:FULL * P + 1].rearrange("(a t) -> a t", a=1)).then_inc(base_loaded, 16)
            dense["load_edges"](sp)
            with sp.If(is_crowded(sp)):
                general["sync"](sp)
            with sp.Else():
                dense["sync"](sp)

        @block.gpsimd
        def _(pool):
            dense["pad_edges"](pool)
            with pool.If(is_crowded(pool)):
                general["gpsimd"](pool)
            with pool.Else():
                dense["gpsimd"](pool)

        @block.scalar
        def _(act):
            with act.If(is_crowded(act)):
                general["scalar"](act)
            with act.Else():
                dense["scalar"](act)

        @block.tensor
        def _(pe):
            with pe.If(is_crowded(pe)):
                general["tensor"](pe)
            with pe.Else():
                dense["tensor"](pe)

        @block.vector
        def _(dve):
            dve.memset(base_row[:, T:T + G], N - 1).then_inc(base_steps, 1)
            dve.memset(same[:, :, :], 0.0).then_inc(base_steps, 1)
            dve.wait_ge(base_loaded, 32)
            dve.tensor_scalar(tile_block[:, 0, :], base_row[:, 0:T], 4, None, ALU.logical_shift_right).then_inc(base_steps, 1)
            dve.tensor_scalar(tile_block[:, 1, :], base_row[:, 0:T], 7, None, ALU.logical_shift_right).then_inc(base_steps, 1)
            dve.tensor_scalar(tile_block[:, 2, :], base_row[:, 0:T], 5, None, ALU.logical_shift_right).then_inc(base_steps, 1)
            dve.wait_ge(base_steps, 5)
            for k, span in ((0, KB - 1), (1, KC - 1), (2, KP - 1)):
                dve.tensor_tensor(same[:, k, 0:T - span], tile_block[:, k, 0:T - span], tile_block[:, k, span:T],
                                  ALU.is_equal).then_inc(base_steps, 1)
            dve.tensor_tensor(same[:, 3, :], base_row[:, G:T + G], base_row[:, 0:T], ALU.subtract).then_inc(base_steps, 1)
            dve.wait_ge(base_steps, 9)
            dve.tensor_scalar(same[:, 3, :], same[:, 3, :], GW - 0.5, None, ALU.is_gt).then_inc(base_steps, 1)
            dve.wait_ge(base_steps, 10)
            dve.wait_ge(sem("dense_ld_edges"), 13 * 16)
            dve.tensor_reduce(crowded[:, :], same[:, :, :].rearrange("a k t -> a (k t)"), AX.X, ALU.max).then_inc(crowded_ready, 1)
            with dve.If(is_crowded(dve)):
                general["vector"](dve)
            with dve.Else():
                dense["vector"](dve)


_INS = ['x', 'src', 'dst', 'edge_attr_64', 'edge_weight', 'L1_gnn_W', 'L1_gnn_b', 'L2_gnn_W_self', 'L2_gnn_W_neigh',
        'L3_gnn_msg_W1', 'L3_gnn_msg_b1', 'L3_gnn_msg_W2', 'L3_gnn_msg_b2', 'L3_gnn_node_W1', 'L3_gnn_node_b1',
        'L3_gnn_node_W2', 'L3_gnn_node_b2', 'L3_gnn_ln_scale', 'L3_gnn_ln_offset']
_OUTS = [((N, D), 'float32')]


def kernel(**inputs):
    import numpy as _np
    import concourse.bacc as _bacc
    from concourse import mybir as _mybir
    from concourse.bass_utils import run_bass_kernel_spmd as _run

    nc = _bacc.Bacc("TRN2", target_bir_lowering=False, num_devices=1)
    arrays, args = {}, []
    for name in _INS:
        a = _np.ascontiguousarray(inputs[name])
        arrays[f"in_{name}_dram"] = a
        args.append(nc.dram_tensor(f"in_{name}_dram", a.shape, _mybir.dt.from_np(a.dtype), kind="ExternalInput").ap())
    for i, (shape, dtype) in enumerate(_OUTS):
        dt = _mybir.dt.from_np(_np.dtype(dtype))
        args.append(nc.dram_tensor(f"out_{i}_dram", shape, dt, kind="ExternalOutput").ap())
    build(nc, *args)
    r = _run(nc, [arrays], core_ids=[0])
    got = tuple(r.results[0][f"out_{i}_dram"] for i in range(len(_OUTS)))
    return got[0]
```
